# Optimizing a Trainium2 kernel written in Bass

```python
import numpy as np
import jax
import jax.numpy as jnp

def _softmax(x, axis=-1):
    return jax.nn.softmax(x, axis=axis)

def _gelu(x):
    return jax.nn.gelu(x, approximate=True)

def _silu(x):
    return jax.nn.silu(x)

def _sigmoid(x):
    return jax.nn.sigmoid(x)

def _layernorm(x, axis=-1, eps=1e-05):
    m = jnp.mean(x, axis=axis, keepdims=True)
    v = jnp.var(x, axis=axis, keepdims=True)
    return (x - m) / jnp.sqrt(v + eps)

def _scatter_add(tgt, idx, src, axis=0):
    return tgt.at[idx].add(src)

def _segment_sum(src, seg, n):
    return jax.ops.segment_sum(src, seg, n)
kernel_name = 'mk_hybrid_d1_jaxref_r8_26ca5f'

def setup_inputs(seed: int=0):
    np.random.seed(seed)
    _w = jnp.asarray

    def _L0_attn_a_setup():
        import jax, jax.numpy as jnp
        import numpy as np
        B, L, H, N = (4, 512, 128, 64)
        LN_EPS = 1e-05

        def _s4d_kernel(log_A_real, A_imag, C_re, C_im, log_dt, length):
            A = -jnp.exp(log_A_real) + 1j * A_imag
            dt = jnp.exp(log_dt)[:, None]
            dtA = dt * A
            C = C_re + 1j * C_im
            Ct = C * (jnp.exp(dtA) - 1.0) / A
            l = jnp.arange(length, dtype=jnp.float32)
            V = jnp.exp(dtA[:, :, None] * l[None, None, :])
            K = 2.0 * jnp.real(jnp.einsum('hn,hnl->hl', Ct, V))
            return K
        key = jax.random.key(seed)
        ks = jax.random.split(key, 6)
        x = jax.random.normal(ks[0], (B, L, H), dtype=jnp.float32)
        log_A_real = jnp.log(0.5 * jnp.ones((H, N), dtype=jnp.float32))
        A_imag = jnp.broadcast_to(jnp.pi * jnp.arange(N, dtype=jnp.float32), (H, N))
        C_re = jax.random.normal(ks[1], (H, N), dtype=jnp.float32) * 0.5
        C_im = jax.random.normal(ks[2], (H, N), dtype=jnp.float32) * 0.5
        u = jax.random.uniform(ks[3], (H,), dtype=jnp.float32)
        log_dt = u * (jnp.log(0.1) - jnp.log(0.001)) + jnp.log(0.001)
        D = jax.random.normal(ks[4], (H,), dtype=jnp.float32)
        ln_w = jnp.ones((H,), dtype=jnp.float32)
        ln_b = jnp.zeros((H,), dtype=jnp.float32)
        return {'x': x, 'log_A_real': log_A_real, 'A_imag': A_imag, 'C_re': C_re, 'C_im': C_im, 'log_dt': log_dt, 'D': D, 'ln_w': ln_w, 'ln_b': ln_b}
    _L0_attn_a_in = _L0_attn_a_setup()

    def _L0_attn_b_setup():
        import math
        import jax, jax.numpy as jnp
        import numpy as np
        B, T, D_MODEL, N_HEADS = (2, 256, 128, 16)
        HEAD_DIM = D_MODEL // N_HEADS

        def _alibi_slopes(n_heads: int) -> np.ndarray:

            def pow2(n):
                start = 2.0 ** (-(8.0 / n))
                return [start * start ** i for i in range(n)]
            if math.log2(n_heads).is_integer():
                s = pow2(n_heads)
            else:
                cp = 2 ** math.floor(math.log2(n_heads))
                base = pow2(cp)
                extra = pow2(2 * cp)[1::2]
                s = base + extra[:n_heads - cp]
            return np.asarray(s, dtype=np.float32)
        SLOPES = jnp.asarray(_alibi_slopes(N_HEADS))
        key = jax.random.key(seed)
        k1, k2, k3 = jax.random.split(key, 3)
        x = jax.random.normal(k1, (B, T, D_MODEL), dtype=jnp.float32)
        Wqkv = jax.random.normal(k2, (D_MODEL, 3 * D_MODEL), dtype=jnp.float32) * 0.02
        Wout = jax.random.normal(k3, (D_MODEL, D_MODEL), dtype=jnp.float32) * 0.02
        return {'x': x, 'Wqkv': Wqkv, 'Wout': Wout}
    _L0_attn_b_in = _L0_attn_b_setup()

    def _L0_ffn_setup():
        import jax, jax.numpy as jnp
        import numpy as np
        B, S, DIM = (4, 256, 128)
        E, K, HID = (8, 2, 512)
        key = jax.random.key(seed)
        ks = jax.random.split(key, 8)
        init = lambda k, sh: jax.random.normal(k, sh, jnp.float32) * 0.02
        return {'x': jax.random.normal(ks[0], (B, S, DIM), jnp.float32), 'gate_w': init(ks[1], (DIM, E)), 'gate_b': jnp.zeros((E,), jnp.float32), 'w1': init(ks[2], (E, DIM, HID)), 'b1': jnp.zeros((E, HID), jnp.float32), 'w2': init(ks[3], (E, HID, DIM)), 'b2': jnp.zeros((E, DIM), jnp.float32), 'ws1': init(ks[4], (DIM, HID)), 'bs1': jnp.zeros((HID,), jnp.float32), 'ws2': init(ks[5], (HID, DIM)), 'bs2': jnp.zeros((DIM,), jnp.float32)}
    _L0_ffn_in = _L0_ffn_setup()
    _d = {'L0_attn_a_x': _L0_attn_a_in['x'], 'L0_attn_a_log_A_real': _L0_attn_a_in['log_A_real'], 'L0_attn_a_A_imag': _L0_attn_a_in['A_imag'], 'L0_attn_a_C_re': _L0_attn_a_in['C_re'], 'L0_attn_a_C_im': _L0_attn_a_in['C_im'], 'L0_attn_a_log_dt': _L0_attn_a_in['log_dt'], 'L0_attn_a_D': _L0_attn_a_in['D'], 'L0_attn_a_ln_w': _L0_attn_a_in['ln_w'], 'L0_attn_a_ln_b': _L0_attn_a_in['ln_b'], 'L0_attn_b_Wqkv': _L0_attn_b_in['Wqkv'], 'L0_attn_b_Wout': _L0_attn_b_in['Wout'], 'L0_ffn_gate_w': _L0_ffn_in['gate_w'], 'L0_ffn_gate_b': _L0_ffn_in['gate_b'], 'L0_ffn_w1': _L0_ffn_in['w1'], 'L0_ffn_b1': _L0_ffn_in['b1'], 'L0_ffn_w2': _L0_ffn_in['w2'], 'L0_ffn_b2': _L0_ffn_in['b2'], 'L0_ffn_ws1': _L0_ffn_in['ws1'], 'L0_ffn_bs1': _L0_ffn_in['bs1'], 'L0_ffn_ws2': _L0_ffn_in['ws2'], 'L0_ffn_bs2': _L0_ffn_in['bs2']}
    _x0 = _d['L0_attn_a_x']
    _d['L0_attn_a_x'] = jax.random.normal(jax.random.fold_in(jax.random.key(seed), 1), (16, 256, 128), dtype=_x0.dtype)
    del _x0
    return _d

def reference(L0_attn_a_x, L0_attn_a_log_A_real, L0_attn_a_A_imag, L0_attn_a_C_re, L0_attn_a_C_im, L0_attn_a_log_dt, L0_attn_a_D, L0_attn_a_ln_w, L0_attn_a_ln_b, L0_attn_b_Wqkv, L0_attn_b_Wout, L0_ffn_gate_w, L0_ffn_gate_b, L0_ffn_w1, L0_ffn_b1, L0_ffn_w2, L0_ffn_b2, L0_ffn_ws1, L0_ffn_bs1, L0_ffn_ws2, L0_ffn_bs2):

    def _L0_attn_a_ref(x, log_A_real, A_imag, C_re, C_im, log_dt, D, ln_w, ln_b):
        import jax, jax.numpy as jnp
        import numpy as np
        B, L, H, N = (4, 512, 128, 64)
        LN_EPS = 1e-05

        def _s4d_kernel(log_A_real, A_imag, C_re, C_im, log_dt, length):
            A = -jnp.exp(log_A_real) + 1j * A_imag
            dt = jnp.exp(log_dt)[:, None]
            dtA = dt * A
            C = C_re + 1j * C_im
            Ct = C * (jnp.exp(dtA) - 1.0) / A
            l = jnp.arange(length, dtype=jnp.float32)
            V = jnp.exp(dtA[:, :, None] * l[None, None, :])
            K = 2.0 * jnp.real(jnp.einsum('hn,hnl->hl', Ct, V))
            return K
        b, length, h = x.shape
        K = _s4d_kernel(log_A_real, A_imag, C_re, C_im, log_dt, length)
        n = 2 * length
        Xf = jnp.fft.rfft(x, n=n, axis=1)
        Kf = jnp.fft.rfft(K, n=n, axis=1)
        y = jnp.fft.irfft(Xf * Kf.T[None, :, :], n=n, axis=1)[:, :length, :]
        z = y + x * D[None, None, :]
        r = x + z
        mu = jnp.mean(r, axis=-1, keepdims=True)
        var = jnp.var(r, axis=-1, keepdims=True)
        out = (r - mu) * jax.lax.rsqrt(var + LN_EPS) * ln_w + ln_b
        return out

    def _L0_attn_b_ref(x, Wqkv, Wout):
        import math
        import jax, jax.numpy as jnp
        import numpy as np
        B, T, D_MODEL, N_HEADS = (2, 256, 128, 16)
        HEAD_DIM = D_MODEL // N_HEADS

        def _alibi_slopes(n_heads: int) -> np.ndarray:

            def pow2(n):
                start = 2.0 ** (-(8.0 / n))
                return [start * start ** i for i in range(n)]
            if math.log2(n_heads).is_integer():
                s = pow2(n_heads)
            else:
                cp = 2 ** math.floor(math.log2(n_heads))
                base = pow2(cp)
                extra = pow2(2 * cp)[1::2]
                s = base + extra[:n_heads - cp]
            return np.asarray(s, dtype=np.float32)
        SLOPES = jnp.asarray(_alibi_slopes(N_HEADS))
        Bc, Tc, Dc = x.shape
        qkv = x @ Wqkv
        q, k, v = jnp.split(qkv, 3, axis=-1)
        q = q.reshape(Bc, Tc, N_HEADS, HEAD_DIM)
        k = k.reshape(Bc, Tc, N_HEADS, HEAD_DIM)
        v = v.reshape(Bc, Tc, N_HEADS, HEAD_DIM)
        scale = 1.0 / math.sqrt(HEAD_DIM)
        logits = jnp.einsum('bihd,bjhd->bhij', q, k) * scale
        pos = jnp.arange(Tc, dtype=jnp.float32)
        rel = pos[None, :] - pos[:, None]
        logits = logits + SLOPES[None, :, None, None] * rel[None, None, :, :]
        causal = pos[:, None] >= pos[None, :]
        logits = jnp.where(causal[None, None, :, :], logits, -jnp.inf)
        attn = jax.nn.softmax(logits, axis=-1)
        out = jnp.einsum('bhij,bjhd->bihd', attn, v).reshape(Bc, Tc, Dc)
        return out @ Wout

    def _L0_ffn_ref(x, gate_w, gate_b, w1, b1, w2, b2, ws1, bs1, ws2, bs2):
        import jax, jax.numpy as jnp
        import numpy as np
        B, S, DIM = (4, 256, 128)
        E, K, HID = (8, 2, 512)
        orig_shape = x.shape
        xf = x.reshape(-1, DIM)
        logits = xf @ gate_w + gate_b
        top_w, top_i = jax.lax.top_k(logits, K)
        gw = jax.nn.softmax(top_w, axis=-1).astype(xf.dtype)
        combine = (gw[:, :, None] * jax.nn.one_hot(top_i, E, dtype=xf.dtype)).sum(axis=1)
        out = jnp.zeros_like(xf)
        for e in range(E):
            h = jax.nn.gelu(xf @ w1[e] + b1[e], approximate=False)
            out = out + combine[:, e:e + 1] * (h @ w2[e] + b2[e])
        shared = jax.nn.gelu(xf @ ws1 + bs1, approximate=False) @ ws2 + bs2
        return (out + shared).reshape(orig_shape)
    x = L0_attn_a_x
    x = x + _L0_attn_a_ref(_layernorm(x, axis=-1), L0_attn_a_log_A_real, L0_attn_a_A_imag, L0_attn_a_C_re, L0_attn_a_C_im, L0_attn_a_log_dt, L0_attn_a_D, L0_attn_a_ln_w, L0_attn_a_ln_b)
    x = x + _L0_ffn_ref(_layernorm(x, axis=-1), L0_ffn_gate_w, L0_ffn_gate_b, L0_ffn_w1, L0_ffn_b1, L0_ffn_w2, L0_ffn_b2, L0_ffn_ws1, L0_ffn_bs1, L0_ffn_ws2, L0_ffn_bs2)
    x = x + _L0_attn_b_ref(_layernorm(x, axis=-1), L0_attn_b_Wqkv, L0_attn_b_Wout)
    x = x + _L0_ffn_ref(_layernorm(x, axis=-1), L0_ffn_gate_w, L0_ffn_gate_b, L0_ffn_w1, L0_ffn_b1, L0_ffn_w2, L0_ffn_b2, L0_ffn_ws1, L0_ffn_bs1, L0_ffn_ws2, L0_ffn_bs2)
    return x

_drawn_inputs = setup_inputs


def setup_inputs(seed=0):
    import zlib

    import numpy as np

    out = dict(_drawn_inputs(seed))
    spreads = {'L0_attn_a_log_A_real': (-0.6931471824645996, 0.6),
     'L0_attn_a_ln_w': (1.0, 0.2),
     'L0_attn_a_ln_b': (0.0, 0.1),
     'L0_ffn_gate_b': (0.0, 0.1),
     'L0_ffn_b1': (0.0, 0.436),
     'L0_ffn_b2': (0.0, 0.1),
     'L0_ffn_bs1': (0.0, 0.333),
     'L0_ffn_bs2': (0.0, 0.1)}
    factors = {'L0_attn_b_Wqkv': 6.095, 'L0_attn_b_Wout': 6.063}
    for name, (base, spread) in spreads.items():
        noise = np.random.default_rng([zlib.crc32(name.encode()), seed]).standard_normal(out[name].shape)
        drawn = base * np.exp(spread * noise) if base else spread * noise
        out[name] = jnp.asarray(drawn.astype(out[name].dtype))
    for name, factor in factors.items():
        out[name] = (out[name] * factor).astype(out[name].dtype)
    return out
```

```python
from contextlib import ExitStack

import numpy as np

import concourse.bass as bass
from concourse import mybir

ALU = mybir.AluOpType
ACT = mybir.ActivationFunctionType
AX = mybir.AxisListType
F32 = mybir.dt.float32
F16 = mybir.dt.float16
BF16 = mybir.dt.bfloat16
I32 = mybir.dt.int32

P = 128
D = 128
NB, SEQ = 16, 256
NT = NB * SEQ // P
TPB = SEQ // P
BANK = 512
EPS = 1e-5

NM = 64
LF = 16
NFFT = 2 * SEQ
NFT = NFFT // P
CB = BANK // D
NCG = NB // CB
ROUND = 12582912.0
TWO_PI_HI = 6.28125
TWO_PI_LO = 2 * np.pi - TWO_PI_HI
PI_IN = 3.1415925

NE, HID = 8, 512
NX = NE + 1
MT = HID // P
GT = BANK // P
NG = NT // GT
WS = 1024.0
NH, HD = 16, 8
GH, HG = 4, 4
WQ = 64.0
LOGIT = WQ * WQ * HD ** 0.5
LOWEST = -3.0e38
ARENA = 25 * 1024


class Bag:
    pass


def norm_statistics(dve, link, stats, m):
    me, mo = stats[:, :, 1], stats[:, :, 4]
    se, so = stats[:, :, 2], stats[:, :, 5]
    dve.tensor_tensor(m.a, me, mo, ALU.add)
    dve.tensor_tensor(m.d, me, mo, ALU.subtract)
    link(dve.tensor_tensor(m.s, se, so, ALU.add))
    dve.tensor_scalar(m.mean, m.a, 0.5, None, ALU.mult)
    dve.tensor_tensor(m.q, m.d, m.d, ALU.mult)
    link(dve.tensor_scalar(m.s, m.s, 1.0 / D, EPS, ALU.mult, ALU.add))
    return dve.scalar_tensor_tensor(m.vareps, m.q, 0.25, m.s, ALU.mult, ALU.add)


def rows_of(buffer, first, last):
    m = Bag()
    m.a, m.d, m.s, m.q, m.mean, m.vareps, m.rstd, m.nmr = (buffer[:, i, first:last] for i in range(8))
    return m


def conv_stage(nc, t):
    with ExitStack() as ctx:
        def sem(name):
            return ctx.enter_context(nc.semaphore("c_" + name))

        scratch = t.arena
        at = [0]

        def carve(*shape):
            n = int(np.prod(shape))
            v = scratch[:, at[0]:at[0] + n]
            at[0] += n
            if len(shape) == 2:
                v = v.rearrange("p (a b) -> p a b", b=shape[1])
            if len(shape) == 3:
                v = v.rearrange("p (a b c) -> p a b c", b=shape[1], c=shape[2])
            return v

        FW = carve(TPB, NFFT)
        IV = carve(NFT, SEQ)
        PRM = carve(6, D)
        WLN = carve(2, D)
        OFF = carve(4)
        DCOL = carve(1)
        KEEP = carve(2)
        TMP = carve(24, D)
        SIN2, SINA, SINB, KQ, PHR = (carve(LF, D) for _ in range(5))
        mag_at = at[0]
        MAG2, MAG1 = carve(LF, D), carve(LF, D)
        KCH = carve(SEQ)
        KLAG = carve(TPB, D)
        SPK = carve(4, 2, D)
        KDIG = PHR
        M4 = KQ.rearrange("p a h -> p (a h)").rearrange("p (k n) -> p k n", n=BANK)
        YS = scratch[:, mag_at:mag_at + 2 * NFT * BANK].rearrange("p (k n) -> p k n", n=BANK)
        RN = SINB.rearrange("p a h -> p (a h)").rearrange("p (k n) -> p k n", n=BANK)
        XN = t.XN
        ps = t.psum

        params_in, x_in, dct_in, ln_in = sem("params_in"), sem("x_in"), sem("dct_in"), sem("ln_in")
        dve_step, pool_step = sem("dve_step"), sem("pool_step")
        exps, dt_ready, decay_ready, angle_ready = sem("exps"), sem("dt_ready"), sem("decay_ready"), sem("angle_ready")
        mags, phase_ready, sines = sem("mags"), sem("phase_ready"), sem("sines")
        ct_ready, e2_ready, e1_ready = sem("ct_ready"), sem("e2_ready"), sem("e1_ready")
        kdig_mm, kdig_sb, kch_mm, kch_sb, klag_mm, klag_sb = (sem(n) for n in (
            "kdig_mm", "kdig_sb", "kch_mm", "kch_sb", "klag_mm", "klag_sb"))
        kf_mm, spk_ready = sem("kf_mm"), sem("spk_ready")
        x_var, x_rstd, xn_ready = sem("x_var"), sem("x_rstd"), sem("xn_ready")
        fwd_mm, prod_ready, ys_ready, inv_mm = (sem(n) for n in (
            "fwd_mm", "prod_ready", "ys_ready", "inv_mm"))
        r_var, r_rstd, r_nmr, rn_ready, inv_read, res_ready = (sem(n) for n in (
            "r_var", "r_rstd", "r_nmr", "rn_ready", "inv_read", "res_ready"))

        block = ctx.enter_context(nc.Block())
        C_RE, C_IM, LAR, AIM, LDT, DT = 2, 3, 0, 1, 4, 5

        @block.sync
        def _(sp):
            sp.dma_start(PRM[:, 0:5, :], t.dram["params"].rearrange("k p h -> p k h")).then_inc(params_in, 16)
            sp.dma_start(OFF, t.dram["offsets"]).then_inc(params_in, 16)
            sp.dma_start(t.RES[:, 0:NT // 2, :], t.dram["x"].rearrange("b (t p) d -> p (b t) d", p=P)[:, 0:NT // 2, :]).then_inc(x_in, 16)
            sp.dma_start(FW, t.dram["fwd"].rearrange("t p f -> p t f")).then_inc(dct_in, 16)
            sp.dma_start(KEEP, t.dram["keep"]).then_inc(dct_in, 16)

        @block.gpsimd
        def _(pool):
            def link(ins):
                link.n += 1
                ins.then_inc(pool_step, 1)
                pool.wait_ge(pool_step, link.n)
            link.n = 0
            m = rows_of(t.NRM, 0, NT)
            link(nc.gpsimd.memset(t.MHALF[:, 0:NT], -0.5))
            pool.wait_ge(x_var, 1)
            nc.gpsimd.tensor_tensor(m.rstd, m.vareps, t.MHALF[:, 0:NT], ALU.pow).then_inc(x_rstd, 1)
            pool.wait_ge(mags, 1)
            pool.wait_ge(sines, 1)
            nc.gpsimd.tensor_tensor(SIN2, SIN2, MAG2, ALU.mult).then_inc(e2_ready, 1)
            m = rows_of(t.NRM, NT, NT + 8 * NCG)

            def sums(g, k):
                pool.wait_ge(prod_ready, 2 * g + k + 1)
                if g >= 2:
                    pool.wait_ge(inv_mm, 2 * (g - 1))
                ys = YS[:, NFT * (g % 2) + k, :]
                yi = YS[:, NFT * (g % 2) + 2 + k, :]
                nc.gpsimd.tensor_tensor(ys, M4[:, 0, :], M4[:, 1, :], ALU.subtract)
                nc.gpsimd.tensor_tensor(yi, M4[:, 2, :], M4[:, 3, :], ALU.add).then_inc(ys_ready, 1)

            def finish(g):
                s = slice(8 * g, 8 * g + 8)
                pool.wait_ge(r_var, g + 1)
                nc.gpsimd.tensor_tensor(m.rstd[:, s], m.vareps[:, s], t.MHALF[:, 0:8], ALU.pow).then_inc(r_rstd, 1)
                for tt in range(TPB):
                    pool.wait_ge(rn_ready, 2 * g + tt + 1)
                    rn = RN[:, 2 * (g % 2) + tt, :].rearrange("p (b h) -> p b h", h=D)
                    res = t.RES[:, 2 * CB * g + tt:2 * CB * (g + 1):2, :]
                    if g == 0 and tt == 0:
                        pool.wait_ge(ln_in, 48)
                    link(nc.gpsimd.tensor_tensor(rn, rn, WLN[:, 0:1, :].broadcast_to([P, CB, D]), ALU.mult))
                    link(nc.gpsimd.tensor_tensor(rn, rn, WLN[:, 1:2, :].broadcast_to([P, CB, D]), ALU.add))
                    nc.gpsimd.tensor_tensor(res, res, rn, ALU.add).then_inc(res_ready, 1)

            for g in range(NCG):
                sums(g, 0)
                sums(g, 1)
                if g >= 1:
                    finish(g - 1)
            finish(NCG - 1)

        @block.scalar
        def _(act):
            act.dma_start(t.RES[:, NT // 2:, :], t.dram["x"].rearrange("b (t p) d -> p (b t) d", p=P)[:, NT // 2:, :]).then_inc(x_in, 16)
            act.dma_start(t.ID, t.dram["ident"]).then_inc(dct_in, 16)
            act.dma_start(IV, t.dram["inv"].rearrange("t p f -> p t f")).then_inc(ln_in, 16)
            act.dma_start(WLN, t.dram["ln"].rearrange("k p h -> p k h")).then_inc(ln_in, 16)
            act.dma_start(DCOL, t.dram["dcol"]).then_inc(ln_in, 16)
            act.wait_ge(params_in, 32)
            nc.scalar.activation(PRM[:, DT, :], PRM[:, LDT, :], ACT.Exp)
            nc.scalar.activation(PRM[:, LAR, :], PRM[:, LAR, :], ACT.Exp).then_inc(exps, 1)
            act.wait_ge(decay_ready, 1)
            for b in range(LF):
                ins = nc.scalar.activation(MAG2[:, b, :], TMP[:, 0, :], ACT.Exp, scale=-float(b))
            ins.then_inc(mags, 1)
            for a in range(LF):
                ins = nc.scalar.activation(MAG1[:, a, :], TMP[:, 0, :], ACT.Exp, scale=-float(LF * a))
            ins.then_inc(mags, 1)
            act.wait_ge(phase_ready, 1)
            nc.scalar.activation(SIN2, SIN2, ACT.Sin).then_inc(sines, 1)
            act.wait_ge(phase_ready, 2)
            nc.scalar.activation(TMP[:, 4:6, :], TMP[:, 4:6, :], ACT.Sin).then_inc(sines, 1)
            act.wait_ge(phase_ready, 3)
            nc.scalar.activation(SINA, SINA, ACT.Sin).then_inc(sines, 1)
            act.wait_ge(phase_ready, 4)
            nc.scalar.activation(SINB, SINB, ACT.Sin).then_inc(sines, 1)
            for q in range(4):
                act.wait_ge(kdig_mm, q + 1)
                nc.scalar.activation(KDIG[0:LF, :, 32 * q:32 * q + 32],
                                     ps[q][0:LF, :].rearrange("a (h b) -> a b h", b=LF),
                                     ACT.Copy, scale=2.0).then_inc(kdig_sb, 1)
            act.wait_ge(klag_mm, 1)
            nc.scalar.activation(KLAG, ps[5][:, 0:SEQ].rearrange("p (t h) -> p t h", h=D), ACT.Copy).then_inc(klag_sb, 1)
            m = rows_of(t.NRM, NT, NT + 8 * NCG)
            for g in range(NCG):
                act.wait_ge(r_nmr, g + 1)
                for tt in range(TPB):
                    if g >= 2:
                        act.wait_ge(res_ready, 2 * (g - 2) + tt + 1)
                    for b in range(CB):
                        j = 8 * g + 4 * tt + b
                        ins = nc.scalar.activation(RN[:, 2 * (g % 2) + tt, D * b:D * b + D],
                                                   ps[6 + tt][:, D * b:D * b + D], ACT.Identity,
                                                   bias=m.nmr[:, j:j + 1], scale=m.rstd[:, j:j + 1])
                    ins.then_inc(rn_ready, 1)

        @block.tensor
        def _(pe):
            def forward(g, k):
                n = 2 * g + k
                if n >= 2:
                    pe.wait_ge(prod_ready, n - 1)
                for i, ft in enumerate((k, 2 + k)):
                    for st in range(TPB):
                        ins = pe.matmul(ps[2 * (n % 2) + i], FW[:, st, P * ft:P * ft + P],
                                        XN[:, 2 * CB * g + st:2 * CB * (g + 1):2, :], start=(st == 0), stop=(st == TPB - 1))
                ins.then_inc(fwd_mm, 1)

            def inverse(g):
                pe.wait_ge(ys_ready, 2 * g + 2)
                for tt in range(TPB):
                    if g >= 1:
                        pe.wait_ge(rn_ready, 2 * (g - 1) + tt + 1)
                    for ft in range(NFT):
                        ins = pe.matmul(ps[6 + tt], IV[:, ft, P * tt:P * tt + P], YS[:, NFT * (g % 2) + ft, :],
                                        start=(ft == 0), stop=(ft == NFT - 1))
                    ins.then_inc(inv_mm, 1)

            pe.wait_ge(e2_ready, 1)
            pe.wait_ge(e1_ready, 1)
            for h in range(D):
                ins = pe.matmul(ps[h // 32][0:LF, LF * (h % 32):LF * (h % 32) + LF], SINA[:, :, h], SIN2[:, :, h],
                                start=True, stop=True)
                if h % 32 == 31:
                    ins.then_inc(kdig_mm, 1)
            pe.wait_ge(dct_in, 48)
            pe.wait_ge(kdig_sb, 4)
            for b in range(LF):
                ins = pe.transpose(ps[4][:, LF * b:LF * b + LF], KDIG[0:LF, b, :], t.ID[0:LF, 0:LF])
            ins.then_inc(kch_mm, 1)
            pe.wait_ge(kch_sb, 1)
            for i in range(TPB):
                ins = pe.transpose(ps[5][:, D * i:D * i + D], KCH[:, P * i:P * i + P], t.ID)
            ins.then_inc(klag_mm, 1)
            pe.wait_ge(klag_sb, 1)
            for ft in range(NFT):
                for st in range(TPB):
                    ins = pe.matmul(ps[4][:, D * ft:D * ft + D], FW[:, st, P * ft:P * ft + P], KLAG[:, st, :],
                                    start=(st == 0), stop=(st == TPB - 1))
            ins.then_inc(kf_mm, 1)
            pe.wait_ge(xn_ready, 1)
            for g in range(NCG):
                for k in range(2):
                    forward(g, k)
                if g >= 1:
                    inverse(g - 1)
            inverse(NCG - 1)

        @block.vector
        def _(dve):
            def link(ins):
                link.n += 1
                ins.then_inc(dve_step, 1)
                dve.wait_ge(dve_step, link.n)
            link.n = 0
            tt_, ts, stt = dve.tensor_tensor, dve.tensor_scalar, dve.scalar_tensor_tensor

            def turn_rest(phase, whole):
                link(ts(whole, phase, 1.0 / (2 * np.pi), ROUND, ALU.mult, ALU.add))
                link(ts(whole, whole, -ROUND, None, ALU.add))
                link(stt(phase, whole, -TWO_PI_HI, phase, ALU.mult, ALU.add))
                link(stt(phase, whole, -TWO_PI_LO, phase, ALU.mult, ALU.add))
                return ts(phase, phase, PI_IN, -PI_IN, ALU.min, ALU.max)

            EA, DTC = PRM[:, LAR, :], PRM[:, DT, :]
            AR, R1, R16, E1R, SN = (TMP[:, i, :] for i in (0, 1, 2, 3, 4))
            CS = TMP[:, 5, :]
            dve.wait_ge(exps, 1)
            tt_(AR, EA, DTC, ALU.mult).then_inc(decay_ready, 1)
            link(tt_(R1, PRM[:, AIM, :], DTC, ALU.mult))
            link(ts(R16, R1, float(LF), None, ALU.mult))
            link(turn_rest(TMP[:, 1:3, :], TMP[:, 6:8, :]))
            for b in range(LF):
                ins = ts(SIN2[:, b, :], R1, float(b), OFF[:, 0:1], ALU.mult, ALU.add)
            link(ins)
            turn_rest(SIN2, KQ).then_inc(phase_ready, 1)
            ts(SN, R1, 1.0, None, ALU.mult)
            link(ts(CS, R1, np.pi / 2, None, ALU.add))
            turn_rest(TMP[:, 4:6, :], TMP[:, 6:8, :]).then_inc(phase_ready, 1)
            for a in range(LF):
                ts(SINA[:, a, :], R16, float(a), OFF[:, 1:2], ALU.mult, ALU.add)
                ins = ts(SINB[:, a, :], R16, float(a), OFF[:, 2:3], ALU.mult, ALU.add)
            link(ins)
            turn_rest(SINA, KQ).then_inc(phase_ready, 1)
            link(ts(KQ[:, 0, 0:1], KQ[:, 0, 0:1], 0.0, None, ALU.mult))
            turn_rest(SINB, KQ).then_inc(phase_ready, 1)
            ER, EI, T0, T1, NR, NI, INV, CTR, CTI, SQ = (TMP[:, i, :] for i in range(8, 18))
            CRE, CIM, AIMC = PRM[:, C_RE, :], PRM[:, C_IM, :], PRM[:, AIM, :]
            dve.wait_ge(mags, 1)
            dve.wait_ge(sines, 2)
            EXD = MAG2[:, 1, :]
            tt_(EI, EXD, SN, ALU.mult)
            tt_(SQ, AIMC, AIMC, ALU.mult)
            link(tt_(ER, EXD, CS, ALU.mult))
            tt_(T1, EA, EA, ALU.mult)
            link(ts(ER, ER, -1.0, None, ALU.add))
            link(tt_(SQ, SQ, T1, ALU.add))
            dve.reciprocal(INV, SQ)
            tt_(NR, CRE, ER, ALU.mult)
            tt_(T0, CIM, EI, ALU.mult)
            tt_(NI, CRE, EI, ALU.mult)
            link(tt_(T1, CIM, ER, ALU.mult))
            tt_(NR, NR, T0, ALU.subtract)
            link(tt_(NI, NI, T1, ALU.add))
            tt_(T0, NI, AIMC, ALU.mult)
            tt_(T1, NR, EA, ALU.mult)
            tt_(CTI, NR, AIMC, ALU.mult)
            link(tt_(ER, NI, EA, ALU.mult))
            tt_(CTR, T0, T1, ALU.subtract)
            link(stt(CTI, CTI, -1.0, ER, ALU.mult, ALU.subtract))
            tt_(CTR, CTR, INV, ALU.mult)
            link(tt_(CTI, CTI, INV, ALU.mult))
            dve.wait_ge(sines, 4)
            dve.wait_ge(mags, 2)
            tt_(SINA, SINA, CTR.rearrange("p (o h) -> p o h", o=1).broadcast_to([P, LF, D]), ALU.mult)
            link(tt_(SINB, SINB, CTI.rearrange("p (o h) -> p o h", o=1).broadcast_to([P, LF, D]), ALU.mult))
            link(tt_(SINA, SINA, SINB, ALU.add))
            tt_(SINA, SINA, MAG1, ALU.mult).then_inc(e1_ready, 1)

            dve.wait_ge(x_in, 32)
            for i in range(NT):
                ins = dve.bn_stats(t.STATS[:, i, :], t.RES[:, i, :])
            link(ins)
            m = rows_of(t.NRM, 0, NT)
            norm_statistics(dve, link, t.STATS[:, 0:NT, :], m).then_inc(x_var, 1)
            dve.wait_ge(x_rstd, 1)
            for i in range(NT):
                ins = ts(XN[:, i, :], t.RES[:, i, :], m.mean[:, i:i + 1], m.rstd[:, i:i + 1], ALU.subtract, ALU.mult)
            ins.then_inc(xn_ready, 1)

            dve.wait_ge(kch_mm, 1)
            dve.wait_ge(ln_in, 48)
            link(dve.tensor_copy(KCH.rearrange("p (a b) -> p b a", b=LF), ps[4][:, 0:SEQ].rearrange("p (b a) -> p b a", a=LF)))
            ts(KCH[:, 0:1], KCH[:, 0:1], DCOL, 1.0, ALU.add, ALU.add).then_inc(kch_sb, 1)
            dve.wait_ge(kf_mm, 1)
            kf = ps[4].rearrange("p (f h) -> p f h", h=D)
            FA, FB, FD = SPK[:, 0], SPK[:, 1], SPK[:, 2]
            dve.tensor_copy(FA, kf[:, 0:2, :])
            dve.tensor_copy(FD[:, 1, :], kf[:, 1, :])
            dve.tensor_copy(FB[:, 1, :], kf[:, 3, :])
            ts(FB[:, 0, :], kf[:, 2, :], KEEP[:, 0:1], None, ALU.mult)
            link(ts(SPK[:, 3, 0, :], kf[:, 2, :], KEEP[:, 1:2], None, ALU.mult))
            link(stt(FD[:, 0, :], kf[:, 0, :], KEEP[:, 0:1], SPK[:, 3, 0, :], ALU.mult, ALU.add))

            def wide(f):
                return f.rearrange("p (o h) -> p o h", o=1).broadcast_to([P, CB, D])

            def products(g, k):
                n = 2 * g + k
                dve.wait_ge(fwd_mm, n + 1)
                if n >= 1:
                    dve.wait_ge(ys_ready, n)
                re = ps[2 * (n % 2)].rearrange("p (b h) -> p b h", h=D)
                im = ps[2 * (n % 2) + 1].rearrange("p (b h) -> p b h", h=D)
                out = M4.rearrange("p k (b h) -> p k b h", h=D)
                tt_(out[:, 0], re, wide(FA[:, k, :]), ALU.mult)
                tt_(out[:, 1], im, wide(FB[:, k, :]), ALU.mult)
                tt_(out[:, 2], re, wide(FB[:, k, :]), ALU.mult)
                tt_(out[:, 3], im, wide(FD[:, k, :]), ALU.mult).then_inc(prod_ready, 1)

            def statistics(g):
                for tt in range(TPB):
                    dve.wait_ge(inv_mm, 2 * g + tt + 1)
                    for b in range(CB):
                        ins = dve.bn_stats(t.STATS[:, 4 * tt + b, :], ps[6 + tt][:, D * b:D * b + D])
                link(ins)
                mg = rows_of(t.NRM, NT + 8 * g, NT + 8 * g + 8)
                norm_statistics(dve, link, t.STATS[:, 0:8, :], mg).then_inc(r_var, 1)
                dve.wait_ge(r_rstd, g + 1)
                stt(mg.nmr, mg.mean, -1.0, mg.rstd, ALU.mult, ALU.mult).then_inc(r_nmr, 1)

            for g in range(NCG):
                for k in range(2):
                    products(g, k)
                if g >= 1:
                    statistics(g - 1)
            statistics(NCG - 1)
def weights_stage(nc, t):
    with ExitStack() as ctx:
        def sem(name):
            return ctx.enter_context(nc.semaphore("w_" + name))
        STG = t.arena[:, 0:4 * HID].rearrange("p (s n) -> p s n", n=HID)
        jobs = []
        for e in range(NX):
            jobs.append((t.dram["w1"][e], t.W1H[:, e, :], t.W1L[:, e, :], HID, WS))
            jobs.append((t.dram["w2"][e].rearrange("(m p) d -> p m d", p=P), t.W2H[:, e], t.W2L[:, e], HID, WS))
        jobs.append((t.dram["gate_w"], t.GWH, t.GWL, NE, WS))
        for k in range(2):
            s = slice(HG * k, HG * k + HG)
            jobs.append((t.dram["w_qk"][:, s, :], t.QKWH[:, s, :], t.QKWL[:, s, :], HG * P, WQ))
        jobs.append((t.dram["w_vo"], t.VOWH, t.VOWL, 2 * D, WQ))
        loaded, high, low = [sem(f"loaded{i}") for i in range(4)], sem("high"), sem("low")
        small = sem("small")
        block = ctx.enter_context(nc.Block())

        def slot(i):
            v = STG[:, i % 4, 0:jobs[i][3]]
            return v.rearrange("p (m d) -> p m d", d=D) if len(jobs[i][1].shape) == 3 else v

        @block.sync
        def _(sp):
            sp.dma_start(t.B1, t.dram["b1"]).then_inc(small, 16)
            sp.dma_start(t.B2, t.dram["b2"]).then_inc(small, 16)
            sp.dma_start(t.GB[:, 0, :], t.dram["gate_b"]).then_inc(small, 16)
            sp.dma_start(t.GB[:, 1, :], t.dram["rank"]).then_inc(small, 16)
            for i, job in enumerate(jobs):
                if i >= 4:
                    sp.wait_ge(low, i - 3)
                sp.dma_start(slot(i), job[0]).then_inc(loaded[i % 4], 16)
            sp.wait_ge(small, 64)

        @block.scalar
        def _(act):
            for i, job in enumerate(jobs):
                act.wait_ge(loaded[i % 4], 16 * (i // 4 + 1))
                nc.scalar.activation(job[1], slot(i), ACT.Copy, scale=job[4]).then_inc(high, 1)

        @block.vector
        def _(dve):
            for i, job in enumerate(jobs):
                dve.wait_ge(high, i + 1)
                dve.scalar_tensor_tensor(job[2], slot(i), job[4], job[1], ALU.mult, ALU.subtract).then_inc(low, 1)


def norm_stage(nc, t, tag):
    with ExitStack() as ctx:
        def sem(name):
            return ctx.enter_context(nc.semaphore(f"n{tag}_{name}"))
        dve_step, var, rstd, xn = sem("dve_step"), sem("var"), sem("rstd"), sem("xn")
        turned, high, low = sem("turned"), sem("high"), sem("low")
        m = rows_of(t.NRM, 0, NT)
        block = ctx.enter_context(nc.Block())

        @block.gpsimd
        def _(pool):
            pool.wait_ge(var, 1)
            nc.gpsimd.tensor_tensor(m.rstd, m.vareps, t.MHALF[:, 0:NT], ALU.pow).then_inc(rstd, 1)

        @block.tensor
        def _(pe):
            for g in range(NG):
                pe.wait_ge(xn, g + 1)
                if g >= 4:
                    pe.wait_ge(low, g - 3)
                for j in range(GT):
                    ins = pe.transpose(t.psum[g % 4][:, P * j:P * j + P], t.XN[:, GT * g + j, :], t.ID)
                ins.then_inc(turned, 1)

        @block.scalar
        def _(act):
            for g in range(NG):
                act.wait_ge(turned, g + 1)
                nc.scalar.activation(t.XTH[:, BANK * g:BANK * (g + 1)], t.psum[g % 4], ACT.Copy).then_inc(high, 1)

        @block.vector
        def _(dve):
            def link(ins):
                link.n += 1
                ins.then_inc(dve_step, 1)
                dve.wait_ge(dve_step, link.n)
            link.n = 0
            for i in range(NT):
                ins = dve.bn_stats(t.STATS[:, i, :], t.RES[:, i, :])
            link(ins)
            norm_statistics(dve, link, t.STATS, m).then_inc(var, 1)
            dve.wait_ge(rstd, 1)
            for g in range(NG):
                for i in range(GT * g, GT * g + GT):
                    ins = dve.tensor_scalar(t.XN[:, i, :], t.RES[:, i, :], m.mean[:, i:i + 1], m.rstd[:, i:i + 1],
                                            ALU.subtract, ALU.mult)
                ins.then_inc(xn, 1)
            for g in range(NG):
                dve.wait_ge(high, g + 1)
                s = slice(BANK * g, BANK * (g + 1))
                dve.tensor_tensor(t.XTL[:, s], t.psum[g % 4], t.XTH[:, s], ALU.subtract).then_inc(low, 1)


def route_stage(nc, t, tag):
    with ExitStack() as ctx:
        def sem(name):
            return ctx.enter_context(nc.semaphore(f"r{tag}_{name}"))
        dve_step, gate_mm, gap, ratio, comb, turned, combt, bias_mm, added = (sem(n) for n in (
            "dve_step", "gate_mm", "gap", "ratio", "comb", "turned", "combt", "bias_mm", "added"))
        n = NT * NE
        at = t.arena
        L, EQ, V, O1, O2 = (at[:, i * n:(i + 1) * n].rearrange("p (t e) -> p t e", e=NE) for i in range(5))
        S = at[:, 5 * n:5 * n + 8 * NT].rearrange("p (k t) -> p k t", t=NT)
        M1, M2, MV, GAP, DEN = (S[:, i, :] for i in range(5))
        CT = at[0:NX, 2048:2048 + NT * P]
        block = ctx.enter_context(nc.Block())

        def wide(v):
            return v.rearrange("p (t o) -> p t o", o=1).broadcast_to([P, NT, NE])

        @block.tensor
        def _(pe):
            for i in range(NT):
                for k, (x, w) in enumerate(((t.XTH, t.GWH), (t.XTL, t.GWH), (t.XTH, t.GWL))):
                    ins = pe.matmul(t.psum[4][:, NE * i:NE * i + NE], x[:, P * i:P * i + P], w, start=(k == 0), stop=(k == 2))
            ins.then_inc(gate_mm, 1)
            pe.wait_ge(comb, 1)
            for g in range(NG):
                if g >= 2:
                    pe.wait_ge(combt, g - 1)
                for j in range(GT):
                    ins = pe.transpose(t.psum[g % 2][0:NX, P * j:P * j + P], t.COMB[:, GT * g + j, :], t.ID)
                ins.then_inc(turned, 1)
            for g in range(NG):
                pe.wait_ge(combt, g + 1)
                if g >= 2:
                    pe.wait_ge(added, g - 1)
                for j in range(GT):
                    i = GT * g + j
                    ins = pe.matmul(t.psum[2 + g % 2][:, D * j:D * j + D], CT[:, P * i:P * i + P], t.B2, start=True, stop=True)
                ins.then_inc(bias_mm, 1)

        @block.scalar
        def _(act):
            act.wait_ge(gap, 1)
            nc.scalar.activation(GAP, GAP, ACT.Exp).then_inc(ratio, 1)
            for g in range(NG):
                act.wait_ge(turned, g + 1)
                nc.scalar.activation(CT[:, BANK * g:BANK * (g + 1)], t.psum[g % 2][0:NX, :], ACT.Copy).then_inc(combt, 1)

        @block.vector
        def _(dve):
            def link(ins):
                link.n += 1
                ins.then_inc(dve_step, 1)
                dve.wait_ge(dve_step, link.n)
            link.n = 0
            tt, ts, stt = dve.tensor_tensor, dve.tensor_scalar, dve.scalar_tensor_tensor
            rank = t.GB[:, 1:2, :].broadcast_to([P, NT, NE])

            def first_of_largest(out, logits, largest):
                link(dve.tensor_reduce(largest, logits, AX.X, ALU.max))
                link(tt(EQ, logits, wide(largest), ALU.is_equal))
                link(tt(V, EQ, rank, ALU.mult))
                link(dve.tensor_reduce(MV, V, AX.X, ALU.max))
                link(tt(out, V, wide(MV), ALU.is_equal))

            dve.wait_ge(gate_mm, 1)
            link(stt(L, t.psum[4][:, 0:n].rearrange("p (t e) -> p t e", e=NE), 1.0 / WS,
                     t.GB[:, 0:1, :].broadcast_to([P, NT, NE]), ALU.mult, ALU.add))
            first_of_largest(O1, L, M1)
            link(stt(L, O1, LOWEST, L, ALU.mult, ALU.add))
            first_of_largest(O2, L, M2)
            tt(GAP, M2, M1, ALU.subtract).then_inc(gap, 1)
            dve.wait_ge(ratio, 1)
            link(ts(DEN, GAP, 1.0, None, ALU.add))
            link(dve.reciprocal(M1, DEN))
            link(tt(M2, GAP, M1, ALU.mult))
            tt(O1, O1, wide(M1), ALU.mult)
            link(tt(O2, O2, wide(M2), ALU.mult))
            dve.memset(t.COMB[:, :, NE:NX], 1.0)
            tt(t.COMB[:, :, 0:NE], O1, O2, ALU.add).then_inc(comb, 1)
            for g in range(NG):
                dve.wait_ge(bias_mm, g + 1)
                res = t.RES[:, GT * g:GT * g + GT, :]
                tt(res, res, t.psum[2 + g % 2].rearrange("p (j d) -> p j d", d=D), ALU.add).then_inc(added, 1)
            dve.wait_ge(turned, NG)
            link(ts(t.COMBE, t.COMBE, 1.0 / WS, None, ALU.mult))


def experts_stage(nc, t, tag):
    with ExitStack() as ctx:
        def sem(name):
            return ctx.enter_context(nc.semaphore(f"x{tag}_{name}"))
        up_mm, hidden, split, down_mm, merged, high, primed = (sem(n) for n in (
            "up_mm", "hidden", "split", "down_mm", "merged", "high", "primed"))
        HF = t.arena[:, 0:2 * MT * BANK].rearrange("p (s m n) -> p s m n", m=MT, n=BANK)
        H16 = t.arena[:, 2 * MT * BANK:4 * MT * BANK].bitcast(F16).rearrange("p (s k m n) -> p s k m n", s=2, k=2, m=MT)
        BIAS = t.arena[:, 4 * MT * BANK:4 * MT * BANK + MT]
        bias_set = sem("bias_set")
        block = ctx.enter_context(nc.Block())

        @block.tensor
        def _(pe):
            with pe.Fori(0, NX) as e:
                def up(g):
                    for m in range(MT):
                        pe.wait_ge(hidden, MT * NG * e + MT * g + m + 1)
                        ms, xs = slice(P * m, P * m + P), slice(BANK * g, BANK * (g + 1))
                        pe.matmul(t.psum[m], t.W1H[:, e, ms], t.XTH[:, xs], start=True, stop=False)
                        pe.matmul(t.psum[m], t.W1H[:, e, ms], t.XTL[:, xs], start=False, stop=False)
                        pe.matmul(t.psum[m], t.W1L[:, e, ms], t.XTH[:, xs], start=False, stop=True).then_inc(up_mm, 1)

                def down(g):
                    pe.wait_ge(split, NG * e + g + 3)
                    pe.wait_ge(merged, NG * e + g + 1)
                    for j in range(GT):
                        out = t.psum[4 + g % 2][:, D * j:D * j + D]
                        for m in range(MT):
                            js = slice(P * j, P * j + P)
                            hh, hl = H16[:, g % 2, 0, m, js], H16[:, g % 2, 1, m, js]
                            pe.matmul(out, hh, t.W2H[:, e, m, :], start=(m == 0), stop=False)
                            pe.matmul(out, hh, t.W2L[:, e, m, :], start=False, stop=False)
                            ins = pe.matmul(out, hl, t.W2H[:, e, m, :], start=False, stop=(m == MT - 1))
                    ins.then_inc(down_mm, 1)

                for g in range(NG):
                    up(g)
                    if g >= 1:
                        down(g - 1)
                down(NG - 1)

        @block.scalar
        def _(act):
            nc.scalar.activation(HF[0:1, 0, 0, 0:1], t.MHALF[0:1, 0:1], ACT.Gelu).then_inc(primed, 1)
            act.wait_ge(primed, 1)
            act.sem_inc(hidden, MT)
            with act.Fori(0, NX) as e:
                act.copy(BIAS, t.B1[:, e, :]).then_inc(bias_set, 1)
                act.wait_ge(bias_set, e + 1)
                for g in range(NG):
                    act.wait_ge(split, NG * e + g + 1)
                    for m in range(MT):
                        act.wait_ge(up_mm, MT * NG * e + MT * g + m + 1)
                        nc.scalar.activation(HF[:, g % 2, m, :], t.psum[m], ACT.Gelu,
                                             bias=BIAS[:, m:m + 1], scale=1.0 / WS).then_inc(hidden, 1)
                act.wait_ge(hidden, MT * NG * e + MT * NG + MT)

        @block.vector
        def _(dve):
            dve.sem_inc(split, 2)
            dve.sem_inc(down_mm, 2)
            dve.sem_inc(merged, 2)
            with dve.Fori(0, NX) as e:
                def split_step(g):
                    s = NG * e + g
                    dve.wait_ge(down_mm, s + 1)
                    dve.wait_ge(hidden, MT * s + 2 * MT)
                    dve.tensor_copy(H16[:, g % 2, 0], HF[:, g % 2]).then_inc(high, 1)
                    dve.wait_ge(high, s + 1)
                    dve.tensor_tensor(H16[:, g % 2, 1], HF[:, g % 2], H16[:, g % 2, 0], ALU.subtract).then_inc(split, 1)

                def merge_step(g):
                    dve.wait_ge(down_mm, NG * e + g + 3)
                    for j in range(GT):
                        res = t.RES[:, GT * g + j, :]
                        ins = dve.scalar_tensor_tensor(res, t.psum[4 + g % 2][:, D * j:D * j + D],
                                                       t.COMBE[:, e, GT * g + j:GT * g + j + 1], res, ALU.mult, ALU.add)
                    ins.then_inc(merged, 1)

                for g in range(NG):
                    split_step(g)
                    if g >= 1:
                        merge_step(g - 1)
                merge_step(NG - 1)
def attention_stage(nc, t):
    with ExitStack() as ctx:
        def sem(name):
            return ctx.enter_context(nc.semaphore(f"a_{name}"))
        at = [0]

        def carve(dt, *shape):
            n = int(np.prod(shape))
            words = n if dt == F32 else n // 2
            v = t.arena[:, at[0]:at[0] + words]
            at[0] += words
            v = v if dt == F32 else v.bitcast(dt)
            names = "abcde"[:len(shape)]
            if len(shape) > 1:
                v = v.rearrange(f"p ({' '.join(names)}) -> p {' '.join(names)}", **dict(zip(names, shape)))
            return v

        QPAD = [carve(F16, HG, GH, SEQ) for _ in range(2)]
        KST = [carve(F16, HG, SEQ) for _ in range(2)]
        QST = carve(F16, HG, SEQ)
        HI = carve(F16, 2, SEQ)
        V32 = [carve(F32, TPB, NH, 32) for _ in range(2)]
        PR = [carve(F32, 3, BANK) for _ in range(2)]
        OT = [carve(F32, HG, SEQ) for _ in range(2)]
        ATT = carve(F32, TPB, D)
        ATH, ATL = carve(F16, SEQ), carve(F16, SEQ)
        MX = carve(F32, TPB, GH, HG)
        M16 = carve(F16, TPB, GH, 2, HG)
        MROW = carve(F16, SEQ)
        RC = carve(F32, TPB, NH)
        IDB, MASKB, MASKT = carve(BF16, P), carve(BF16, GH, P), carve(BF16, GH, P)
        ID16 = carve(F16, P)
        CWF, CRF = carve(F32, 2 * HG, P), carve(F32, SEQ)
        CW, CR = carve(F16, 2 * HG, P), carve(F16, SEQ)
        LOWROW = carve(F32, 2)
        XH = t.XTH.rearrange("p (b n) -> p b n", n=SEQ)
        XL = t.XTL.rearrange("p (b n) -> p b n", n=SEQ)
        RESB = t.RES.rearrange("p (b t) d -> p b (t d)", t=TPB)
        ps = t.psum

        (consts_in, cleared, masks, cast, ready, m_high, rc_set) = (sem(n) for n in (
            "consts_in", "cleared", "masks", "cast", "ready", "m_high", "rc_set"))
        (proj, hi, parts, vset, qpad_in, m_mm, m_red, m16, mt_mm, mrow_set, mrow_in) = (sem(n) for n in (
            "proj", "hi", "parts", "vset", "qpad_in", "m_mm", "m_red", "m16", "mt_mm", "mrow_set", "mrow_in"))
        (st_mm, exps, av_mm, ot_set, ft_mm, att, fa_mm, att_hi, att_lo, fo_mm, added) = (sem(n) for n in (
            "st_mm", "exps", "av_mm", "ot_set", "ft_mm", "att", "fa_mm", "att_hi", "att_lo", "fo_mm", "added"))
        block = ctx.enter_context(nc.Block())

        def after(eng, s, n):
            if not (isinstance(n, int) and n <= 0):
                eng.wait_ge(s, n)

        def batches(eng, body, lead=None):
            if lead:
                lead()
            body(0, 0, True, False)
            body(1, 1, False, False)
            with eng.Fori(0, (NB - 4) // 2) as k:
                for i in range(2):
                    body(2 * k + (2 + i), i, False, False)
            body(NB - 2, 0, False, False)
            body(NB - 1, 1, False, True)

        @block.sync
        def _(sp):
            sp.dma_start(CWF[0:3], t.dram["cw"]).then_inc(consts_in, 16)
            sp.dma_start(CRF[0:3], t.dram["cr"]).then_inc(consts_in, 16)
            sp.dma_start(LOWROW, t.dram["lowrow"]).then_inc(consts_in, 16)
            after(sp, ready, 1)

            def spread_q(c, r):
                after(sp, parts, 8 * c + 7)
                for g in range(GH):
                    q = slice(32 * g, 32 * g + 32)
                    sp.dma_start(QPAD[r][q, :, g, :], QST[q, :, :]).then_inc(qpad_in, 16)

            def spread_m(b, q):
                after(sp, mrow_set, b + 1)
                for g in range(GH):
                    for c in range(2):
                        row = 32 * g + 26 + c
                        src = 8 * g + 4 * c
                        sp.dma_start(QPAD[q][row:row + 1, :, g, :], MROW[src:src + HG, :]).then_inc(mrow_in, 16)

            def body(b, q, first, last):
                spread_m(b, q)
                if not last:
                    spread_q(b + 1, 1 - q)
            batches(sp, body, lambda: spread_q(0, 0))

        @block.gpsimd
        def _(pool):
            for v in (QPAD[0], QPAD[1], V32[0], V32[1], IDB, MASKB, MASKT):
                nc.gpsimd.memset(v, 0.0).then_inc(cleared, 1)
            pool.wait_ge(cleared, 7)
            for v in V32:
                nc.gpsimd.memset(v[:, :, :, 8:9], 1.0).then_inc(masks, 1)
            nc.gpsimd.affine_select(out=IDB, in_=IDB, compare_op=ALU.not_equal, fill=1.0, base=0,
                                    pattern=[[-1, P]], channel_multiplier=1).then_inc(masks, 1)
            nc.gpsimd.affine_select(out=MASKB, in_=MASKB, compare_op=ALU.is_ge, fill=-1.0e30, base=0,
                                    pattern=[[0, GH], [-1, P]], channel_multiplier=1).then_inc(masks, 1)
            nc.gpsimd.affine_select(out=MASKT, in_=MASKT, compare_op=ALU.is_ge, fill=-1.0e30, base=0,
                                    pattern=[[0, GH], [1, P]], channel_multiplier=-1).then_inc(masks, 1)

        @block.tensor
        def _(pe):
            def project(c, G, k):
                n = 2 * G + k
                if G > 0:
                    after(pe, parts, 8 * c + n - 1)
                for i, (w, x) in enumerate(((t.QKWH, XH), (t.QKWH, XL), (t.QKWL, XH))):
                    pe.matmul(ps[k][:, 0:SEQ], w[:, HG * k + G, :], x[:, c, :], start=(i == 0), stop=False)
                pe.matmul(ps[k][:, 0:SEQ], CW[0:3, HG * k + G, :], CR[0:3, :], start=False, stop=True).then_inc(proj, 1)

            def values(c):
                after(pe, parts, 8 * c + 7)
                for tile in range(TPB):
                    js = slice(P * tile, P * tile + P)
                    for i, (x, w) in enumerate(((XH, t.VOWH), (XL, t.VOWH), (XH, t.VOWL))):
                        ins = pe.matmul(ps[0][:, js], x[:, c, js], w[:, 0:D], start=(i == 0), stop=(i == 2))
                ins.then_inc(proj, 1)

            def maxima(c, r, G):
                if G == 0:
                    after(pe, qpad_in, 64 * c + 64)
                    after(pe, parts, 8 * c + 8)
                for k in range(3):
                    n = 3 * G + k
                    bank = ps[2 + n % 2]
                    after(pe, m_red, 12 * c + n - 1)
                    if k == 0:
                        pe.matmul(bank, IDB, MASKB.rearrange("p g n -> p (g n)"), start=True, stop=False)
                        for g in range(GH):
                            ins = pe.matmul(bank[:, P * g:P * g + P], QPAD[r][:, G, g, 0:P], KST[r][:, G, 0:P],
                                            start=False, stop=(g == GH - 1))
                    else:
                        out = bank.rearrange("p (h t n) -> p h t n", t=TPB, n=P)
                        pe.matmul(out[:, :, 1, :], IDB, MASKB[:, 0:2, :], start=True, stop=False, skip_group_check=True)
                        for h in range(2):
                            g = 2 * (k - 1) + h
                            for tile in range(TPB):
                                ins = pe.matmul(out[:, h, tile, :], QPAD[r][:, G, g, P:2 * P],
                                                KST[r][:, G, P * tile:P * tile + P], start=False,
                                                stop=(h == 1 and tile == 1), skip_group_check=True)
                    ins.then_inc(m_mm, 1)

            def turn_maxima(b):
                after(pe, m16, b + 1)
                after(pe, ot_set, 2 * b)
                for tile in range(TPB):
                    ins = pe.transpose(ps[4].bitcast(F16)[0:32, P * tile:P * tile + P],
                                       M16[:, tile].rearrange("p g c h -> p (g c h)"), ID16)
                ins.then_inc(mt_mm, 1)

            def scores(b, q, G):
                if G == 0:
                    after(pe, mrow_in, 128 * b + 128)
                after(pe, exps, 4 * b + G)
                for a in range(2):
                    out = ps[5 + a].rearrange("p (h t n) -> p h t n", t=TPB, n=P)
                    pe.matmul(out[:, :, 0, :], IDB, MASKT[:, 0:2, :], start=True, stop=False, skip_group_check=True)
                    pe.matmul(ps[5 + a], KST[q][:, G, 0:P], QPAD[q][:, G, 2 * a:2 * a + 2, :], start=False, stop=True,
                              skip_group_check=True)
                pe.matmul(ps[7], IDB, MASKT.rearrange("p g n -> p (g n)"), start=True, stop=False)
                pe.matmul(ps[7], KST[q][:, G, P:2 * P], QPAD[q][:, G, :, P:2 * P], start=False, stop=True).then_inc(st_mm, 1)

            def weigh(b, q, G):
                after(pe, exps, 4 * b + G + 1)
                if G == 0:
                    after(pe, mrow_set, b + 1)
                    after(pe, vset, b + 1)
                if G == 2:
                    after(pe, ot_set, 2 * b + 1)
                half = ps[4][:, SEQ * (G % 2):SEQ * (G % 2) + SEQ]
                for g in range(GH):
                    out = half[32 * g:32 * g + 32, :]
                    early = PR[G % 2][:, g // 2, SEQ * (g % 2):SEQ * (g % 2) + SEQ]
                    late = PR[G % 2][:, 2, P * g:P * g + P]
                    pe.matmul(out, V32[q][:, 0, 4 * G + g, :], early, start=True, stop=False)
                    ins = pe.matmul(out[:, P:2 * P], V32[q][:, 1, 4 * G + g, :], late, start=False, stop=True)
                ins.then_inc(av_mm, 1)

            def turn_back(b, q):
                after(pe, ot_set, 2 * b + 2)
                after(pe, added, b)
                for tile in range(TPB):
                    for G in range(HG):
                        ins = pe.transpose(ps[tile][:, P * G:P * G + P], OT[q][:, G, P * tile:P * tile + P], t.ID)
                    ins.then_inc(ft_mm, 1)

            def turn_out(b):
                after(pe, att, 2 * b + 2)
                for tile in range(TPB):
                    ins = pe.transpose(ps[0][:, P * tile:P * tile + P], ATT[:, tile, :], t.ID)
                ins.then_inc(fa_mm, 1)

            def project_out(b):
                after(pe, att_lo, b + 1)
                for tile in range(TPB):
                    js = slice(P * tile, P * tile + P)
                    for i, (x, w) in enumerate(((ATH, t.VOWH), (ATL, t.VOWH), (ATH, t.VOWL))):
                        ins = pe.matmul(ps[1][:, js], x[:, js], w[:, D:2 * D], start=(i == 0), stop=(i == 2))
                ins.then_inc(fo_mm, 1)

            def body(b, q, first, last):
                r = 1 - q
                if not last:
                    after(pe, vset, b + 1)
                    after(pe, added, b - 1)
                    for G in range(2):
                        project(b + 1, G, 0)
                        project(b + 1, G, 1)
                turn_maxima(b)
                if not last:
                    for G in range(2, HG):
                        project(b + 1, G, 0)
                        project(b + 1, G, 1)
                    values(b + 1)
                scores(b, q, 0)
                for G in range(HG):
                    if not last:
                        maxima(b + 1, r, G)
                    if not first:
                        if G == 0:
                            after(pe, vset, b + 2) if not last else None
                            turn_back(b - 1, r)
                        if G == 1:
                            turn_out(b - 1)
                        if G == 2:
                            project_out(b - 1)
                    if G < HG - 1:
                        scores(b, q, G + 1)
                    weigh(b, q, G)

            def lead():
                pe.wait_ge(cast, 3)
                pe.wait_ge(masks, 5)
                for G in range(HG):
                    project(0, G, 0)
                    project(0, G, 1)
                values(0)
                for G in range(HG):
                    maxima(0, 0, G)
            batches(pe, body, lead)
            turn_back(NB - 1, 1)
            turn_out(NB - 1)
            project_out(NB - 1)

        @block.scalar
        def _(act):
            act.wait_ge(consts_in, 48)
            nc.scalar.activation(CW[0:3], CWF[0:3], ACT.Copy).then_inc(cast, 1)
            nc.scalar.activation(CR[0:3], CRF[0:3], ACT.Copy).then_inc(cast, 1)
            nc.scalar.activation(ID16, t.ID, ACT.Copy).then_inc(cast, 1)
            nc.scalar.activation(RC[0:1, 0, 0:1], t.MHALF[0:1, 0:1], ACT.Exp).then_inc(cast, 1)
            act.wait_ge(cast, 4)
            act.sem_inc(ready, 1)

            def highs(c, G):
                for k in range(2):
                    n = 2 * G + k
                    after(act, proj, 9 * c + n + 1)
                    after(act, parts, 8 * c + n - 1)
                    nc.scalar.activation(HI[:, k, :], ps[k][:, 0:SEQ], ACT.Copy).then_inc(hi, 1)

            def values(c, r):
                after(act, proj, 9 * c + 9)
                after(act, av_mm, 4 * c - 4)
                if isinstance(c, int) and c == 0:
                    act.wait_ge(masks, 2)
                nc.scalar.activation(V32[r][:, :, :, 0:8], ps[0][:, 0:SEQ].rearrange("p (t h d) -> p t h d", t=TPB, d=8),
                                     ACT.Copy).then_inc(vset, 1)

            def expo(b, G):
                after(act, st_mm, 4 * b + G + 1)
                after(act, av_mm, 4 * b + G - 1)
                nc.scalar.activation(PR[G % 2], ps3, ACT.Exp, scale=1.0 / LOGIT).then_inc(exps, 1)

            def take_out(b, q, half):
                after(act, av_mm, 4 * b + 2 * half + 2)
                nc.scalar.activation(OT[q][:, 2 * half:2 * half + 2, :], ps[4].rearrange("p (g n) -> p g n", n=SEQ),
                                     ACT.Copy).then_inc(ot_set, 1)

            def out_high(b):
                after(act, fa_mm, b + 1)
                nc.scalar.activation(ATH, ps[0][:, 0:SEQ], ACT.Copy).then_inc(att_hi, 1)

            ps3 = t.psum_all[:, 5:8, :]

            def body(b, q, first, last):
                r = 1 - q
                if not last:
                    highs(b + 1, 0)
                    highs(b + 1, 1)
                after(act, mt_mm, b + 1)
                after(act, mrow_in, 128 * b)
                nc.scalar.activation(MROW[0:32, :], ps[4].bitcast(F16)[0:32, 0:SEQ], ACT.Copy).then_inc(mrow_set, 1)
                if not last:
                    highs(b + 1, 2)
                    highs(b + 1, 3)
                    values(b + 1, r)
                expo(b, 0)
                expo(b, 1)
                for G in range(HG):
                    if G == 1 and not first:
                        out_high(b - 1)
                    if G == 1:
                        take_out(b, q, 0)
                    if G + 2 < HG:
                        expo(b, G + 2)
                take_out(b, q, 1)

            def lead():
                for G in range(HG):
                    highs(0, G)
                values(0, 0)
            batches(act, body, lead)
            out_high(NB - 1)

        @block.vector
        def _(dve):
            tt, ts, stt = dve.tensor_tensor, dve.tensor_scalar, dve.scalar_tensor_tensor
            dve.wait_ge(consts_in, 48)

            def split(c, r, G):
                for k in range(2):
                    n = 2 * G + k
                    after(dve, hi, 8 * c + n + 1)
                    if G == 0 and k == 0:
                        after(dve, qpad_in, 64 * c)
                    out = QST if k == 0 else KST[r]
                    stt(out[:, G, :], HI[:, k, :], LOWROW[:, k:k + 1], ps[k][:, 0:SEQ], ALU.mult, ALU.add).then_inc(parts, 1)

            def reduce(c, G):
                for k in range(3):
                    n = 3 * G + k
                    after(dve, m_mm, 12 * c + n + 1)
                    if k == 0:
                        out, src = MX[:, 0, :, G], ps[2 + n % 2].rearrange("p (g n) -> p g n", n=P)
                    else:
                        out, src = MX[:, 1, 2 * (k - 1):2 * k, G], ps[2 + n % 2].rearrange("p (g n) -> p g n", n=SEQ)
                    dve.tensor_reduce(out, src, AX.X, ALU.max).then_inc(m_red, 1)

            def split_maxima(c):
                after(dve, m_red, 12 * c + 12)
                after(dve, mt_mm, c)
                mx = MX.rearrange("p t g h -> p (t g) h")
                hi_m, lo_m = (M16[:, :, :, i, :].rearrange("p t g h -> p (t g) h") for i in range(2))
                ts(hi_m, mx, -1.0 / 1024, None, ALU.mult).then_inc(m_high, 1)
                dve.wait_ge(m_high, c + 1)
                stt(lo_m, mx, -1.0 / 1024, hi_m, ALU.mult, ALU.subtract).then_inc(m16, 1)

            def normalise(b, tile):
                after(dve, ft_mm, 2 * b + tile + 1)
                src = ps[tile].rearrange("p (h d) -> p h d", d=32)
                dve.reciprocal(RC[:, tile, :], src[:, :, 8]).then_inc(rc_set, 1)
                dve.wait_ge(rc_set, 2 * b + tile + 1)
                tt(ATT[:, tile, :].rearrange("p (h d) -> p h d", d=8), src[:, :, 0:8],
                   RC[:, tile, :].rearrange("p (h o) -> p h o", o=1).broadcast_to([P, NH, 8]), ALU.mult).then_inc(att, 1)

            def out_low(b):
                after(dve, att_hi, b + 1)
                tt(ATL, ps[0][:, 0:SEQ], ATH, ALU.subtract).then_inc(att_lo, 1)

            def add(b):
                after(dve, fo_mm, b + 1)
                stt(RESB[:, b, :], ps[1][:, 0:SEQ], 1.0 / (WQ * WQ), RESB[:, b, :], ALU.mult, ALU.add).then_inc(added, 1)

            def body(b, q, first, last):
                r = 1 - q
                if not last:
                    for G in range(HG):
                        split(b + 1, r, G)
                for G in range(HG):
                    if not last:
                        reduce(b + 1, G)
                    if not first:
                        if G == 0:
                            normalise(b - 1, 0)
                            normalise(b - 1, 1)
                        if G == 1:
                            out_low(b - 1)
                        if G == 2:
                            add(b - 1)
                if not last:
                    split_maxima(b + 1)

            def lead():
                for G in range(HG):
                    split(0, 0, G)
                for G in range(HG):
                    reduce(0, G)
                split_maxima(0)
            batches(dve, body, lead)
            normalise(NB - 1, 0)
            normalise(NB - 1, 1)
            out_low(NB - 1)
            add(NB - 1)
def host_tables():
    c = {}
    s = np.arange(SEQ)
    f = np.arange(SEQ)
    ang = 2 * np.pi * np.outer(s, f) / NFFT
    fwd = np.concatenate([np.cos(ang), -np.sin(ang)], 1)
    fwd[:, SEQ] = (-1.0) ** s
    inv = np.concatenate([2 * np.cos(ang.T), -2 * np.sin(ang.T)], 0) / NFFT
    inv[0] = 1.0 / NFFT
    inv[SEQ] = (-1.0) ** s / NFFT
    c["fwd"] = fwd.reshape(TPB, P, NFFT)
    c["inv"] = inv.reshape(NFT, P, SEQ)
    off = np.zeros((P, 4))
    off[:NM] = [np.pi / 2, np.pi / 2, np.pi, 0]
    off[NM:] = [np.pi, 0, np.pi / 2, 0]
    c["offsets"] = off
    keep = np.zeros((P, 2))
    keep[:, 0] = 1
    keep[0] = [0, 1]
    c["keep"] = keep
    c["rank"] = np.tile(np.arange(NE, 0, -1.0), (P, 1))
    slopes = 2.0 ** (-8.0 / NH * np.arange(1, NH + 1)) * LOGIT / WQ
    cw = np.zeros((3, 2, HG, GH, 32))
    cw[2, 0, :, :, 24:26] = WQ
    high = slopes.astype(np.float16).astype(np.float64)
    cw[0, 1, :, :, 24:26] = high.reshape(HG, GH, 1)
    cw[1, 1, :, :, 24:26] = (slopes - high).astype(np.float16).astype(np.float64).reshape(HG, GH, 1)
    cw[2, 1, :, :, 26:28] = 1024
    c["cw"] = cw.reshape(3, 2 * HG, P)
    c["cr"] = np.stack([np.arange(SEQ), np.arange(SEQ), np.ones(SEQ)])
    low = np.zeros((GH, 32, 2))
    low[:, 16:24, 0] = -1
    low[:, 8:16, 1] = -1
    low[:, 25, 1] = -1
    c["lowrow"] = low.reshape(P, 2)
    c["ident"] = np.eye(P)
    return {k: np.ascontiguousarray(v, dtype=np.float32) for k, v in c.items()}


def build(nc, dram):
    with ExitStack() as ctx:
        t = Bag()
        t.dram = dram

        def sb(name, shape, dt=F32):
            return ctx.enter_context(nc.sbuf_tensor(name, shape, dt))
        t.RES = sb("RES", [P, NT, D])[:]
        t.XN = sb("XN", [P, NT, D])[:]
        t.ID = sb("ID", [P, P])[:]
        t.STATS = sb("STATS", [P, NT, 6])[:]
        t.NRM = sb("NRM", [P, 8, 2 * NT])[:]
        t.MHALF = sb("MHALF", [P, NT])[:]
        t.psum_all = ctx.enter_context(nc.psum_tensor("banks", [P, 8, BANK], F32))[:]
        t.psum = [t.psum_all[:, i, :] for i in range(8)]
        t.W1H, t.W1L = sb("W1H", [P, NX, HID], F16)[:], sb("W1L", [P, NX, HID], F16)[:]
        t.W2H, t.W2L = sb("W2H", [P, NX, MT, D], F16)[:], sb("W2L", [P, NX, MT, D], F16)[:]
        t.GWH, t.GWL = sb("GWH", [P, NE], F16)[:], sb("GWL", [P, NE], F16)[:]
        t.QKWH, t.QKWL = sb("QKWH", [P, 2 * HG, P], F16)[:], sb("QKWL", [P, 2 * HG, P], F16)[:]
        t.VOWH, t.VOWL = sb("VOWH", [P, 2 * D], F16)[:], sb("VOWL", [P, 2 * D], F16)[:]
        t.XTH, t.XTL = sb("XTH", [P, NT * P], F16)[:], sb("XTL", [P, NT * P], F16)[:]
        t.B1 = sb("B1", [P, NX, MT])[:]
        t.GB = sb("GB", [P, 2, NE])[:]
        t.B2 = sb("B2", [NX, D])[:]
        t.COMBE = sb("COMB", [P, NX, NT])[:]
        t.COMB = t.COMBE.rearrange("p e t -> p t e")
        t.arena = sb("ARENA", [P, ARENA])[:]
        conv_stage(nc, t)
        weights_stage(nc, t)
        norm_stage(nc, t, "f")
        route_stage(nc, t, "f")
        experts_stage(nc, t, "f")
        norm_stage(nc, t, "a")
        attention_stage(nc, t)
        norm_stage(nc, t, "g")
        route_stage(nc, t, "g")
        experts_stage(nc, t, "g")
        write_out(nc, t)


def write_out(nc, t):
    with nc.semaphore("stored") as stored, nc.Block() as block:
        @block.sync
        def _(sp):
            sp.dma_start(t.dram["out"].rearrange("b (t p) d -> p (b t) d", p=P), t.RES).then_inc(stored, 16)
            sp.wait_ge(stored, 16)


def kernel(**inputs):
    import concourse.bacc as bacc
    from concourse.bass_utils import run_bass_kernel_spmd

    def of(name):
        return np.asarray(inputs["L0_" + name])

    def both(a):
        return np.concatenate([a.T, a.T], 0)

    arrays = host_tables()
    arrays["x"] = of("attn_a_x")
    arrays["params"] = np.stack([both(of("attn_a_log_A_real")), both(of("attn_a_A_imag")), both(of("attn_a_C_re")),
                                 both(of("attn_a_C_im")), np.broadcast_to(of("attn_a_log_dt"), (P, D))])
    arrays["ln"] = np.stack([np.broadcast_to(of("attn_a_ln_w"), (P, D)), np.broadcast_to(of("attn_a_ln_b"), (P, D))])
    arrays["dcol"] = of("attn_a_D").reshape(D, 1)
    arrays["w1"] = np.concatenate([of("ffn_w1"), of("ffn_ws1")[None]])
    arrays["w2"] = np.concatenate([of("ffn_w2"), of("ffn_ws2")[None]])
    arrays["b1"] = np.concatenate([of("ffn_b1"), of("ffn_bs1")[None]]).reshape(NX, MT, P).transpose(2, 0, 1)
    arrays["b2"] = np.concatenate([of("ffn_b2"), of("ffn_bs2")[None]])
    qkv = of("attn_b_Wqkv").reshape(D, 3, HG, GH, 1, HD)
    w_qk = np.zeros((D, 2, HG, GH, 4, HD), np.float32)
    w_qk[:, :, :, :, 0:3] = qkv[:, 0:2]
    arrays["w_qk"] = w_qk.reshape(D, 2 * HG, P)
    arrays["w_vo"] = np.concatenate([of("attn_b_Wqkv")[:, 2 * D:], of("attn_b_Wout")], 1)
    arrays["gate_w"] = of("ffn_gate_w")
    arrays["gate_b"] = np.broadcast_to(of("ffn_gate_b"), (P, NE))
    arrays = {k: np.ascontiguousarray(v) for k, v in arrays.items()}
    nc = bacc.Bacc("TRN2", target_bir_lowering=False, num_devices=1)
    dram = {k: nc.dram_tensor("in_" + k, v.shape, F32, kind="ExternalInput").ap() for k, v in arrays.items()}
    dram["out"] = nc.dram_tensor("out_x", (NB, SEQ, D), F32, kind="ExternalOutput").ap()
    build(nc, dram)
    result = run_bass_kernel_spmd(nc, [{"in_" + k: v for k, v in arrays.items()}], core_ids=[0])
    return result.results[0]["out_x"]
```

```python
from contextlib import ExitStack

import numpy as np

import concourse.bass as bass
from concourse import mybir

ALU = mybir.AluOpType
ACT = mybir.ActivationFunctionType
AX = mybir.AxisListType
F32 = mybir.dt.float32
F16 = mybir.dt.float16
BF16 = mybir.dt.bfloat16
I32 = mybir.dt.int32

P = 128
D = 128
NB, SEQ = 16, 256
NT = NB * SEQ // P
TPB = SEQ // P
BANK = 512
EPS = 1e-5

NM = 64
LF = 16
NFFT = 2 * SEQ
NFT = NFFT // P
CB = BANK // D
NCG = NB // CB
ROUND = 12582912.0
TWO_PI_HI = 6.28125
TWO_PI_LO = 2 * np.pi - TWO_PI_HI
TURN = 6.283185

NE, HID = 8, 512
NX = NE + 1
MT = HID // P
GT = BANK // P
NG = NT // GT
WS = 1024.0
UN = 8
TS = 2 * P
SLOTS = 2 * NT * P // TS + NE
ROW = 2 * D + 2
NH, HD = 16, 8
GH, HG = 4, 4
WQ = 64.0
LOGIT = WQ * WQ * HD ** 0.5
LOWEST = -3.0e38
ARENA = 22 * 1024 + 512


class Bag:
    pass


def norm_statistics(dve, link, stats, m):
    me, mo = stats[:, :, 1], stats[:, :, 4]
    se, so = stats[:, :, 2], stats[:, :, 5]
    dve.tensor_tensor(m.a, me, mo, ALU.add)
    dve.tensor_tensor(m.d, me, mo, ALU.subtract)
    link(dve.tensor_tensor(m.s, se, so, ALU.add))
    dve.tensor_scalar(m.mean, m.a, 0.5, None, ALU.mult)
    dve.tensor_tensor(m.q, m.d, m.d, ALU.mult)
    link(dve.tensor_scalar(m.s, m.s, 1.0 / D, EPS, ALU.mult, ALU.add))
    return dve.scalar_tensor_tensor(m.vareps, m.q, 0.25, m.s, ALU.mult, ALU.add)


def rows_of(buffer, first, last):
    m = Bag()
    m.a, m.d, m.s, m.q, m.mean, m.vareps, m.rstd, m.nmr = (buffer[:, i, first:last] for i in range(8))
    return m


def stage_semaphores(nc, ctx, prefix):
    taken = []

    def sem(name):
        taken.append(nc.alloc_semaphore(name=prefix + name))
        return taken[-1]

    def clear():
        nc.clear_and_free_semaphores(taken)
        nc.all_engine_barrier()
    ctx.callback(clear)
    return sem


def weight_jobs(t):
    jobs = []
    for e in range(NX):
        jobs.append((t.dram["w1"][e], t.W1H[:, e, :], t.W1L[:, e, :], HID, WS))
        jobs.append((t.dram["w2"][e].rearrange("(m p) d -> p m d", p=P), t.W2H[:, e], t.W2L[:, e], HID, WS))
    jobs.append((t.dram["gate_w"], t.GWH, t.GWL, NE, WS))
    for k in range(2):
        s = slice(HG * k, HG * k + HG)
        jobs.append((t.dram["w_qk"][:, s, :], t.QKWH[:, s, :], t.QKWL[:, s, :], HG * P, WQ))
    jobs.append((t.dram["w_vo"], t.VOWH, t.VOWL, 2 * D, WQ))
    return jobs


def conv_stage(nc, t):
    with ExitStack() as ctx:
        sem = stage_semaphores(nc, ctx, "c_")

        scratch = t.arena
        at = [0]

        def carve(*shape):
            n = int(np.prod(shape))
            v = scratch[:, at[0]:at[0] + n]
            at[0] += n
            if len(shape) == 2:
                v = v.rearrange("p (a b) -> p a b", b=shape[1])
            if len(shape) == 3:
                v = v.rearrange("p (a b c) -> p a b c", b=shape[1], c=shape[2])
            return v

        FW = carve(TPB, NFFT)
        IV = carve(NFT, SEQ)
        PRM = carve(6, D)
        WLN = carve(2, D)
        OFF = carve(4)
        DCOL = carve(1)
        KEEP = carve(2)
        TMP = carve(24, D)
        SIN2, SINA, SINB, KQ, PHR = (carve(LF, D) for _ in range(5))
        mag_at = at[0]
        MAG2, MAG1 = carve(LF, D), carve(LF, D)
        KCH = carve(SEQ)
        KLAG = carve(TPB, D)
        SPK = carve(4, 2, D)
        KDIG = PHR
        M4 = KQ.rearrange("p a h -> p (a h)").rearrange("p (k n) -> p k n", n=BANK)
        YS = scratch[:, mag_at:mag_at + 2 * NFT * BANK].rearrange("p (k n) -> p k n", n=BANK)
        RN = SINB.rearrange("p a h -> p (a h)").rearrange("p (k n) -> p k n", n=BANK)
        XN = t.XN
        ps = t.psum

        params_in, x_in, dct_in, ln_in = sem("params_in"), sem("x_in"), sem("dct_in"), sem("ln_in")
        dve_step, pool_step = sem("dve_step"), sem("pool_step")
        exps, dt_ready, decay_ready, angle_ready = sem("exps"), sem("dt_ready"), sem("decay_ready"), sem("angle_ready")
        mags, phase_ready, sines = sem("mags"), sem("phase_ready"), sem("sines")
        ct_ready, e2_ready, e1_ready = sem("ct_ready"), sem("e2_ready"), sem("e1_ready")
        kdig_mm, kdig_sb, kch_mm, kch_sb, klag_mm, klag_sb = (sem(n) for n in (
            "kdig_mm", "kdig_sb", "kch_mm", "kch_sb", "klag_mm", "klag_sb"))
        kf_mm, spk_ready = sem("kf_mm"), sem("spk_ready")
        x_var, x_rstd, xn_ready = sem("x_var"), sem("x_rstd"), sem("xn_ready")
        fwd_mm, prod_ready, ys_ready, inv_mm = (sem(n) for n in (
            "fwd_mm", "prod_ready", "ys_ready", "inv_mm"))
        r_var, r_rstd, r_nmr, rn_ready, inv_read, res_ready = (sem(n) for n in (
            "r_var", "r_rstd", "r_nmr", "rn_ready", "inv_read", "res_ready"))

        empty_row, emptied = sem("empty_row"), sem("emptied")
        jobs = weight_jobs(t)
        NS = len(t.STG)
        job_in, high, low = [sem(f"job_in{i}") for i in range(NS)], sem("high"), sem("low")
        small, fixed, b2_scaled, b2_high, x_nmr, scaled, mag_sines = sem("small"), sem("fixed"), sem("b2_scaled"), sem("b2_high"), sem("x_nmr"), sem("scaled"), sem("mag_sines")

        def staged(i):
            v = t.STG[i % NS][:, 0:jobs[i][3]]
            return v.rearrange("p (m d) -> p m d", d=D) if len(jobs[i][1].shape) == 3 else v

        EARLY = NS
        share = -(-(len(jobs) - EARLY) // NCG)
        portions = [range(0, EARLY)] + [range(EARLY + share * g, min(EARLY + share * (g + 1), len(jobs))) for g in range(NCG)]
        block = ctx.enter_context(nc.Block())
        C_RE, C_IM, LAR, AIM, LDT, DT = 2, 3, 0, 1, 4, 5

        @block.sync
        def _(sp):
            sp.dma_start(PRM[:, 0:5, :], t.dram["params"].rearrange("k p h -> p k h")).then_inc(params_in, 16)
            sp.dma_start(OFF, t.dram["offsets"]).then_inc(params_in, 16)
            sp.dma_start(t.RES[:, 0:NT // 2, :], t.dram["x"].rearrange("b (t p) d -> p (b t) d", p=P)[:, 0:NT // 2, :]).then_inc(x_in, 16)
            sp.dma_start(FW, t.dram["fwd"].rearrange("t p f -> p t f")).then_inc(dct_in, 16)
            sp.dma_start(KEEP, t.dram["keep"]).then_inc(dct_in, 16)
            def load(i):
                if i >= NS:
                    sp.wait_ge(low, i - NS + 1)
                sp.dma_start(staged(i), jobs[i][0]).then_inc(job_in[i % NS], 16)
            for i in range(NS):
                load(i)
            for v, name in ((t.LOW, "lowrow"), (t.B1, "b1"), (t.B2, "b2_rows"), (t.GB[:, 0, :], "gate_b"), (t.GB[:, 1, :], "rank"),
                            (t.SLOTNO, "slotno")):
                sp.dma_start(v, t.dram[name]).then_inc(small, 16)
            sp.wait_ge(empty_row, 2)
            for tag in "fg":
                sp.dma_start(t.dram["slots" + tag].rearrange("(s p) r -> p s r", p=P),
                             t.EMPTY.bitcast(I32).rearrange("p (o r) -> p o r", o=1).broadcast_to([P, SLOTS * TS // P, ROW // 2])).then_inc(emptied, 16)
            for i in range(NS, len(jobs)):
                load(i)
            sp.wait_ge(small, 96)
            sp.wait_ge(emptied, 32)

        @block.gpsimd
        def _(pool):
            def link(ins):
                link.n += 1
                ins.then_inc(pool_step, 1)
                pool.wait_ge(pool_step, link.n)
            link.n = 0
            nc.gpsimd.memset(t.EMPTY.bitcast(I32)[:, 0:ROW // 2 - 1], 0).then_inc(empty_row, 1)
            nc.gpsimd.memset(t.EMPTY.bitcast(I32)[:, ROW // 2 - 1:ROW // 2], 1 << 20).then_inc(empty_row, 1)
            link(nc.gpsimd.memset(t.MHALF[:, 0:NT], -0.5))
            nc.gpsimd.memset(t.ONES16, 1.0)
            link(nc.gpsimd.memset(t.BEFORE, 1.0))
            nc.gpsimd.affine_select(out=t.BEFORE, in_=t.BEFORE, compare_op=ALU.is_gt, fill=0.0, base=0,
                                    pattern=[[1, P]], channel_multiplier=-1).then_inc(fixed, 1)
            pool.wait_ge(mags, 1)
            pool.wait_ge(sines, 1)
            nc.gpsimd.tensor_tensor(SIN2, SIN2, MAG2, ALU.mult).then_inc(e2_ready, 1)
            m = rows_of(t.NRM, 0, NT)
            pool.wait_ge(x_var, 1)
            nc.gpsimd.tensor_tensor(m.rstd, m.vareps, t.MHALF[:, 0:NT], ALU.pow).then_inc(x_rstd, 1)
            pool.wait_ge(mags, 2)
            pool.wait_ge(sines, 4)
            nc.gpsimd.tensor_tensor(SINB, SINB, MAG1, ALU.mult).then_inc(mag_sines, 1)
            m = rows_of(t.NRM, NT, NT + 8 * NCG)

            def sums(g, k):
                pool.wait_ge(prod_ready, 2 * g + k + 1)
                if g >= 2:
                    pool.wait_ge(inv_mm, 2 * (g - 1))
                ys = YS[:, NFT * (g % 2) + k, :]
                yi = YS[:, NFT * (g % 2) + 2 + k, :]
                nc.gpsimd.tensor_tensor(ys, M4[:, 0, :], M4[:, 1, :], ALU.subtract)
                nc.gpsimd.tensor_tensor(yi, M4[:, 2, :], M4[:, 3, :], ALU.add).then_inc(ys_ready, 1)

            def finish(g):
                s = slice(8 * g, 8 * g + 8)
                pool.wait_ge(r_var, g + 1)
                nc.gpsimd.tensor_tensor(m.rstd[:, s], m.vareps[:, s], t.MHALF[:, 0:8], ALU.pow).then_inc(r_rstd, 1)
                for tt in range(TPB):
                    pool.wait_ge(scaled, 2 * g + tt + 1)
                    rn = RN[:, 2 * (g % 2) + tt, :].rearrange("p (b h) -> p b h", h=D)
                    res = t.RES[:, 2 * CB * g + tt:2 * CB * (g + 1):2, :]
                    link(nc.gpsimd.tensor_tensor(rn, rn, WLN[:, 1:2, :].broadcast_to([P, CB, D]), ALU.add))
                    nc.gpsimd.tensor_tensor(res, res, rn, ALU.add).then_inc(res_ready, 1)

            for g in range(NCG):
                sums(g, 0)
                sums(g, 1)
                if g >= 1:
                    finish(g - 1)
            finish(NCG - 1)

        @block.scalar
        def _(act):
            act.dma_start(t.RES[:, NT // 2:, :], t.dram["x"].rearrange("b (t p) d -> p (b t) d", p=P)[:, NT // 2:, :]).then_inc(x_in, 16)
            act.dma_start(t.ID, t.dram["ident"]).then_inc(dct_in, 16)
            act.dma_start(IV, t.dram["inv"].rearrange("t p f -> p t f")).then_inc(ln_in, 16)
            act.dma_start(WLN, t.dram["ln"].rearrange("k p h -> p k h")).then_inc(ln_in, 16)
            act.dma_start(DCOL, t.dram["dcol"]).then_inc(ln_in, 16)
            act.wait_ge(params_in, 32)
            nc.scalar.activation(PRM[:, DT, :], PRM[:, LDT, :], ACT.Exp)
            nc.scalar.activation(PRM[:, LAR, :], PRM[:, LAR, :], ACT.Exp).then_inc(exps, 1)
            act.wait_ge(decay_ready, 1)
            for b in range(LF):
                ins = nc.scalar.activation(MAG2[:, b, :], TMP[:, 0, :], ACT.Exp, scale=-float(b))
            ins.then_inc(mags, 1)
            for a in range(LF):
                ins = nc.scalar.activation(MAG1[:, a, :], TMP[:, 0, :], ACT.Exp, scale=-float(LF * a))
            ins.then_inc(mags, 1)
            act.wait_ge(phase_ready, 1)
            nc.scalar.activation(SIN2, SIN2, ACT.Sin, scale=TURN).then_inc(sines, 1)
            act.wait_ge(phase_ready, 2)
            nc.scalar.activation(TMP[:, 4:6, :], TMP[:, 4:6, :], ACT.Sin, scale=TURN).then_inc(sines, 1)
            act.wait_ge(phase_ready, 3)
            nc.scalar.activation(SINA, SINA, ACT.Sin, scale=TURN).then_inc(sines, 1)
            act.wait_ge(phase_ready, 4)
            nc.scalar.activation(SINB, SINB, ACT.Sin, scale=TURN).then_inc(sines, 1)
            m = rows_of(t.NRM, 0, NT)
            act.wait_ge(x_nmr, 1)
            for i in range(NT):
                ins = nc.scalar.activation(XN[:, i, :], t.RES[:, i, :], ACT.Identity,
                                           bias=m.nmr[:, i:i + 1], scale=m.rstd[:, i:i + 1])
                if i % (TPB * CB) == TPB * CB - 1:
                    ins.then_inc(xn_ready, 1)
            act.wait_ge(dct_in, 48)
            nc.scalar.activation(t.ID16, t.ID, ACT.Copy)

            def split_high(portion):
                for i in portion:
                    act.wait_ge(job_in[i % NS], 16 * (i // NS + 1))
                    nc.scalar.activation(jobs[i][1], staged(i), ACT.Copy, scale=jobs[i][4]).then_inc(high, 1)
            split_high(portions[0][0:4])
            act.wait_ge(small, 96)
            nc.scalar.activation(t.B2, t.B2, ACT.Copy, scale=WS).then_inc(b2_scaled, 1)
            act.wait_ge(b2_scaled, 1)
            nc.scalar.activation(t.B2P, t.B2, ACT.Copy).then_inc(b2_high, 1)
            for q in range(4):
                act.wait_ge(kdig_mm, q + 1)
                nc.scalar.activation(KDIG[0:LF, :, 32 * q:32 * q + 32],
                                     ps[4 + q][0:LF, :].rearrange("a (h b) -> a b h", b=LF),
                                     ACT.Copy, scale=2.0).then_inc(kdig_sb, 1)
            act.wait_ge(klag_mm, 1)
            nc.scalar.activation(KLAG, ps[5][:, 0:SEQ].rearrange("p (t h) -> p t h", h=D), ACT.Copy).then_inc(klag_sb, 1)
            split_high(portions[0][4:])
            m = rows_of(t.NRM, NT, NT + 8 * NCG)
            for g in range(NCG):
                split_high(portions[g + 1])
                act.wait_ge(r_nmr, g + 1)
                for tt in range(TPB):
                    if g >= 2:
                        act.wait_ge(res_ready, 2 * (g - 2) + tt + 1)
                    for b in range(CB):
                        j = 8 * g + 4 * tt + b
                        ins = nc.scalar.activation(RN[:, 2 * (g % 2) + tt, D * b:D * b + D],
                                                   ps[6 - 2 * (g % 2) + tt][:, D * b:D * b + D], ACT.Identity,
                                                   bias=m.nmr[:, j:j + 1], scale=m.rstd[:, j:j + 1])
                    ins.then_inc(rn_ready, 1)

        @block.tensor
        def _(pe):
            def forward(g, k):
                n = 2 * g + k
                if n >= 2:
                    pe.wait_ge(prod_ready, n - 1)
                for i, ft in enumerate((k, 2 + k)):
                    for st in range(TPB):
                        ins = pe.matmul(ps[2 * (n % 2) + i], FW[:, st, P * ft:P * ft + P],
                                        XN[:, 2 * CB * g + st:2 * CB * (g + 1):2, :], start=(st == 0), stop=(st == TPB - 1))
                ins.then_inc(fwd_mm, 1)

            def inverse(g):
                pe.wait_ge(ys_ready, 2 * g + 2)
                for tt in range(TPB):
                    if g >= 2:
                        pe.wait_ge(rn_ready, 2 * (g - 2) + tt + 1)
                    for ft in range(NFT):
                        ins = pe.matmul(ps[6 - 2 * (g % 2) + tt], IV[:, ft, P * tt:P * tt + P], YS[:, NFT * (g % 2) + ft, :],
                                        start=(ft == 0), stop=(ft == NFT - 1))
                    ins.then_inc(inv_mm, 1)

            pe.wait_ge(dct_in, 48)
            pe.wait_ge(xn_ready, 1)
            forward(0, 0)
            pe.wait_ge(e2_ready, 1)
            pe.wait_ge(e1_ready, 1)
            for h in range(D):
                ins = pe.matmul(ps[4 + h // 32][0:LF, LF * (h % 32):LF * (h % 32) + LF], SINA[:, :, h], SIN2[:, :, h],
                                start=True, stop=True)
                if h % 32 == 31:
                    ins.then_inc(kdig_mm, 1)
            forward(0, 1)
            pe.wait_ge(kdig_sb, 4)
            for b in range(LF):
                ins = pe.transpose(ps[4][:, LF * b:LF * b + LF], KDIG[0:LF, b, :], t.ID[0:LF, 0:LF])
            ins.then_inc(kch_mm, 1)
            pe.wait_ge(kch_sb, 1)
            for i in range(TPB):
                ins = pe.transpose(ps[5][:, D * i:D * i + D], KCH[:, P * i:P * i + P], t.ID)
            ins.then_inc(klag_mm, 1)
            pe.wait_ge(klag_sb, 1)
            for ft in range(NFT):
                for st in range(TPB):
                    ins = pe.matmul(ps[4][:, D * ft:D * ft + D], FW[:, st, P * ft:P * ft + P], KLAG[:, st, :],
                                    start=(st == 0), stop=(st == TPB - 1))
            ins.then_inc(kf_mm, 1)
            for g in range(NCG):
                if g >= 1:
                    pe.wait_ge(xn_ready, g + 1)
                    for k in range(2):
                        forward(g, k)
                if g >= 1:
                    inverse(g - 1)
            inverse(NCG - 1)

        @block.vector
        def _(dve):
            def link(ins):
                link.n += 1
                ins.then_inc(dve_step, 1)
                dve.wait_ge(dve_step, link.n)
            link.n = 0
            tt_, ts, stt = dve.tensor_tensor, dve.tensor_scalar, dve.scalar_tensor_tensor

            def turn_rest(phase, whole):
                link(ts(whole, phase, ROUND, -ROUND, ALU.add, ALU.add))
                return tt_(phase, phase, whole, ALU.subtract)

            EA, DTC = PRM[:, LAR, :], PRM[:, DT, :]
            AR, R1, R16, E1R, SN = (TMP[:, i, :] for i in (0, 1, 2, 3, 4))
            CS = TMP[:, 5, :]
            dve.wait_ge(exps, 1)
            tt_(AR, EA, DTC, ALU.mult).then_inc(decay_ready, 1)
            link(tt_(R1, PRM[:, AIM, :], DTC, ALU.mult))
            link(ts(R16, R1, float(LF), None, ALU.mult))
            steps, whole = TMP[:, 1:3, :], TMP[:, 6:8, :]
            link(ts(whole, steps, 1.0 / (2 * np.pi), ROUND, ALU.mult, ALU.add))
            link(ts(whole, whole, -ROUND, None, ALU.add))
            link(stt(steps, whole, -TWO_PI_HI, steps, ALU.mult, ALU.add))
            link(stt(steps, whole, -TWO_PI_LO, steps, ALU.mult, ALU.add))
            link(ts(steps, steps, 1.0 / (2 * np.pi), None, ALU.mult))
            for b in range(LF):
                ins = ts(SIN2[:, b, :], R1, float(b), OFF[:, 0:1], ALU.mult, ALU.add)
            link(ins)
            turn_rest(SIN2, KQ).then_inc(phase_ready, 1)
            ts(SN, R1, 1.0, None, ALU.mult)
            link(ts(CS, R1, 0.25, None, ALU.add))
            turn_rest(TMP[:, 4:6, :], TMP[:, 6:8, :]).then_inc(phase_ready, 1)
            for a in range(LF):
                ts(SINA[:, a, :], R16, float(a), OFF[:, 1:2], ALU.mult, ALU.add)
                ins = ts(SINB[:, a, :], R16, float(a), OFF[:, 2:3], ALU.mult, ALU.add)
            link(ins)
            turn_rest(SINA, PHR).then_inc(phase_ready, 1)
            turn_rest(SINB, KQ).then_inc(phase_ready, 1)
            dve.wait_ge(x_in, 32)
            for i in range(NT):
                ins = dve.bn_stats(t.STATS[:, i, :], t.RES[:, i, :])
            link(ins)
            m = rows_of(t.NRM, 0, NT)
            norm_statistics(dve, link, t.STATS[:, 0:NT, :], m).then_inc(x_var, 1)
            ER, EI, T0, T1, NR, NI, INV, CTR, CTI, SQ = (TMP[:, i, :] for i in range(8, 18))
            CRE, CIM, AIMC = PRM[:, C_RE, :], PRM[:, C_IM, :], PRM[:, AIM, :]
            dve.wait_ge(mags, 1)
            dve.wait_ge(sines, 2)
            EXD = MAG2[:, 1, :]
            tt_(EI, EXD, SN, ALU.mult)
            tt_(SQ, AIMC, AIMC, ALU.mult)
            link(tt_(ER, EXD, CS, ALU.mult))
            tt_(T1, EA, EA, ALU.mult)
            link(ts(ER, ER, -1.0, None, ALU.add))
            link(tt_(SQ, SQ, T1, ALU.add))
            dve.reciprocal(INV, SQ)
            tt_(NR, CRE, ER, ALU.mult)
            tt_(T0, CIM, EI, ALU.mult)
            tt_(NI, CRE, EI, ALU.mult)
            link(tt_(T1, CIM, ER, ALU.mult))
            tt_(NR, NR, T0, ALU.subtract)
            link(tt_(NI, NI, T1, ALU.add))
            tt_(T0, NI, AIMC, ALU.mult)
            tt_(T1, NR, EA, ALU.mult)
            tt_(CTI, NR, AIMC, ALU.mult)
            link(tt_(ER, NI, EA, ALU.mult))
            tt_(CTR, T0, T1, ALU.subtract)
            link(stt(CTI, CTI, -1.0, ER, ALU.mult, ALU.subtract))
            tt_(CTR, CTR, INV, ALU.mult)
            link(tt_(CTI, CTI, INV, ALU.mult))
            dve.wait_ge(x_rstd, 1)
            stt(m.nmr, m.mean, -1.0, m.rstd, ALU.mult, ALU.mult).then_inc(x_nmr, 1)
            dve.wait_ge(sines, 4)
            dve.wait_ge(mags, 2)
            link(tt_(SINA, SINA, MAG1, ALU.mult))
            tt_(SINA, SINA, CTR.rearrange("p (o h) -> p o h", o=1).broadcast_to([P, LF, D]), ALU.mult)
            dve.wait_ge(mag_sines, 1)
            link(tt_(SINB, SINB, CTI.rearrange("p (o h) -> p o h", o=1).broadcast_to([P, LF, D]), ALU.mult))
            tt_(SINA, SINA, SINB, ALU.add).then_inc(e1_ready, 1)

            def split_low(portion):
                for i in portion:
                    dve.wait_ge(high, i + 1)
                    stt(jobs[i][2], staged(i), jobs[i][4], jobs[i][1], ALU.mult, ALU.subtract).then_inc(low, 1)
            split_low(portions[0][0:4])
            dve.wait_ge(b2_high, 1)
            stt(t.B2P, t.B2P, t.LOW[0:2, 2:3], t.B2, ALU.mult, ALU.add)

            dve.wait_ge(kch_mm, 1)
            dve.wait_ge(ln_in, 48)
            link(dve.tensor_copy(KCH.rearrange("p (a b) -> p b a", b=LF), ps[4][:, 0:SEQ].rearrange("p (b a) -> p b a", a=LF)))
            ts(KCH[:, 0:1], KCH[:, 0:1], DCOL, 1.0, ALU.add, ALU.add).then_inc(kch_sb, 1)
            dve.wait_ge(kf_mm, 1)
            kf = ps[4].rearrange("p (f h) -> p f h", h=D)
            FA, FB, FD = SPK[:, 0], SPK[:, 1], SPK[:, 2]
            dve.tensor_copy(FA, kf[:, 0:2, :])
            dve.tensor_copy(FD[:, 1, :], kf[:, 1, :])
            dve.tensor_copy(FB[:, 1, :], kf[:, 3, :])
            ts(FB[:, 0, :], kf[:, 2, :], KEEP[:, 0:1], None, ALU.mult)
            link(ts(SPK[:, 3, 0, :], kf[:, 2, :], KEEP[:, 1:2], None, ALU.mult))
            link(stt(FD[:, 0, :], kf[:, 0, :], KEEP[:, 0:1], SPK[:, 3, 0, :], ALU.mult, ALU.add))

            def wide(f):
                return f.rearrange("p (o h) -> p o h", o=1).broadcast_to([P, CB, D])

            def products(g, k):
                n = 2 * g + k
                dve.wait_ge(fwd_mm, n + 1)
                if n >= 1:
                    dve.wait_ge(ys_ready, n)
                re = ps[2 * (n % 2)].rearrange("p (b h) -> p b h", h=D)
                im = ps[2 * (n % 2) + 1].rearrange("p (b h) -> p b h", h=D)
                out = M4.rearrange("p k (b h) -> p k b h", h=D)
                tt_(out[:, 0], re, wide(FA[:, k, :]), ALU.mult)
                tt_(out[:, 1], im, wide(FB[:, k, :]), ALU.mult)
                tt_(out[:, 2], re, wide(FB[:, k, :]), ALU.mult)
                tt_(out[:, 3], im, wide(FD[:, k, :]), ALU.mult).then_inc(prod_ready, 1)

            def statistics(g):
                for tt in range(TPB):
                    dve.wait_ge(inv_mm, 2 * g + tt + 1)
                    for b in range(CB):
                        ins = dve.bn_stats(t.STATS[:, 4 * tt + b, :], ps[6 - 2 * (g % 2) + tt][:, D * b:D * b + D])
                link(ins)
                mg = rows_of(t.NRM, NT + 8 * g, NT + 8 * g + 8)
                norm_statistics(dve, link, t.STATS[:, 0:8, :], mg).then_inc(r_var, 1)
                dve.wait_ge(r_rstd, g + 1)
                stt(mg.nmr, mg.mean, -1.0, mg.rstd, ALU.mult, ALU.mult).then_inc(r_nmr, 1)

            def scale(g):
                for tt in range(TPB):
                    dve.wait_ge(rn_ready, 2 * g + tt + 1)
                    rn = RN[:, 2 * (g % 2) + tt, :].rearrange("p (b h) -> p b h", h=D)
                    tt_(rn, rn, WLN[:, 0:1, :].broadcast_to([P, CB, D]), ALU.mult).then_inc(scaled, 1)

            def residual_statistics(g):
                dve.wait_ge(res_ready, 2 * g + 2)
                for i in range(TPB * CB * g, TPB * CB * (g + 1)):
                    dve.bn_stats(t.RSTATS[:, i, :], t.RES[:, i, :])

            for g in range(NCG):
                for k in range(2):
                    products(g, k)
                if g >= 1:
                    statistics(g - 1)
                if g == 0:
                    split_low(portions[0][4:])
                split_low(portions[g + 1])
                if g >= 2:
                    residual_statistics(g - 2)
                if g >= 1:
                    scale(g - 1)
            statistics(NCG - 1)
            scale(NCG - 1)
            residual_statistics(NCG - 2)
            residual_statistics(NCG - 1)

CHUNK = 2 * GT


def norm_program(nc, t, sem):
    dve_step, var, rstd, nmr = sem("n_dve_step"), sem("n_var"), sem("n_rstd"), sem("n_nmr")
    xn, turned, high, low = [sem("n_xn_act"), sem("n_xn_dve")], sem("n_turned"), sem("n_high"), sem("n_low")
    m = rows_of(t.NRM, 0, NT)
    part = Bag()
    part.low = low

    def tiles(c):
        return slice(CHUNK * c, CHUNK * c + CHUNK)

    def gpsimd(pool):
        pool.wait_ge(var, 1)
        for c in range(NT // CHUNK):
            s = tiles(c)
            nc.gpsimd.tensor_tensor(m.rstd[:, s], m.vareps[:, s], t.MHALF[:, s], ALU.pow).then_inc(rstd, 1)

    def tensor(pe):
        for g in range(NG):
            c = g // 2
            pe.wait_ge(xn[c % 2], 2 * (c // 2) + g % 2 + 1)
            if g >= 4:
                pe.wait_ge(low, g - 3)
            for j in range(GT):
                ins = pe.transpose(t.psum[g % 4][:, P * j:P * j + P], t.XN[:, GT * g + j, :], t.ID)
            ins.then_inc(turned, 1)

    def scalar(act):
        done = 0
        for c in range(0, NT // CHUNK, 2):
            act.wait_ge(nmr, c + 1)
            for i in range(CHUNK * c, CHUNK * c + CHUNK):
                ins = nc.scalar.activation(t.XN[:, i, :], t.RES[:, i, :], ACT.Identity,
                                           bias=m.nmr[:, i:i + 1], scale=m.rstd[:, i:i + 1])
                if i % GT == GT - 1:
                    ins.then_inc(xn[0], 1)
            for g in range(done, 2 if c == 0 else NG):
                act.wait_ge(turned, g + 1)
                nc.scalar.activation(t.XTH[:, BANK * g:BANK * (g + 1)], t.psum[g % 4], ACT.Copy).then_inc(high, 1)
            done = 2

    def vector(dve):
        def link(ins):
            link.n += 1
            ins.then_inc(dve_step, 1)
            dve.wait_ge(dve_step, link.n)
        link.n = 0
        norm_statistics(dve, link, t.RSTATS, m).then_inc(var, 1)
        for c in range(NT // CHUNK):
            s = tiles(c)
            dve.wait_ge(rstd, c + 1)
            dve.scalar_tensor_tensor(m.nmr[:, s], m.mean[:, s], -1.0, m.rstd[:, s], ALU.mult, ALU.mult).then_inc(nmr, 1)
            if c % 2 == 1:
                for i in range(CHUNK * c, CHUNK * c + CHUNK):
                    ins = dve.tensor_scalar(t.XN[:, i, :], t.RES[:, i, :], m.mean[:, i:i + 1], m.rstd[:, i:i + 1],
                                            ALU.subtract, ALU.mult)
                    if i % GT == GT - 1:
                        ins.then_inc(xn[1], 1)
        for g in range(NG):
            dve.wait_ge(high, g + 1)
            s = slice(BANK * g, BANK * (g + 1))
            dve.tensor_tensor(t.XTL[:, s], t.psum[g % 4], t.XTH[:, s], ALU.subtract).then_inc(low, 1)
    part.gpsimd, part.tensor, part.scalar, part.vector = gpsimd, tensor, scalar, vector
    return part


def norm_stage(nc, t, tag):
    with ExitStack() as ctx:
        norm = norm_program(nc, t, stage_semaphores(nc, ctx, f"n{tag}_"))
        block = ctx.enter_context(nc.Block())

        @block.gpsimd
        def _(pool):
            norm.gpsimd(pool)

        @block.tensor
        def _(pe):
            norm.tensor(pe)

        @block.scalar
        def _(act):
            norm.scalar(act)

        @block.vector
        def _(dve):
            norm.vector(dve)


def shared_stage(nc, t, tag):
    with ExitStack() as ctx:
        sem = stage_semaphores(nc, ctx, f"x{tag}_")
        norm = norm_program(nc, t, sem)
        up_mm, hidden, split, down_mm, merged, high, primed = (sem(n) for n in (
            "up_mm", "hidden", "split", "down_mm", "merged", "high", "primed"))
        dve_step, gate_mm, gap, ratio, chosen_set, ranked, row_high, row_low, iotas, placed = (sem(n) for n in (
            "dve_step", "gate_mm", "gap", "ratio", "chosen_set", "ranked", "row_high", "row_low", "iotas", "placed"))
        sent, second = [sem(f"sent{i}") for i in range(2)], sem("second")
        HF = t.arena[:, 0:2 * MT * BANK].rearrange("p (s m n) -> p s m n", m=MT, n=BANK)
        H16 = t.arena[:, 2 * MT * BANK:4 * MT * BANK].bitcast(F16).rearrange("p (s k m n) -> p s k m n", s=2, k=2, m=MT)
        e = NE
        BIAS = t.B1[:, e, :]
        ROWI = t.ROWS.bitcast(I32)
        n = NT * NE
        at = t.arena[:, 4 * MT * BANK:]
        L, EQ, V, O1, O2 = (at[:, i * n:(i + 1) * n].rearrange("p (t e) -> p t e", e=NE) for i in range(5))
        INC, POS, TEMP = (at[:, i * n:(i + 1) * n].rearrange("p (e t) -> p e t", t=NT) for i in range(5, 8))
        ONE = at[:, 8 * n:9 * n]
        CHOSEN = at[:, 9 * n:9 * n + n // 2].bitcast(F16).rearrange("p (e t) -> p e t", t=NT)
        S = at[:, 10 * n:10 * n + 8 * NT].rearrange("p (k t) -> p k t", t=NT)
        M1, M2, MV, GAP, DEN, PK = (S[:, i, :] for i in range(6))
        E8 = at[:, 11 * n:11 * n + 8 * NE].rearrange("p (k e) -> p k e", e=NE)
        LASTS, COUNT, TILES, UPTO, SHIFT = (E8[:, i, :] for i in range(5))
        CMP = at[0:1, 12 * n:12 * n + SLOTS * NE].rearrange("p (s e) -> p s e", e=NE)
        EIDF = at[0:1, 12 * n + SLOTS * NE:12 * n + SLOTS * (NE + 1)]
        block = ctx.enter_context(nc.Block())

        def wide(v):
            return v.rearrange("p (t o) -> p t o", o=1).broadcast_to([P, NT, NE])

        HALVES = [slice(NT // 2 * h, NT // 2 * (h + 1)) for h in range(2)]

        @block.gpsimd
        def _(pool):
            norm.gpsimd(pool)
            nc.gpsimd.iota(ROWI[:, :, ROW // 2 - 1], pattern=[[P, NT]], base=0, channel_multiplier=1).then_inc(iotas, 1)
            for h, s in enumerate(HALVES):
                pool.wait_ge(row_high, h + 1)
                nc.gpsimd.tensor_tensor(t.ROWS[:, s, D:2 * D], t.XN[:, s, :], t.ROWS[:, s, 0:D], ALU.subtract).then_inc(row_low, 1)
            pool.wait_ge(iotas, 1)
            pool.wait_ge(row_low, 2)
            xs = t.dram["slots" + tag]
            for k in range(2):
                pool.wait_ge(placed, k + 1)
                for h, s in enumerate(HALVES):
                    if k == 1:
                        pool.wait_ge(sent[h], 16 * NT // 2)
                        nc.gpsimd.iota(ROWI[:, s, ROW // 2 - 1], pattern=[[P, NT // 2]], base=NT * P + NT // 2 * P * h,
                                       channel_multiplier=1).then_inc(second, 1)
                        pool.wait_ge(second, h + 1)
                    for i in range(NT // 2 * h, NT // 2 * (h + 1)):
                        nc.gpsimd.indirect_dma_start(xs, bass.IndirectOffsetOnAxis(ap=t.PLACE[:, k, i:i + 1], axis=0),
                                                     ROWI[:, i, :], None).then_inc(sent[h], 16)
            for h in range(2):
                pool.wait_ge(sent[h], 16 * NT)

        @block.tensor
        def _(pe):
            norm.tensor(pe)
            pe.wait_ge(norm.low, NG)
            for i in range(NT):
                for k, (x, w) in enumerate(((t.XTH, t.GWH), (t.XTL, t.GWH), (t.XTH, t.GWL))):
                    ins = pe.matmul(t.psum[6][:, NE * i:NE * i + NE], x[:, P * i:P * i + P], w, start=(k == 0), stop=(k == 2))
            ins.then_inc(gate_mm, 1)
            pe.wait_ge(chosen_set, 1)
            pe.matmul(t.psum[6][:, 0:n], t.BEFORE, CHOSEN.rearrange("p e t -> p (e t)"), start=True, stop=True)
            pe.matmul(t.psum[7][:, 0:n], t.ONES16, CHOSEN.rearrange("p e t -> p (e t)"), start=True, stop=True).then_inc(ranked, 1)

            def up(g):
                for m in range(MT):
                    pe.wait_ge(hidden, MT * g + m + 1)
                    ms, xs = slice(P * m, P * m + P), slice(BANK * g, BANK * (g + 1))
                    pe.matmul(t.psum[m], t.W1H[:, e, ms], t.XTH[:, xs], start=True, stop=False)
                    pe.matmul(t.psum[m], t.W1H[:, e, ms], t.XTL[:, xs], start=False, stop=False)
                    pe.matmul(t.psum[m], t.W1L[:, e, ms], t.XTH[:, xs], start=False, stop=True).then_inc(up_mm, 1)

            def down(g):
                pe.wait_ge(split, g + 3)
                pe.wait_ge(merged, g + 1)
                for j in range(GT):
                    out = t.psum[4 + g % 2][:, D * j:D * j + D]
                    pe.matmul(out, t.ONES16[0:2, :], t.B2P[0:2, e, :], start=True, stop=False)
                    for m in range(MT):
                        js = slice(P * j, P * j + P)
                        hh, hl = H16[:, g % 2, 0, m, js], H16[:, g % 2, 1, m, js]
                        pe.matmul(out, hh, t.W2H[:, e, m, :], start=False, stop=False)
                        pe.matmul(out, hh, t.W2L[:, e, m, :], start=False, stop=False)
                        ins = pe.matmul(out, hl, t.W2H[:, e, m, :], start=False, stop=(m == MT - 1))
                ins.then_inc(down_mm, 1)

            for g in range(NG):
                up(g)
                if g >= 1:
                    down(g - 1)
            down(NG - 1)

        @block.scalar
        def _(act):
            norm.scalar(act)
            for s in HALVES:
                nc.scalar.activation(t.ROWS[:, s, 0:D], t.XN[:, s, :], ACT.Copy).then_inc(row_high, 1)
            act.wait_ge(gap, 1)
            nc.scalar.activation(GAP, GAP, ACT.Exp).then_inc(ratio, 1)
            nc.scalar.activation(HF[0:1, 0, 0, 0:1], t.MHALF[0:1, 0:1], ACT.Gelu).then_inc(primed, 1)
            act.wait_ge(primed, 1)
            act.sem_inc(hidden, MT)
            for g in range(NG):
                act.wait_ge(split, g + 1)
                for m in range(MT):
                    act.wait_ge(up_mm, MT * g + m + 1)
                    nc.scalar.activation(HF[:, g % 2, m, :], t.psum[m], ACT.Gelu,
                                         bias=BIAS[:, m:m + 1], scale=1.0 / WS).then_inc(hidden, 1)

        @block.vector
        def _(dve):
            norm.vector(dve)

            def link(ins):
                link.n += 1
                ins.then_inc(dve_step, 1)
                dve.wait_ge(dve_step, link.n)
            link.n = 0
            tt, ts, stt = dve.tensor_tensor, dve.tensor_scalar, dve.scalar_tensor_tensor
            rank = t.GB[:, 1:2, :].broadcast_to([P, NT, NE])

            def first_of_largest(out, logits, largest):
                link(dve.tensor_reduce(largest, logits, AX.X, ALU.max))
                link(tt(EQ, logits, wide(largest), ALU.is_equal))
                link(tt(V, EQ, rank, ALU.mult))
                link(dve.tensor_reduce(MV, V, AX.X, ALU.max))
                link(tt(out, V, wide(MV), ALU.is_equal))

            dve.sem_inc(split, 2)
            dve.sem_inc(down_mm, 2)
            dve.sem_inc(merged, 2)
            dve.memset(ONE, 1.0)
            dve.memset(t.EID[0:1, 1, 0, 0:2], 0)
            dve.memset(t.EID[0:1, 2, SLOTS // UN - 1, UN - 2:UN], 0)
            dve.wait_ge(gate_mm, 1)
            link(stt(L, t.psum[6][:, 0:n].rearrange("p (t e) -> p t e", e=NE), 1.0 / WS,
                     t.GB[:, 0:1, :].broadcast_to([P, NT, NE]), ALU.mult, ALU.add))
            first_of_largest(O1, L, M1)
            link(stt(L, O1, LOWEST, L, ALU.mult, ALU.add))
            first_of_largest(O2, L, M2)
            tt(CHOSEN.rearrange("p e t -> p t e"), O1, O2, ALU.add).then_inc(chosen_set, 1)
            tt(GAP, M2, M1, ALU.subtract).then_inc(gap, 1)
            dve.wait_ge(ranked, 1)
            before, totals = (t.psum[i][:, 0:n] for i in (6, 7))
            inc = INC.rearrange("p e t -> p (e t)")
            link(dve.tensor_tensor_scan(inc, ONE, totals, 0.0, ALU.mult, ALU.add))
            link(tt(TEMP.rearrange("p e t -> p (e t)"), inc, totals, ALU.subtract))
            tt(POS.rearrange("p e t -> p (e t)"), TEMP.rearrange("p e t -> p (e t)"), before, ALU.add)
            link(dve.tensor_copy(LASTS, INC[:, :, NT - 1]))
            dve.tensor_copy(COUNT[:, 0:1], LASTS[:, 0:1])
            link(tt(COUNT[:, 1:NE], LASTS[:, 1:NE], LASTS[:, 0:NE - 1], ALU.subtract))
            link(ts(TILES, COUNT, TS - 1.0, 1.0 / TS, ALU.add, ALU.mult))
            link(ts(TILES, TILES, -(TS - 1.0) / (2 * TS), ROUND, ALU.add, ALU.add))
            link(ts(TILES, TILES, -ROUND, None, ALU.add))
            link(dve.tensor_tensor_scan(UPTO, ONE[:, 0:NE], TILES, 0.0, ALU.mult, ALU.add))
            tt(SHIFT, UPTO, TILES, ALU.subtract)
            link(tt(LASTS, LASTS, COUNT, ALU.subtract))
            link(stt(SHIFT, SHIFT, float(TS), LASTS, ALU.mult, ALU.subtract))
            link(tt(POS, POS, SHIFT.rearrange("p (e o) -> p e o", o=1).broadcast_to([P, NE, NT]), ALU.add))
            for k, chosen in enumerate((O1, O2)):
                link(tt(V, chosen, POS.rearrange("p e t -> p t e"), ALU.mult))
                link(dve.tensor_reduce(PK, V, AX.X, ALU.add))
                dve.tensor_copy(t.PLACE[:, k, :], PK).then_inc(placed, 1)
                dve.wait_ge(placed, k + 1)
            link(tt(CMP, t.SLOTNO.rearrange("p (s o) -> p s o", o=1).broadcast_to([1, SLOTS, NE]),
                    UPTO[0:1].rearrange("p (o e) -> p o e", o=1).broadcast_to([1, SLOTS, NE]), ALU.is_ge))
            link(dve.tensor_reduce(EIDF, CMP, AX.X, ALU.add))
            link(ts(EIDF, EIDF, NE - 1.0, None, ALU.min))
            flat = t.EID.rearrange("p k r u -> p k (r u)")
            dve.tensor_copy(flat[:, 0, :], EIDF)
            dve.tensor_copy(flat[:, 1, 2:SLOTS], EIDF[:, 0:SLOTS - 2])
            dve.tensor_copy(flat[:, 2, 0:SLOTS - 2], EIDF[:, 2:SLOTS])
            dve.wait_ge(ratio, 1)
            link(ts(DEN, GAP, 1.0, None, ALU.add))
            link(dve.reciprocal(M1, DEN))
            link(tt(M2, GAP, M1, ALU.mult))
            ts(t.WEIGHT[:, 0, :], M1, 1.0 / WS, None, ALU.mult)
            ts(t.WEIGHT[:, 1, :], M2, 1.0 / WS, None, ALU.mult)

            def split_step(g):
                dve.wait_ge(down_mm, g + 1)
                dve.wait_ge(hidden, MT * g + 2 * MT)
                dve.tensor_copy(H16[:, g % 2, 0], HF[:, g % 2]).then_inc(high, 1)
                dve.wait_ge(high, g + 1)
                dve.tensor_tensor(H16[:, g % 2, 1], HF[:, g % 2], H16[:, g % 2, 0], ALU.subtract).then_inc(split, 1)

            def merge_step(g):
                dve.wait_ge(down_mm, g + 3)
                res = t.RES[:, GT * g:GT * g + GT, :]
                stt(res, t.psum[4 + g % 2].rearrange("p (j d) -> p j d", d=D), 1.0 / WS, res, ALU.mult, ALU.add).then_inc(merged, 1)

            for g in range(NG):
                split_step(g)
                if g >= 1:
                    merge_step(g - 1)
            merge_step(NG - 1)


def routed_stage(nc, t, tag, store=None):
    with ExitStack() as ctx:
        sem = stage_semaphores(nc, ctx, f"s{tag}_")
        at = [0]

        def carve(dt, *shape):
            n = int(np.prod(shape))
            words = n if dt == F32 else n // 2
            v = t.arena[:, at[0]:at[0] + words]
            at[0] += words
            v = v if dt == F32 else v.bitcast(dt)
            names = "abcde"[:len(shape)]
            if len(shape) > 1:
                v = v.rearrange(f"p ({' '.join(names)}) -> p {' '.join(names)}", **dict(zip(names, shape)))
            return v

        NHALF = TS // P
        CT = 8
        SLOT = [carve(F16, NHALF, ROW) for _ in range(UN)]
        XST = [carve(F16, 2, TS) for _ in range(2)]
        HF = [carve(F32, MT, TS) for _ in range(2)]
        H16 = [carve(F16, 2, MT, TS) for _ in range(4)]
        Y = [carve(F32, NHALF, D) for _ in range(4)]
        BIAS = [carve(F32, MT) for _ in range(4)]
        BACK = [carve(F32, 2, CT, D) for _ in range(2)]
        xs, yo = t.dram["slots" + tag], t.dram["expert_out" + tag]
        slot_in, y_out = [sem(f"slot_in{i}") for i in range(UN)], [sem(f"y_out{i}") for i in range(4)]
        turned, xt_set, up_mm, hidden, high, split, down_mm, y_set = (sem(n) for n in (
            "turned", "xt_set", "up_mm", "hidden", "high", "split", "down_mm", "y_set"))
        back_in, back_added, first_added, primed, gated, stored = (
            [sem(f"back_in{i}") for i in range(2)], sem("back_added"), sem("first_added"), sem("primed"), sem("gated"), sem("stored"))
        ps = t.psum
        UP = [t.psum_all[:, 2 + 2 * i:4 + 2 * i, :].rearrange("p b (m n) -> p (b m) n", n=TS) for i in range(2)]
        bias_set = sem("bias_set")
        block = ctx.enter_context(nc.Block())

        def after(eng, s, n):
            if not (isinstance(n, int) and n <= 0):
                eng.wait_ge(s, n)

        def rounds(eng, body):
            body(0, True, False)
            with eng.Fori(1, SLOTS // UN - 1) as k:
                body(k, False, False)
            body(SLOTS // UN - 1, False, True)

        def written(k, i):
            return k * (16 * NHALF * UN // 4) + 16 * NHALF * (i // 4 + 1)

        names = [0]

        def expert_values(eng, k, table):
            names[0] += 1
            regs = [eng.alloc_register(f"{tag}_experts{names[0]}_{i}") for i in range(UN)]
            eng.load(regs, t.EID[0:1, table, k, :])
            return [eng.snap(r, min_val=0, max_val=NE - 1) for r in regs]

        @block.sync
        def _(sp):
            tiles = xs.rearrange("(s h p) r -> s p h r", p=P, h=NHALF)

            def body(k, first, last):
                for i in range(UN):
                    after(sp, y_out[i % 4], written(k, i) - 16 * NHALF * (UN // 4))
                    sp.dma_start(SLOT[i].bitcast(I32), tiles[k * UN + i]).then_inc(slot_in[i], 16)
            rounds(sp, body)
            for i in range(4):
                sp.wait_ge(y_out[i], 16 * NHALF * SLOTS // 4)
            rows = yo.rearrange("(k t p) d -> p k t d", k=2, p=P)

            def fetch(c):
                for k in range(2):
                    sp.dma_start(BACK[c % 2][:, k], rows[:, k, CT * c:CT * c + CT]).then_inc(back_in[c % 2], 16)
            fetch(0)
            fetch(1)
            for c in range(NT // CT):
                if c + 2 < NT // CT or store is not None:
                    sp.wait_ge(back_added, c + 1)
                if c + 2 < NT // CT:
                    fetch(c + 2)
                if store is not None:
                    sp.dma_start(store[:, CT * c:CT * c + CT, :], t.RES[:, CT * c:CT * c + CT, :]).then_inc(stored, 16)
            if store is not None:
                sp.wait_ge(stored, 16 * NT // CT)

        @block.gpsimd
        def _(pool):
            def body(k, first, last):
                for i in range(UN):
                    after(pool, gated, k * UN + i)
                    after(pool, y_set, k * UN + i + 1)
                    nc.gpsimd.tensor_tensor(t.GATE[:, 0:1], t.MHALF[:, 0:1], t.MHALF[:, 0:1], ALU.add).then_inc(gated, 1)
                    for h in range(NHALF):
                        target = SLOT[i].bitcast(I32)[:, h, ROW // 2 - 1:ROW // 2]
                        nc.gpsimd.indirect_dma_start(yo, bass.IndirectOffsetOnAxis(ap=target, axis=0), Y[i % 4][:, h], None,
                                                     bounds_check=2 * NT * P - 1, oob_is_err=False).then_inc(y_out[i % 4], 16)
            rounds(pool, body)

        @block.tensor
        def _(pe):
            def turn(k, i):
                n = k * UN + i
                after(pe, slot_in[i], 16 * k + 16)
                after(pe, xt_set, n - 1)
                for part in range(2):
                    for h in range(NHALF):
                        at = TS * part + P * h
                        ins = pe.transpose(ps[i % 2].bitcast(F16)[:, at:at + P],
                                           SLOT[i][:, h, P * part:P * part + P], t.ID16)
                ins.then_inc(turned, 1)

            def up(k, i, e):
                n = k * UN + i
                after(pe, xt_set, n + 1)
                after(pe, hidden, n - 1)
                for m in range(MT):
                    out, ms = UP[i % 2][:, m, :], slice(P * m, P * m + P)
                    pe.matmul(out, t.W1H[:, e, ms], XST[i % 2][:, 0], start=True, stop=False)
                    pe.matmul(out, t.W1H[:, e, ms], XST[i % 2][:, 1], start=False, stop=False)
                    ins = pe.matmul(out, t.W1L[:, e, ms], XST[i % 2][:, 0], start=False, stop=True)
                ins.then_inc(up_mm, 1)

            def down(k, i, e):
                n = k * UN + i
                after(pe, split, n + 1)
                after(pe, y_set, n - 1)
                for h in range(NHALF):
                    out = ps[6 + i % 2][:, D * h:D * h + D]
                    pe.matmul(out, t.ONES16[0:2, :], t.B2P[0:2, e, :], start=True, stop=False)
                    for m in range(MT):
                        hh, hl = (H16[i % 4][:, part, m, P * h:P * h + P] for part in range(2))
                        pe.matmul(out, hh, t.W2L[:, e, m, :], start=False, stop=False)
                        pe.matmul(out, hh, t.W2H[:, e, m, :], start=False, stop=False)
                        ins = pe.matmul(out, hl, t.W2H[:, e, m, :], start=False, stop=(m == MT - 1))
                ins.then_inc(down_mm, 1)

            def body(k, first, last):
                mine = expert_values(pe, k, 0)
                late = expert_values(pe, k, 1)
                if first:
                    turn(0, 0)
                for i in range(UN):
                    if not (last and i == UN - 1):
                        turn(k if i < UN - 1 else k + 1, (i + 1) % UN)
                    up(k, i, mine[i])
                    if not (first and i < 2):
                        down(k, i - 2, late[i])
                if last:
                    down(k, UN - 2, mine[UN - 2])
                    down(k, UN - 1, mine[UN - 1])
            rounds(pe, body)

        @block.scalar
        def _(act):
            def take(k, i):
                n = k * UN + i
                after(act, turned, n + 1)
                after(act, up_mm, n - 1)
                nc.scalar.activation(XST[i % 2], ps[i % 2].bitcast(F16)[:, 0:2 * TS].rearrange("p (k n) -> p k n", n=TS),
                                     ACT.Copy).then_inc(xt_set, 1)

            def body(k, first, last):
                if first:
                    take(0, 0)
                for i in range(UN):
                    n = k * UN + i
                    if not (last and i == UN - 1):
                        take(k if i < UN - 1 else k + 1, (i + 1) % UN)
                    after(act, bias_set, n + 1)
                    after(act, split, n - 1)
                    after(act, up_mm, n + 1)
                    for m in range(MT):
                        ins = nc.scalar.activation(HF[i % 2][:, m], UP[i % 2][:, m], ACT.Gelu,
                                                   bias=BIAS[i % 4][:, m:m + 1], scale=1.0 / WS)
                    ins.then_inc(hidden, 1)
            nc.scalar.activation(t.GATE[0:1, 1:2], t.MHALF[0:1, 0:1], ACT.Gelu).then_inc(primed, 1)
            rounds(act, body)

        @block.vector
        def _(dve):
            def take_out(k, i):
                n = k * UN + i
                after(dve, down_mm, n + 1)
                after(dve, y_out[i % 4], written(k, i) - 16 * NHALF)
                dve.tensor_copy(Y[i % 4], ps[6 + i % 2][:, 0:NHALF * D].rearrange("p (h d) -> p h d", d=D)).then_inc(y_set, 1)

            def fetch_bias(i, e):
                dve.tensor_copy(BIAS[i % 4], t.B1[:, e, :]).then_inc(bias_set, 1)

            def body(k, first, last):
                ahead = expert_values(dve, k, 2)
                if first:
                    for i, e in enumerate(expert_values(dve, 0, 0)[0:2]):
                        fetch_bias(i, e)
                for i in range(UN):
                    n = k * UN + i
                    after(dve, hidden, n + 1)
                    after(dve, down_mm, n - 3)
                    dve.tensor_copy(H16[i % 4][:, 0], HF[i % 2]).then_inc(high, 1)
                    dve.wait_ge(high, n + 1)
                    dve.tensor_tensor(H16[i % 4][:, 1], HF[i % 2], H16[i % 4][:, 0], ALU.subtract).then_inc(split, 1)
                    if not (last and i >= UN - 2):
                        fetch_bias(i + 2, ahead[i])
                    if not (first and i < 2):
                        take_out(k, i - 2)
                if last:
                    take_out(k, UN - 2)
                    take_out(k, UN - 1)
            rounds(dve, body)
            for c in range(NT // CT):
                dve.wait_ge(back_in[c % 2], 32 * (c // 2 + 1))
                for k in range(2):
                    for j in range(CT):
                        i = CT * c + j
                        res = t.RES[:, i, :]
                        ins = dve.scalar_tensor_tensor(res, BACK[c % 2][:, k, j], t.WEIGHT[:, k, i:i + 1], res, ALU.mult, ALU.add)
                    if k == 0:
                        ins.then_inc(first_added, 1)
                        dve.wait_ge(first_added, c + 1)
                ins.then_inc(back_added, 1)
                if store is None:
                    dve.wait_ge(back_added, c + 1)
                    for i in range(CT * c, CT * c + CT):
                        dve.bn_stats(t.RSTATS[:, i, :], t.RES[:, i, :])
def attention_stage(nc, t):
    with ExitStack() as ctx:
        sem = stage_semaphores(nc, ctx, "a_")
        at = [0]

        def carve(dt, *shape):
            n = int(np.prod(shape))
            words = n if dt == F32 else n // 2
            v = t.arena[:, at[0]:at[0] + words]
            at[0] += words
            v = v if dt == F32 else v.bitcast(dt)
            names = "abcde"[:len(shape)]
            if len(shape) > 1:
                v = v.rearrange(f"p ({' '.join(names)}) -> p {' '.join(names)}", **dict(zip(names, shape)))
            return v

        QPAD = [carve(F16, HG, GH, SEQ) for _ in range(2)]
        KST = [carve(F16, HG, SEQ) for _ in range(2)]
        QST = carve(F16, HG, SEQ)
        HI = carve(F16, 2, SEQ)
        V32 = [carve(F32, TPB, NH, 32) for _ in range(2)]
        PR = [carve(F32, 3, BANK) for _ in range(2)]
        OT = [carve(F32, HG, SEQ) for _ in range(2)]
        ATT = carve(F32, TPB, D)
        ATH, ATL = carve(F16, SEQ), carve(F16, SEQ)
        MX = carve(F32, 2, TPB, GH, 2)
        M16 = carve(F16, 2, TPB, GH, 2, 2)
        MROW = [carve(F16, SEQ) for _ in range(2)]
        RC = carve(F32, TPB, NH)
        IDB, MASKB, MASKT = carve(BF16, P), carve(BF16, GH, P), carve(BF16, GH, P)
        ID16 = t.ID16
        CWF, CRF = carve(F32, 2 * HG, P), carve(F32, SEQ)
        CW, CR = carve(F16, 2 * HG, P), carve(F16, SEQ)
        LOWROW = t.LOW
        XH = t.XTH.rearrange("p (b n) -> p b n", n=SEQ)
        XL = t.XTL.rearrange("p (b n) -> p b n", n=SEQ)
        RESB = t.RES.rearrange("p (b t) d -> p b (t d)", t=TPB)
        ps = t.psum

        (consts_in, cleared, masks, cast, ready, m_high, rc_set) = (sem(n) for n in (
            "consts_in", "cleared", "masks", "cast", "ready", "m_high", "rc_set"))
        (proj, v_mm, hi, parts, vset, m_mm, m_red, m16, mt_mm, mrow_set) = (sem(n) for n in (
            "proj", "v_mm", "hi", "parts", "vset", "m_mm", "m_red", "m16", "mt_mm", "mrow_set"))
        qpad_in, mrow_in = [sem(f"qpad_in{h}") for h in range(2)], [sem(f"mrow_in{h}") for h in range(2)]
        (st_mm, exps, av_mm, ot_set, ft_mm, att, fa_mm, att_hi, att_lo, fo_mm, added) = (sem(n) for n in (
            "st_mm", "exps", "av_mm", "ot_set", "ft_mm", "att", "fa_mm", "att_hi", "att_lo", "fo_mm", "added"))
        block = ctx.enter_context(nc.Block())

        def after(eng, s, n):
            if not (isinstance(n, int) and n <= 0):
                eng.wait_ge(s, n)

        def steps(body):
            def peeled(b):
                body(b, b % 2, (0 <= b < NB, -1 <= b < NB - 1, b < NB - 2, 1 <= b, 2 <= b))
            return peeled, lambda b, q: body(b, q, (True, True, True, True, True))

        def pipeline(eng, body):
            peeled, full = steps(body)
            for b in range(-2, 2):
                peeled(b)
            with eng.Fori(0, (NB - 4) // 2) as k:
                for i in range(2):
                    full(2 * k + (2 + i), i)
            for b in range(NB - 2, NB + 1):
                peeled(b)

        @block.sync
        def _(sp):
            sp.dma_start(CWF[0:3], t.dram["cw"]).then_inc(consts_in, 16)
            sp.dma_start(CRF[0:3], t.dram["cr"]).then_inc(consts_in, 16)
            sp.wait_ge(ready, 1)

            def spread_q(c, r, h):
                after(sp, parts, 8 * c + 4 * h + 4)
                for g in range(GH):
                    q = slice(32 * g, 32 * g + 32)
                    sp.dma_start(QPAD[r][q, 2 * h:2 * h + 2, g, :], QST[q, 2 * h:2 * h + 2, :]).then_inc(qpad_in[h], 16)

            def spread_m(c, r, h):
                after(sp, mrow_set, 2 * c + h + 1)
                for g in range(GH):
                    for part in range(2):
                        row, src = 32 * g + 26 + part, 4 * g + 2 * part
                        sp.dma_start(QPAD[r][row:row + 1, 2 * h:2 * h + 2, g, :],
                                     MROW[h][src:src + 2, :]).then_inc(mrow_in[h], 16)

            def body(b, q, stages):
                second, first, projections, output, finished = stages
                if second:
                    spread_m(b, q, 1)
                if projections:
                    spread_q(b + 2, q, 0)
                if first:
                    spread_m(b + 1, 1 - q, 0)
                if projections:
                    spread_q(b + 2, q, 1)
            pipeline(sp, body)

        @block.gpsimd
        def _(pool):
            for v in (QPAD[0], QPAD[1], V32[0], V32[1], IDB, MASKB, MASKT):
                nc.gpsimd.memset(v, 0.0).then_inc(cleared, 1)
            pool.wait_ge(cleared, 7)
            for v in V32:
                nc.gpsimd.memset(v[:, :, :, 8:9], 1.0).then_inc(masks, 1)
            nc.gpsimd.affine_select(out=IDB, in_=IDB, compare_op=ALU.not_equal, fill=1.0, base=0,
                                    pattern=[[-1, P]], channel_multiplier=1).then_inc(masks, 1)
            nc.gpsimd.affine_select(out=MASKB, in_=MASKB, compare_op=ALU.is_ge, fill=-1.0e30, base=0,
                                    pattern=[[0, GH], [-1, P]], channel_multiplier=1).then_inc(masks, 1)
            nc.gpsimd.affine_select(out=MASKT, in_=MASKT, compare_op=ALU.is_ge, fill=-1.0e30, base=0,
                                    pattern=[[0, GH], [1, P]], channel_multiplier=-1).then_inc(masks, 1)

        @block.tensor
        def _(pe):
            def project(c, G):
                for k in range(2):
                    out = ps[0][:, SEQ * k:SEQ * k + SEQ]
                    for i, (w, x) in enumerate(((t.QKWH, XH), (t.QKWH, XL), (t.QKWL, XH))):
                        pe.matmul(out, w[:, HG * k + G, :], x[:, c, :], start=(i == 0), stop=False)
                    ins = pe.matmul(out, CW[0:3, HG * k + G, :], CR[0:3, :], start=False, stop=True)
                ins.then_inc(proj, 1)

            def values(c):
                for tile in range(TPB):
                    js = slice(P * tile, P * tile + P)
                    for i, (x, w) in enumerate(((XH, t.VOWH), (XL, t.VOWH), (XH, t.VOWL))):
                        ins = pe.matmul(ps[0][:, js], x[:, c, js], w[:, 0:D], start=(i == 0), stop=(i == 2))
                ins.then_inc(v_mm, 1)

            def maxima(c, r, G, blocks):
                if G % 2 == 0 and 0 in blocks:
                    after(pe, qpad_in[G // 2], 64 * c + 64)
                for k in blocks:
                    n = 3 * G + k
                    bank = ps[2 + n % 2]
                    after(pe, m_red, 12 * c + n - 1)
                    if k == 0:
                        pe.matmul(bank, IDB, MASKB.rearrange("p g n -> p (g n)"), start=True, stop=False)
                        for g in range(GH):
                            ins = pe.matmul(bank[:, P * g:P * g + P], QPAD[r][:, G, g, 0:P], KST[r][:, G, 0:P],
                                            start=False, stop=(g == GH - 1))
                    else:
                        out = bank.rearrange("p (h t n) -> p h t n", t=TPB, n=P)
                        pe.matmul(out[:, :, 1, :], IDB, MASKB[:, 0:2, :], start=True, stop=False, skip_group_check=True)
                        for h in range(2):
                            g = 2 * (k - 1) + h
                            for tile in range(TPB):
                                ins = pe.matmul(out[:, h, tile, :], QPAD[r][:, G, g, P:2 * P],
                                                KST[r][:, G, P * tile:P * tile + P], start=False,
                                                stop=(h == 1 and tile == 1), skip_group_check=True)
                    ins.then_inc(m_mm, 1)

            def turn_maxima(c, h):
                after(pe, m16, 2 * c + h + 1)
                for tile in range(TPB):
                    ins = pe.transpose(ps[0].bitcast(F16)[0:16, P * tile:P * tile + P],
                                       M16[:, h, tile].rearrange("p g c h -> p (g c h)"), ID16)
                ins.then_inc(mt_mm, 1)

            def scores(b, q, G):
                if G % 2 == 0:
                    after(pe, mrow_in[G // 2], 128 * b + 128)
                after(pe, exps, 4 * b + G)
                for a in range(2):
                    out = ps[5 + a].rearrange("p (h t n) -> p h t n", t=TPB, n=P)
                    pe.matmul(out[:, :, 0, :], IDB, MASKT[:, 0:2, :], start=True, stop=False, skip_group_check=True)
                    pe.matmul(ps[5 + a], KST[q][:, G, 0:P], QPAD[q][:, G, 2 * a:2 * a + 2, :], start=False, stop=True,
                              skip_group_check=True)
                pe.matmul(ps[7], IDB, MASKT.rearrange("p g n -> p (g n)"), start=True, stop=False)
                pe.matmul(ps[7], KST[q][:, G, P:2 * P], QPAD[q][:, G, :, P:2 * P], start=False, stop=True).then_inc(st_mm, 1)

            def weigh(b, q, G):
                after(pe, exps, 4 * b + G + 1)
                if G == 0:
                    after(pe, vset, b + 1)
                if G % 2 == 0:
                    after(pe, ot_set, 2 * b - 1 + G // 2)
                half = ps[4][:, SEQ * (G % 2):SEQ * (G % 2) + SEQ]
                for g in range(GH):
                    out = half[32 * g:32 * g + 32, :]
                    early = PR[G % 2][:, g // 2, SEQ * (g % 2):SEQ * (g % 2) + SEQ]
                    late = PR[G % 2][:, 2, P * g:P * g + P]
                    pe.matmul(out, V32[q][:, 0, 4 * G + g, :], early, start=True, stop=False)
                    ins = pe.matmul(out[:, P:2 * P], V32[q][:, 1, 4 * G + g, :], late, start=False, stop=True)
                ins.then_inc(av_mm, 1)

            def turn_back(b, q, tile):
                if tile == 0:
                    after(pe, ot_set, 2 * b + 2)
                    after(pe, added, b)
                else:
                    after(pe, att, 2 * b + 1)
                for G in range(HG):
                    ins = pe.transpose(ps[1][:, P * G:P * G + P], OT[q][:, G, P * tile:P * tile + P], t.ID)
                ins.then_inc(ft_mm, 1)

            def turn_out(b):
                after(pe, att, 2 * b + 2)
                for tile in range(TPB):
                    ins = pe.transpose(ps[1][:, P * tile:P * tile + P], ATT[:, tile, :], t.ID)
                ins.then_inc(fa_mm, 1)

            def project_out(b):
                after(pe, att_lo, b + 1)
                for tile in range(TPB):
                    js, out = slice(P * tile, P * tile + P), slice(SEQ + P * tile, SEQ + P * tile + P)
                    for i, (x, w) in enumerate(((ATH, t.VOWH), (ATL, t.VOWH), (ATH, t.VOWL))):
                        ins = pe.matmul(ps[1][:, out], x[:, js], w[:, D:2 * D], start=(i == 0), stop=(i == 2))
                ins.then_inc(fo_mm, 1)

            def body(b, q, stages):
                second, first, projections, output, finished = stages
                for G in range(HG):
                    if second:
                        scores(b, q, G)
                    if G == 0 and second:
                        after(pe, vset, b + 1)
                        turn_maxima(b, 1)
                    if G == 2 and first:
                        if projections:
                            after(pe, parts, 8 * b + 20)
                        turn_maxima(b + 1, 0)
                    if first:
                        maxima(b + 1, 1 - q, G, (0, 1))
                    if projections:
                        if G % 2 == 0:
                            after(pe, mrow_set, 2 * b + 2 + G // 2)
                        after(pe, parts, 8 * b + 16 + 2 * G)
                        project(b + 2, G)
                    if first:
                        maxima(b + 1, 1 - q, G, (2,))
                    if output:
                        if G < TPB:
                            turn_back(b - 1, 1 - q, G)
                        elif G == 2:
                            turn_out(b - 1)
                        else:
                            project_out(b - 1)
                    if second:
                        weigh(b, q, G)
                    if first and G == HG - 1:
                        if projections:
                            after(pe, parts, 8 * b + 24)
                        after(pe, mrow_set, 2 * b + 3)
                        values(b + 1)

            pe.wait_ge(cast, 2)
            pe.wait_ge(masks, 5)
            pipeline(pe, body)

        @block.scalar
        def _(act):
            act.wait_ge(consts_in, 32)
            nc.scalar.activation(CW[0:3], CWF[0:3], ACT.Copy).then_inc(cast, 1)
            nc.scalar.activation(CR[0:3], CRF[0:3], ACT.Copy).then_inc(cast, 1)
            nc.scalar.activation(RC[0:1, 0, 0:1], t.MHALF[0:1, 0:1], ACT.Exp).then_inc(cast, 1)
            act.wait_ge(cast, 3)
            act.wait_ge(masks, 2)
            act.sem_inc(ready, 1)

            def highs(c, G):
                after(act, proj, 4 * c + G + 1)
                nc.scalar.activation(HI, ps[0].rearrange("p (k n) -> p k n", n=SEQ), ACT.Copy).then_inc(hi, 1)

            def values(c, r):
                after(act, v_mm, c + 1)
                nc.scalar.activation(V32[r][:, :, :, 0:8], ps[0][:, 0:SEQ].rearrange("p (t h d) -> p t h d", t=TPB, d=8),
                                     ACT.Copy).then_inc(vset, 1)

            def maxima_rows(c, h):
                after(act, mt_mm, 2 * c + h + 1)
                after(act, mrow_in[h], 128 * c)
                nc.scalar.activation(MROW[h][0:16, :], ps[0].bitcast(F16)[0:16, 0:SEQ], ACT.Copy).then_inc(mrow_set, 1)

            def expo(b, G):
                after(act, st_mm, 4 * b + G + 1)
                after(act, av_mm, 4 * b + G - 1)
                nc.scalar.activation(PR[G % 2], t.psum_all[:, 5:8, :], ACT.Exp, scale=1.0 / LOGIT).then_inc(exps, 1)

            def take_out(b, q, half):
                after(act, av_mm, 4 * b + 2 * half + 2)
                nc.scalar.activation(OT[q][:, 2 * half:2 * half + 2, :], ps[4].rearrange("p (g n) -> p g n", n=SEQ),
                                     ACT.Copy).then_inc(ot_set, 1)

            def out_high(b):
                after(act, fa_mm, b + 1)
                nc.scalar.activation(ATH, ps[1][:, 0:SEQ], ACT.Copy).then_inc(att_hi, 1)

            def body(b, q, stages):
                second, first, projections, output, finished = stages
                for G in range(HG):
                    if second:
                        expo(b, G)
                    if G == 0 and second:
                        maxima_rows(b, 1)
                    if G == 2 and first:
                        maxima_rows(b + 1, 0)
                    if projections:
                        highs(b + 2, G)
                    if output and G == 2:
                        out_high(b - 1)
                    if second and G % 2 == 1:
                        take_out(b, q, G // 2)
                if first:
                    values(b + 1, 1 - q)
            pipeline(act, body)

        @block.vector
        def _(dve):
            tt, ts, stt = dve.tensor_tensor, dve.tensor_scalar, dve.scalar_tensor_tensor

            def split(c, r, G):
                after(dve, hi, 4 * c + G + 1)
                if G % 2 == 0:
                    after(dve, qpad_in[G // 2], 64 * c)
                after(dve, st_mm, 4 * c + G - 7)
                for k, out in enumerate((QST, KST[r])):
                    stt(out[:, G, :], HI[:, k, :], LOWROW[:, k:k + 1], ps[0][:, SEQ * k:SEQ * k + SEQ],
                        ALU.mult, ALU.add).then_inc(parts, 1)

            def reduce(c, G):
                for k in range(3):
                    n = 3 * G + k
                    after(dve, m_mm, 12 * c + n + 1)
                    if k == 0:
                        out, src = MX[:, G // 2, 0, :, G % 2], ps[2 + n % 2].rearrange("p (g n) -> p g n", n=P)
                    else:
                        out, src = MX[:, G // 2, 1, 2 * (k - 1):2 * k, G % 2], ps[2 + n % 2].rearrange("p (g n) -> p g n", n=SEQ)
                    dve.tensor_reduce(out, src, AX.X, ALU.max).then_inc(m_red, 1)

            def split_maxima(c, h):
                after(dve, m_red, 12 * c + 6 * h + 6)
                after(dve, mt_mm, 2 * c + h - 1)
                mx = MX[:, h].rearrange("p t g h -> p (t g) h")
                hi_m, lo_m = (M16[:, h, :, :, i, :].rearrange("p t g h -> p (t g) h") for i in range(2))
                ts(hi_m, mx, -1.0 / 1024, None, ALU.mult).then_inc(m_high, 1)
                after(dve, m_high, 2 * c + h + 1)
                stt(lo_m, mx, -1.0 / 1024, hi_m, ALU.mult, ALU.subtract).then_inc(m16, 1)

            def normalise(b, tile):
                after(dve, ft_mm, 2 * b + tile + 1)
                src = ps[1].rearrange("p (h d) -> p h d", d=32)
                dve.reciprocal(RC[:, tile, :], src[:, :, 8]).then_inc(rc_set, 1)
                dve.wait_ge(rc_set, 2 * b + tile + 1)
                tt(ATT[:, tile, :].rearrange("p (h d) -> p h d", d=8), src[:, :, 0:8],
                   RC[:, tile, :].rearrange("p (h o) -> p h o", o=1).broadcast_to([P, NH, 8]), ALU.mult).then_inc(att, 1)

            def statistics(b):
                for tile in range(TPB):
                    dve.bn_stats(t.RSTATS[:, TPB * b + tile, :], t.RES[:, TPB * b + tile, :])

            def out_low(b):
                after(dve, att_hi, b + 1)
                tt(ATL, ps[1][:, 0:SEQ], ATH, ALU.subtract).then_inc(att_lo, 1)

            def add(b):
                after(dve, fo_mm, b + 1)
                stt(RESB[:, b, :], ps[1][:, SEQ:2 * SEQ], 1.0 / (WQ * WQ), RESB[:, b, :], ALU.mult, ALU.add).then_inc(added, 1)

            def body(b, q, stages):
                second, first, projections, output, finished = stages
                for G in range(HG):
                    if first:
                        reduce(b + 1, G)
                    if finished and G == 2:
                        after(dve, added, b - 1)
                    if projections:
                        split(b + 2, q, G)
                    if finished and G == 2:
                        statistics(b - 2)
                    if first and G % 2 == 1:
                        split_maxima(b + 1, G // 2)
                    if output:
                        if G < TPB:
                            normalise(b - 1, G)
                        elif G == 2:
                            out_low(b - 1)
                        else:
                            add(b - 1)
            pipeline(dve, body)
            dve.wait_ge(added, NB)
            statistics(NB - 1)
def host_tables():
    c = {}
    s = np.arange(SEQ)
    f = np.arange(SEQ)
    ang = 2 * np.pi * np.outer(s, f) / NFFT
    fwd = np.concatenate([np.cos(ang), -np.sin(ang)], 1)
    fwd[:, SEQ] = (-1.0) ** s
    inv = np.concatenate([2 * np.cos(ang.T), -2 * np.sin(ang.T)], 0) / NFFT
    inv[0] = 1.0 / NFFT
    inv[SEQ] = (-1.0) ** s / NFFT
    c["fwd"] = fwd.reshape(TPB, P, NFFT)
    c["inv"] = inv.reshape(NFT, P, SEQ)
    off = np.zeros((P, 4))
    off[:NM] = [0.25, 0.25, 0.5, 0]
    off[NM:] = [0.5, 0, 0.25, 0]
    c["offsets"] = off
    keep = np.zeros((P, 2))
    keep[:, 0] = 1
    keep[0] = [0, 1]
    c["keep"] = keep
    c["rank"] = np.tile(np.arange(NE, 0, -1.0), (P, 1))
    slopes = 2.0 ** (-8.0 / NH * np.arange(1, NH + 1)) * LOGIT / WQ
    cw = np.zeros((3, 2, HG, GH, 32))
    cw[2, 0, :, :, 24:26] = WQ
    high = slopes.astype(np.float16).astype(np.float64)
    cw[0, 1, :, :, 24:26] = high.reshape(HG, GH, 1)
    cw[1, 1, :, :, 24:26] = (slopes - high).astype(np.float16).astype(np.float64).reshape(HG, GH, 1)
    cw[2, 1, :, :, 26:28] = 1024
    c["cw"] = cw.reshape(3, 2 * HG, P)
    c["cr"] = np.stack([np.arange(SEQ), np.arange(SEQ), np.ones(SEQ)])
    c["slotno"] = np.arange(SLOTS).reshape(1, SLOTS)
    low = np.zeros((GH, 32, 3))
    low[0, 1, 2] = -1
    low[:, 16:24, 0] = -1
    low[:, 8:16, 1] = -1
    low[:, 25, 1] = -1
    c["lowrow"] = low.reshape(P, 3)
    c["ident"] = np.eye(P)
    return {k: np.ascontiguousarray(v, dtype=np.float32) for k, v in c.items()}


def build(nc, dram):
    with ExitStack() as ctx:
        t = Bag()
        t.dram = dram

        def sb(name, shape, dt=F32):
            return ctx.enter_context(nc.sbuf_tensor(name, shape, dt))
        t.RES = sb("RES", [P, NT, D])[:]
        t.XN = sb("XN", [P, NT, D])[:]
        t.ID = sb("ID", [P, P])[:]
        t.STATS = sb("STATS", [P, NT, 6])[:]
        t.RSTATS = sb("RSTATS", [P, NT, 6])[:]
        t.NRM = sb("NRM", [P, 8, 2 * NT])[:]
        t.MHALF = sb("MHALF", [P, NT])[:]
        t.psum_all = ctx.enter_context(nc.psum_tensor("banks", [P, 8, BANK], F32))[:]
        t.psum = [t.psum_all[:, i, :] for i in range(8)]
        t.W1H, t.W1L = sb("W1H", [P, NX, HID], F16)[:], sb("W1L", [P, NX, HID], F16)[:]
        t.W2H, t.W2L = sb("W2H", [P, NX, MT, D], F16)[:], sb("W2L", [P, NX, MT, D], F16)[:]
        t.GWH, t.GWL = sb("GWH", [P, NE], F16)[:], sb("GWL", [P, NE], F16)[:]
        t.QKWH, t.QKWL = sb("QKWH", [P, 2 * HG, P], F16)[:], sb("QKWL", [P, 2 * HG, P], F16)[:]
        t.VOWH, t.VOWL = sb("VOWH", [P, 2 * D], F16)[:], sb("VOWL", [P, 2 * D], F16)[:]
        t.XTH, t.XTL = sb("XTH", [P, NT * P], F16)[:], sb("XTL", [P, NT * P], F16)[:]
        t.B1 = sb("B1", [P, NX, MT])[:]
        t.ID16, t.ONES16, t.BEFORE = sb("ID16", [P, P], F16)[:], sb("ONES16", [P, P], F16)[:], sb("BEFORE", [P, P], F16)[:]
        t.LOW, t.GATE = sb("LOW", [P, 3])[:], sb("GATE", [P, 2])[:]
        t.EID = sb("EID", [1, 3, SLOTS // UN, UN], I32)[:]
        t.SLOTNO = sb("SLOTNO", [1, SLOTS])[:]
        t.PLACE, t.WEIGHT = sb("PLACE", [P, 2, NT], I32)[:], sb("WEIGHT", [P, 2, NT])[:]
        t.EMPTY = sb("EMPTY", [P, ROW], F16)[:]
        t.GB = sb("GB", [P, 2, NE])[:]
        t.B2, t.B2P = sb("B2", [2, NX, D])[:], sb("B2P", [2, NX, D], F16)[:]
        t.STG = [half.bitcast(F32)[:, HID * i:HID * i + HID] for half in (t.XTH, t.XTL) for i in range(NT * P // (2 * HID))]
        t.arena = sb("ARENA", [P, ARENA])[:]
        t.ROWS = t.arena[:, ARENA - NT * ROW // 2:ARENA].bitcast(F16).rearrange("p (t r) -> p t r", r=ROW)
        conv_stage(nc, t)
        shared_stage(nc, t, "f")
        routed_stage(nc, t, "f")
        norm_stage(nc, t, "a")
        attention_stage(nc, t)
        shared_stage(nc, t, "g")
        routed_stage(nc, t, "g", store=dram["out"].rearrange("b (t p) d -> p (b t) d", p=P))


def kernel(**inputs):
    import concourse.bacc as bacc
    from concourse.bass_utils import run_bass_kernel_spmd

    def of(name):
        return np.asarray(inputs["L0_" + name])

    def both(a):
        return np.concatenate([a.T, a.T], 0)

    arrays = host_tables()
    arrays["x"] = of("attn_a_x")
    arrays["params"] = np.stack([both(of("attn_a_log_A_real")), both(of("attn_a_A_imag")), both(of("attn_a_C_re")),
                                 both(of("attn_a_C_im")), np.broadcast_to(of("attn_a_log_dt"), (P, D))])
    arrays["ln"] = np.stack([np.broadcast_to(of("attn_a_ln_w"), (P, D)), np.broadcast_to(of("attn_a_ln_b"), (P, D))])
    arrays["dcol"] = of("attn_a_D").reshape(D, 1)
    arrays["w1"] = np.concatenate([of("ffn_w1"), of("ffn_ws1")[None]])
    arrays["w2"] = np.concatenate([of("ffn_w2"), of("ffn_ws2")[None]])
    arrays["b1"] = np.concatenate([of("ffn_b1"), of("ffn_bs1")[None]]).reshape(NX, MT, P).transpose(2, 0, 1)
    arrays["b2_rows"] = np.broadcast_to(np.concatenate([of("ffn_b2"), of("ffn_bs2")[None]]), (2, NX, D))
    qkv = of("attn_b_Wqkv").reshape(D, 3, HG, GH, 1, HD)
    w_qk = np.zeros((D, 2, HG, GH, 4, HD), np.float32)
    w_qk[:, :, :, :, 0:3] = qkv[:, 0:2]
    arrays["w_qk"] = w_qk.reshape(D, 2 * HG, P)
    arrays["w_vo"] = np.concatenate([of("attn_b_Wqkv")[:, 2 * D:], of("attn_b_Wout")], 1)
    arrays["gate_w"] = of("ffn_gate_w")
    arrays["gate_b"] = np.broadcast_to(of("ffn_gate_b"), (P, NE))
    arrays = {k: np.ascontiguousarray(v) for k, v in arrays.items()}
    nc = bacc.Bacc("TRN2", target_bir_lowering=False, num_devices=1)
    dram = {k: nc.dram_tensor("in_" + k, v.shape, F32, kind="ExternalInput").ap() for k, v in arrays.items()}
    for tag in "fg":
        dram["slots" + tag] = nc.dram_tensor("slots_" + tag, (SLOTS * TS, ROW // 2), I32).ap()
        dram["expert_out" + tag] = nc.dram_tensor("expert_out_" + tag, (2 * NT * P, D), F32).ap()
    dram["out"] = nc.dram_tensor("out_x", (NB, SEQ, D), F32, kind="ExternalOutput").ap()
    build(nc, dram)
    result = run_bass_kernel_spmd(nc, [{"in_" + k: v for k, v in arrays.items()}], core_ids=[0])
    return result.results[0]["out_x"]
```

```python
from contextlib import ExitStack

import numpy as np

import concourse.bass as bass
from concourse import mybir

ALU = mybir.AluOpType
ACT = mybir.ActivationFunctionType
AX = mybir.AxisListType
F32 = mybir.dt.float32
F16 = mybir.dt.float16
BF16 = mybir.dt.bfloat16
I32 = mybir.dt.int32

P = 128
D = 128
NB, SEQ = 16, 256
NT = NB * SEQ // P
TPB = SEQ // P
BANK = 512
EPS = 1e-5

NM = 64
LF = 16
NFFT = 2 * SEQ
NFT = NFFT // P
CB = BANK // D
NCG = NB // CB
ROUND = 12582912.0
TWO_PI_HI = 6.28125
TWO_PI_LO = 2 * np.pi - TWO_PI_HI
TURN = 6.283185

NE, HID = 8, 512
NX = NE + 1
MT = HID // P
GT = BANK // P
NG = NT // GT
WS = 1024.0
UN = 8
TS = 2 * P
SLOTS = (2 * NT * P + NE * (TS - 1)) // TS
ROUNDS = -(-SLOTS // UN)
ROW = 2 * D + 2
NH, HD = 16, 8
GH, HG = 4, 4
WQ = 64.0
LOGIT = WQ * WQ * HD ** 0.5
LOWEST = -3.0e38
ARENA = 22 * 1024 + 512


class Bag:
    pass


def norm_statistics(dve, link, stats, m):
    me, mo = stats[:, :, 1], stats[:, :, 4]
    se, so = stats[:, :, 2], stats[:, :, 5]
    dve.tensor_tensor(m.a, me, mo, ALU.add)
    dve.tensor_tensor(m.d, me, mo, ALU.subtract)
    link(dve.tensor_tensor(m.s, se, so, ALU.add))
    dve.tensor_scalar(m.mean, m.a, 0.5, None, ALU.mult)
    dve.tensor_tensor(m.q, m.d, m.d, ALU.mult)
    link(dve.tensor_scalar(m.s, m.s, 1.0 / D, EPS, ALU.mult, ALU.add))
    return dve.scalar_tensor_tensor(m.vareps, m.q, 0.25, m.s, ALU.mult, ALU.add)


def rows_of(buffer, first, last):
    m = Bag()
    m.a, m.d, m.s, m.q, m.mean, m.vareps, m.rstd, m.nmr = (buffer[:, i, first:last] for i in range(8))
    return m


def stage_semaphores(nc, ctx, prefix):
    taken = []

    def sem(name):
        taken.append(nc.alloc_semaphore(name=prefix + name))
        return taken[-1]

    def clear():
        nc.clear_and_free_semaphores(taken)
        nc.all_engine_barrier()
    ctx.callback(clear)
    return sem


def weight_jobs(t):
    jobs = []
    for e in range(NX):
        jobs.append((t.dram["w1"][e], t.W1H[:, e, :], t.W1L[:, e, :], HID, WS))
        jobs.append((t.dram["w2"][e].rearrange("(m p) d -> p m d", p=P), t.W2H[:, e], t.W2L[:, e], HID, WS))
    jobs.append((t.dram["gate_w"], t.GWH, t.GWL, NE, WS))
    for k in range(2):
        s = slice(HG * k, HG * k + HG)
        jobs.append((t.dram["w_qk"][:, s, :], t.QKWH[:, s, :], t.QKWL[:, s, :], HG * P, WQ))
    jobs.append((t.dram["w_vo"], t.VOWH, t.VOWL, 2 * D, WQ))
    return jobs


def conv_stage(nc, t):
    with ExitStack() as ctx:
        sem = stage_semaphores(nc, ctx, "c_")

        scratch = t.arena
        at = [0]

        def carve(*shape):
            n = int(np.prod(shape))
            v = scratch[:, at[0]:at[0] + n]
            at[0] += n
            if len(shape) == 2:
                v = v.rearrange("p (a b) -> p a b", b=shape[1])
            if len(shape) == 3:
                v = v.rearrange("p (a b c) -> p a b c", b=shape[1], c=shape[2])
            return v

        FW = carve(TPB, NFFT)
        IV = carve(NFT, SEQ)
        PRM = carve(6, D)
        WLN = carve(2, D)
        OFF = carve(4)
        DCOL = carve(1)
        KEEP = carve(2)
        TMP = carve(24, D)
        SIN2, SINA, SINB, KQ, PHR = (carve(LF, D) for _ in range(5))
        mag_at = at[0]
        MAG2, MAG1 = carve(LF, D), carve(LF, D)
        KCH = carve(SEQ)
        KLAG = carve(TPB, D)
        SPK = carve(4, 2, D)
        WHOLEB = t.XN[:, NT - LF:, :]
        KDIG = PHR
        M4 = [v.rearrange("p a h -> p (a h)").rearrange("p (k n) -> p k n", n=BANK) for v in (KQ, PHR)]
        YS = scratch[:, mag_at:mag_at + 2 * NFT * BANK].rearrange("p (k n) -> p k n", n=BANK)
        RN = SINB.rearrange("p a h -> p (a h)").rearrange("p (k n) -> p k n", n=BANK)
        XN = t.XN
        ps = t.psum

        params_in, x_in, dct_in, ln_in = sem("params_in"), sem("x_in"), sem("dct_in"), sem("ln_in")
        dve_step, pool_step = sem("dve_step"), sem("pool_step")
        exps, dt_ready, decay_ready, angle_ready = sem("exps"), sem("dt_ready"), sem("decay_ready"), sem("angle_ready")
        mags, phase_ready, sines = sem("mags"), sem("phase_ready"), sem("sines")
        ct_ready, e2_ready, e1_ready = sem("ct_ready"), sem("e2_ready"), sem("e1_ready")
        kdig_mm, kdig_sb, kch_mm, kch_sb, klag_mm, klag_sb = (sem(n) for n in (
            "kdig_mm", "kdig_sb", "kch_mm", "kch_sb", "klag_mm", "klag_sb"))
        kf_mm, spk_ready = sem("kf_mm"), sem("spk_ready")
        x_var, x_rstd, xn_ready = sem("x_var"), sem("x_rstd"), sem("xn_ready")
        fwd_mm, prod_ready, ys_ready, inv_mm = (sem(n) for n in (
            "fwd_mm", "prod_ready", "ys_ready", "inv_mm"))
        r_var, r_rstd, r_nmr, rn_ready, inv_read, res_ready = (sem(n) for n in (
            "r_var", "r_rstd", "r_nmr", "rn_ready", "inv_read", "res_ready"))

        empty_row, emptied = sem("empty_row"), sem("emptied")
        jobs = weight_jobs(t)
        NS = len(t.STG)
        job_in, high, low = [sem(f"job_in{i}") for i in range(NS)], sem("high"), sem("low")
        steps_ready, phase_b_ready = sem("steps_ready"), sem("phase_b_ready")
        small, fixed, b2_scaled, b2_high, x_nmr, scaled = sem("small"), sem("fixed"), sem("b2_scaled"), sem("b2_high"), sem("x_nmr"), sem("scaled")

        def staged(i):
            v = t.STG[i % NS][:, 0:jobs[i][3]]
            return v.rearrange("p (m d) -> p m d", d=D) if len(jobs[i][1].shape) == 3 else v

        EARLY = NS
        share = -(-(len(jobs) - EARLY) // NCG)
        portions = [range(0, EARLY)] + [range(EARLY + share * g, min(EARLY + share * (g + 1), len(jobs))) for g in range(NCG)]
        block = ctx.enter_context(nc.Block())
        C_RE, C_IM, LAR, AIM, LDT, DT = 2, 3, 0, 1, 4, 5

        @block.sync
        def _(sp):
            sp.dma_start(PRM[:, 0:5, :], t.dram["params"].rearrange("k p h -> p k h")).then_inc(params_in, 16)
            sp.dma_start(OFF, t.dram["offsets"]).then_inc(params_in, 16)
            sp.dma_start(t.RES[:, 0:NT // 2, :], t.dram["x"].rearrange("b (t p) d -> p (b t) d", p=P)[:, 0:NT // 2, :]).then_inc(x_in, 16)
            sp.dma_start(FW, t.dram["fwd"].rearrange("t p f -> p t f")).then_inc(dct_in, 16)
            sp.dma_start(KEEP, t.dram["keep"]).then_inc(dct_in, 16)
            def load(i):
                if i >= NS:
                    sp.wait_ge(low, i - NS + 1)
                sp.dma_start(staged(i), jobs[i][0]).then_inc(job_in[i % NS], 16)
            for i in range(NS):
                load(i)
            for v, name in ((t.LOW, "lowrow"), (t.B1, "b1"), (t.B2, "b2_rows"), (t.GB[:, 0, :], "gate_b"), (t.GB[:, 1, :], "rank"),
                            (t.SLOTNO, "slotno")):
                sp.dma_start(v, t.dram[name]).then_inc(small, 16)
            sp.wait_ge(empty_row, 2)
            for tag in "fg":
                sp.dma_start(t.dram["slots" + tag].rearrange("(s p) r -> p s r", p=P),
                             t.EMPTY.bitcast(I32).rearrange("p (o r) -> p o r", o=1).broadcast_to([P, SLOTS * TS // P, ROW // 2])).then_inc(emptied, 16)
            for i in range(NS, len(jobs)):
                load(i)
            sp.wait_ge(small, 96)
            sp.wait_ge(emptied, 32)

        @block.gpsimd
        def _(pool):
            def link(ins):
                link.n += 1
                ins.then_inc(pool_step, 1)
                pool.wait_ge(pool_step, link.n)
            link.n = 0
            nc.gpsimd.memset(t.EMPTY.bitcast(I32)[:, 0:ROW // 2 - 1], 0).then_inc(empty_row, 1)
            nc.gpsimd.memset(t.EMPTY.bitcast(I32)[:, ROW // 2 - 1:ROW // 2], 1 << 20).then_inc(empty_row, 1)
            link(nc.gpsimd.memset(t.MHALF[:, 0:NT], -0.5))
            nc.gpsimd.memset(t.ONES16, 1.0)
            link(nc.gpsimd.memset(t.BEFORE, 1.0))
            nc.gpsimd.affine_select(out=t.BEFORE, in_=t.BEFORE, compare_op=ALU.is_gt, fill=0.0, base=0,
                                    pattern=[[1, P]], channel_multiplier=-1).then_inc(fixed, 1)

            def root_x(g):
                m = rows_of(t.NRM, TPB * CB * g, TPB * CB * (g + 1))
                pool.wait_ge(x_var, g + 1)
                nc.gpsimd.tensor_tensor(m.rstd, m.vareps, t.MHALF[:, 0:TPB * CB], ALU.pow).then_inc(x_rstd, 1)

            pool.wait_ge(steps_ready, 1)
            for a in range(LF):
                ins = nc.gpsimd.tensor_scalar(SINB[:, a, :], TMP[:, 2, :], float(a), OFF[:, 2:3], ALU.mult, ALU.add)
            link(ins)
            root_x(0)
            link(nc.gpsimd.tensor_scalar(WHOLEB, SINB, ROUND, -ROUND, ALU.add, ALU.add))
            nc.gpsimd.tensor_tensor(SINB, SINB, WHOLEB, ALU.subtract).then_inc(phase_b_ready, 1)
            pool.wait_ge(mags, 1)
            pool.wait_ge(sines, 1)
            nc.gpsimd.tensor_tensor(SIN2, SIN2, MAG2, ALU.mult).then_inc(e2_ready, 1)
            for g in range(1, NCG):
                root_x(g)
            m = rows_of(t.NRM, NT, NT + 8 * NCG)

            def sums(g, k):
                pool.wait_ge(prod_ready, 2 * g + k + 1)
                if g >= 2:
                    pool.wait_ge(inv_mm, 2 * (g - 1))
                ys = YS[:, NFT * (g % 2) + k, :]
                yi = YS[:, NFT * (g % 2) + 2 + k, :]
                nc.gpsimd.tensor_tensor(ys, M4[k][:, 0, :], M4[k][:, 1, :], ALU.subtract)
                nc.gpsimd.tensor_tensor(yi, M4[k][:, 2, :], M4[k][:, 3, :], ALU.add).then_inc(ys_ready, 1)

            def root(g):
                s = slice(8 * g, 8 * g + 8)
                pool.wait_ge(r_var, g + 1)
                nc.gpsimd.tensor_tensor(m.rstd[:, s], m.vareps[:, s], t.MHALF[:, 0:8], ALU.pow).then_inc(r_rstd, 1)

            def finish(g):
                for tt in range(TPB if g < NCG - 1 else 1):
                    pool.wait_ge(scaled, 2 * g + tt + 1)
                    rn = RN[:, 2 * (g % 2) + tt, :].rearrange("p (b h) -> p b h", h=D)
                    res = t.RES[:, 2 * CB * g + tt:2 * CB * (g + 1):2, :]
                    link(nc.gpsimd.tensor_tensor(rn, rn, WLN[:, 1:2, :].broadcast_to([P, CB, D]), ALU.add))
                    nc.gpsimd.tensor_tensor(res, res, rn, ALU.add).then_inc(res_ready, 1)

            for g in range(NCG):
                sums(g, 0)
                sums(g, 1)
                if g >= 1:
                    root(g - 1)
                if g >= 2:
                    finish(g - 2)
            finish(NCG - 2)
            root(NCG - 1)
            finish(NCG - 1)

        @block.scalar
        def _(act):
            act.dma_start(t.RES[:, NT // 2:, :], t.dram["x"].rearrange("b (t p) d -> p (b t) d", p=P)[:, NT // 2:, :]).then_inc(x_in, 16)
            act.dma_start(t.ID, t.dram["ident"]).then_inc(dct_in, 16)
            act.dma_start(IV, t.dram["inv"].rearrange("t p f -> p t f")).then_inc(ln_in, 16)
            act.dma_start(WLN, t.dram["ln"].rearrange("k p h -> p k h")).then_inc(ln_in, 16)
            act.dma_start(DCOL, t.dram["dcol"]).then_inc(ln_in, 16)
            act.wait_ge(params_in, 32)
            nc.scalar.activation(PRM[:, DT, :], PRM[:, LDT, :], ACT.Exp)
            nc.scalar.activation(PRM[:, LAR, :], PRM[:, LAR, :], ACT.Exp).then_inc(exps, 1)
            act.wait_ge(decay_ready, 1)
            for b in range(LF):
                ins = nc.scalar.activation(MAG2[:, b, :], TMP[:, 0, :], ACT.Exp, scale=-float(b))
            ins.then_inc(mags, 1)
            for a in range(LF):
                ins = nc.scalar.activation(MAG1[:, a, :], TMP[:, 0, :], ACT.Exp, scale=-float(LF * a))
            ins.then_inc(mags, 1)
            act.wait_ge(phase_ready, 1)
            nc.scalar.activation(SIN2, SIN2, ACT.Sin, scale=TURN).then_inc(sines, 1)
            act.wait_ge(phase_ready, 2)
            nc.scalar.activation(TMP[:, 4:6, :], TMP[:, 4:6, :], ACT.Sin, scale=TURN).then_inc(sines, 1)
            act.wait_ge(phase_ready, 3)
            nc.scalar.activation(SINA, SINA, ACT.Sin, scale=TURN).then_inc(sines, 1)
            m = rows_of(t.NRM, 0, NT)

            def normalise(g):
                act.wait_ge(x_nmr, g + 1)
                for i in range(TPB * CB * g, TPB * CB * (g + 1)):
                    ins = nc.scalar.activation(XN[:, i, :], t.RES[:, i, :], ACT.Identity,
                                               bias=m.nmr[:, i:i + 1], scale=m.rstd[:, i:i + 1])
                ins.then_inc(xn_ready, 1)
            normalise(0)
            act.wait_ge(phase_b_ready, 1)
            nc.scalar.activation(SINB, SINB, ACT.Sin, scale=TURN).then_inc(sines, 1)
            act.wait_ge(dct_in, 48)
            nc.scalar.activation(t.ID16, t.ID, ACT.Copy)

            def split_high(portion):
                for i in portion:
                    act.wait_ge(job_in[i % NS], 16 * (i // NS + 1))
                    nc.scalar.activation(jobs[i][1], staged(i), ACT.Copy, scale=jobs[i][4]).then_inc(high, 1)
            split_high(portions[0])
            act.wait_ge(small, 96)
            nc.scalar.activation(t.B2, t.B2, ACT.Copy, scale=WS).then_inc(b2_scaled, 1)
            act.wait_ge(b2_scaled, 1)
            nc.scalar.activation(t.B2P, t.B2, ACT.Copy).then_inc(b2_high, 1)
            for q in range(4):
                act.wait_ge(kdig_mm, q + 1)
                nc.scalar.activation(KDIG[0:LF, :, 32 * q:32 * q + 32],
                                     ps[4 + q][0:LF, :].rearrange("a (h b) -> a b h", b=LF),
                                     ACT.Copy, scale=2.0).then_inc(kdig_sb, 1)
            normalise(1)
            act.wait_ge(klag_mm, 1)
            nc.scalar.activation(KLAG, ps[5][:, 0:SEQ].rearrange("p (t h) -> p t h", h=D), ACT.Copy).then_inc(klag_sb, 1)
            for g in range(2, NCG):
                normalise(g)
            m = rows_of(t.NRM, NT, NT + 8 * NCG)
            for g in range(NCG):
                split_high(portions[g + 1])
                act.wait_ge(r_nmr, g + 1)
                for tt in range(TPB):
                    if g >= 2:
                        act.wait_ge(res_ready, 2 * (g - 2) + tt + 1)
                    for b in range(CB):
                        j = 8 * g + 4 * tt + b
                        ins = nc.scalar.activation(RN[:, 2 * (g % 2) + tt, D * b:D * b + D],
                                                   ps[6 - 2 * (g % 2) + tt][:, D * b:D * b + D], ACT.Identity,
                                                   bias=m.nmr[:, j:j + 1], scale=m.rstd[:, j:j + 1])
                    ins.then_inc(rn_ready, 1)

        @block.tensor
        def _(pe):
            def forward(g, k):
                n = 2 * g + k
                if n >= 2:
                    pe.wait_ge(prod_ready, n - 1)
                for i, ft in enumerate((k, 2 + k)):
                    for st in range(TPB):
                        ins = pe.matmul(ps[2 * (n % 2) + i], FW[:, st, P * ft:P * ft + P],
                                        XN[:, 2 * CB * g + st:2 * CB * (g + 1):2, :], start=(st == 0), stop=(st == TPB - 1))
                ins.then_inc(fwd_mm, 1)

            def inverse(g):
                pe.wait_ge(ys_ready, 2 * g + 2)
                for tt in range(TPB):
                    if g >= 2:
                        pe.wait_ge(rn_ready, 2 * (g - 2) + tt + 1)
                    for ft in range(NFT):
                        ins = pe.matmul(ps[6 - 2 * (g % 2) + tt], IV[:, ft, P * tt:P * tt + P], YS[:, NFT * (g % 2) + ft, :],
                                        start=(ft == 0), stop=(ft == NFT - 1))
                    ins.then_inc(inv_mm, 1)

            pe.wait_ge(dct_in, 48)
            pe.wait_ge(xn_ready, 1)
            forward(0, 0)
            forward(0, 1)
            pe.wait_ge(e2_ready, 1)
            pe.wait_ge(e1_ready, 1)
            for h in range(D):
                ins = pe.matmul(ps[4 + h // 32][0:LF, LF * (h % 32):LF * (h % 32) + LF], SINA[:, :, h], SIN2[:, :, h],
                                start=True, stop=True)
                if h % 32 == 31:
                    ins.then_inc(kdig_mm, 1)
            pe.wait_ge(kdig_sb, 4)
            for b in range(LF):
                ins = pe.transpose(ps[4][:, LF * b:LF * b + LF], KDIG[0:LF, b, :], t.ID[0:LF, 0:LF])
            ins.then_inc(kch_mm, 1)
            pe.wait_ge(kch_sb, 1)
            for i in range(TPB):
                ins = pe.transpose(ps[5][:, D * i:D * i + D], KCH[:, P * i:P * i + P], t.ID)
            ins.then_inc(klag_mm, 1)
            pe.wait_ge(klag_sb, 1)
            for ft in range(NFT):
                for st in range(TPB):
                    ins = pe.matmul(ps[4][:, D * ft:D * ft + D], FW[:, st, P * ft:P * ft + P], KLAG[:, st, :],
                                    start=(st == 0), stop=(st == TPB - 1))
            ins.then_inc(kf_mm, 1)
            for g in range(NCG):
                if g >= 1:
                    pe.wait_ge(xn_ready, g + 1)
                    for k in range(2):
                        forward(g, k)
                if g >= 1:
                    inverse(g - 1)
            inverse(NCG - 1)

        @block.vector
        def _(dve):
            def link(ins):
                link.n += 1
                ins.then_inc(dve_step, 1)
                dve.wait_ge(dve_step, link.n)
            link.n = 0
            tt_, ts, stt = dve.tensor_tensor, dve.tensor_scalar, dve.scalar_tensor_tensor

            def turn_rest(phase, whole):
                link(ts(whole, phase, ROUND, -ROUND, ALU.add, ALU.add))
                return tt_(phase, phase, whole, ALU.subtract)

            def x_statistics(g):
                tiles = slice(TPB * CB * g, TPB * CB * (g + 1))
                for i in range(tiles.start, tiles.stop):
                    ins = dve.bn_stats(t.STATS[:, i, :], t.RES[:, i, :])
                link(ins)
                norm_statistics(dve, link, t.STATS[:, tiles, :], rows_of(t.NRM, tiles.start, tiles.stop)).then_inc(x_var, 1)

            def x_offsets(g):
                m = rows_of(t.NRM, TPB * CB * g, TPB * CB * (g + 1))
                dve.wait_ge(x_rstd, g + 1)
                stt(m.nmr, m.mean, -1.0, m.rstd, ALU.mult, ALU.mult).then_inc(x_nmr, 1)

            EA, DTC = PRM[:, LAR, :], PRM[:, DT, :]
            AR, R1, R16, SN = (TMP[:, i, :] for i in (0, 1, 2, 4))
            CS = TMP[:, 5, :]
            dve.wait_ge(exps, 1)
            tt_(AR, EA, DTC, ALU.mult).then_inc(decay_ready, 1)
            link(tt_(R1, PRM[:, AIM, :], DTC, ALU.mult))
            link(ts(R16, R1, float(LF), None, ALU.mult))
            steps, whole = TMP[:, 1:3, :], TMP[:, 6:8, :]
            link(ts(whole, steps, 1.0 / (2 * np.pi), ROUND, ALU.mult, ALU.add))
            link(ts(whole, whole, -ROUND, None, ALU.add))
            link(stt(steps, whole, -TWO_PI_HI, steps, ALU.mult, ALU.add))
            link(stt(steps, whole, -TWO_PI_LO, steps, ALU.mult, ALU.add))
            ts(steps, steps, 1.0 / (2 * np.pi), None, ALU.mult).then_inc(steps_ready, 1)
            dve.wait_ge(steps_ready, 1)
            for b in range(LF):
                ins = ts(SIN2[:, b, :], R1, float(b), OFF[:, 0:1], ALU.mult, ALU.add)
            link(ins)
            turn_rest(SIN2, KQ).then_inc(phase_ready, 1)
            dve.wait_ge(x_in, 32)
            x_statistics(0)
            ts(SN, R1, 1.0, None, ALU.mult)
            link(ts(CS, R1, 0.25, None, ALU.add))
            turn_rest(TMP[:, 4:6, :], TMP[:, 6:8, :]).then_inc(phase_ready, 1)
            for a in range(LF):
                ins = ts(SINA[:, a, :], R16, float(a), OFF[:, 1:2], ALU.mult, ALU.add)
            link(ins)
            turn_rest(SINA, PHR).then_inc(phase_ready, 1)
            x_offsets(0)
            ER, EI, T0, T1, NR, NI, INV, CTR, CTI, SQ = (TMP[:, i, :] for i in range(8, 18))
            CRE, CIM, AIMC = PRM[:, C_RE, :], PRM[:, C_IM, :], PRM[:, AIM, :]
            dve.wait_ge(mags, 1)
            dve.wait_ge(sines, 2)
            EXD = MAG2[:, 1, :]
            tt_(EI, EXD, SN, ALU.mult)
            tt_(SQ, AIMC, AIMC, ALU.mult)
            link(tt_(ER, EXD, CS, ALU.mult))
            tt_(T1, EA, EA, ALU.mult)
            link(ts(ER, ER, -1.0, None, ALU.add))
            link(tt_(SQ, SQ, T1, ALU.add))
            dve.reciprocal(INV, SQ)
            tt_(NR, CRE, ER, ALU.mult)
            tt_(T0, CIM, EI, ALU.mult)
            tt_(NI, CRE, EI, ALU.mult)
            link(tt_(T1, CIM, ER, ALU.mult))
            tt_(NR, NR, T0, ALU.subtract)
            link(tt_(NI, NI, T1, ALU.add))
            tt_(T0, NI, AIMC, ALU.mult)
            tt_(T1, NR, EA, ALU.mult)
            tt_(CTI, NR, AIMC, ALU.mult)
            link(tt_(ER, NI, EA, ALU.mult))
            tt_(CTR, T0, T1, ALU.subtract)
            link(stt(CTI, CTI, -1.0, ER, ALU.mult, ALU.subtract))
            tt_(CTR, CTR, INV, ALU.mult)
            link(tt_(CTI, CTI, INV, ALU.mult))
            dve.wait_ge(sines, 3)
            dve.wait_ge(mags, 2)
            link(tt_(SINA, SINA, MAG1, ALU.mult))
            tt_(SINA, SINA, CTR.rearrange("p (o h) -> p o h", o=1).broadcast_to([P, LF, D]), ALU.mult)
            dve.wait_ge(sines, 4)
            link(tt_(SINB, SINB, MAG1, ALU.mult))
            link(tt_(SINB, SINB, CTI.rearrange("p (o h) -> p o h", o=1).broadcast_to([P, LF, D]), ALU.mult))
            tt_(SINA, SINA, SINB, ALU.add).then_inc(e1_ready, 1)

            def split_low(portion):
                for i in portion:
                    dve.wait_ge(high, i + 1)
                    stt(jobs[i][2], staged(i), jobs[i][4], jobs[i][1], ALU.mult, ALU.subtract).then_inc(low, 1)
            x_statistics(1)
            x_statistics(2)
            x_offsets(1)
            split_low(portions[0][0:4])

            dve.wait_ge(kch_mm, 1)
            dve.wait_ge(ln_in, 48)
            link(dve.tensor_copy(KCH.rearrange("p (a b) -> p b a", b=LF), ps[4][:, 0:SEQ].rearrange("p (b a) -> p b a", a=LF)))
            ts(KCH[:, 0:1], KCH[:, 0:1], DCOL, 1.0, ALU.add, ALU.add).then_inc(kch_sb, 1)
            x_statistics(3)
            x_offsets(2)
            x_offsets(3)
            dve.wait_ge(kf_mm, 1)
            kf = ps[4].rearrange("p (f h) -> p f h", h=D)
            FA, FB, FD = SPK[:, 0], SPK[:, 1], SPK[:, 2]
            dve.tensor_copy(FA, kf[:, 0:2, :])
            dve.tensor_copy(FD[:, 1, :], kf[:, 1, :])
            dve.tensor_copy(FB[:, 1, :], kf[:, 3, :])
            ts(FB[:, 0, :], kf[:, 2, :], KEEP[:, 0:1], None, ALU.mult)
            link(ts(SPK[:, 3, 0, :], kf[:, 2, :], KEEP[:, 1:2], None, ALU.mult))
            link(stt(FD[:, 0, :], kf[:, 0, :], KEEP[:, 0:1], SPK[:, 3, 0, :], ALU.mult, ALU.add))

            def wide(f):
                return f.rearrange("p (o h) -> p o h", o=1).broadcast_to([P, CB, D])

            def products(g, k):
                n = 2 * g + k
                dve.wait_ge(fwd_mm, n + 1)
                if n >= 2:
                    dve.wait_ge(ys_ready, n - 1)
                re = ps[2 * (n % 2)].rearrange("p (b h) -> p b h", h=D)
                im = ps[2 * (n % 2) + 1].rearrange("p (b h) -> p b h", h=D)
                out = M4[k].rearrange("p k (b h) -> p k b h", h=D)
                tt_(out[:, 0], re, wide(FA[:, k, :]), ALU.mult)
                tt_(out[:, 1], im, wide(FB[:, k, :]), ALU.mult)
                tt_(out[:, 2], re, wide(FB[:, k, :]), ALU.mult)
                tt_(out[:, 3], im, wide(FD[:, k, :]), ALU.mult).then_inc(prod_ready, 1)

            def statistics(g):
                for tt in range(TPB):
                    dve.wait_ge(inv_mm, 2 * g + tt + 1)
                    for b in range(CB):
                        ins = dve.bn_stats(t.STATS[:, 4 * tt + b, :], ps[6 - 2 * (g % 2) + tt][:, D * b:D * b + D])
                link(ins)
                mg = rows_of(t.NRM, NT + 8 * g, NT + 8 * g + 8)
                norm_statistics(dve, link, t.STATS[:, 0:8, :], mg).then_inc(r_var, 1)
                dve.wait_ge(r_rstd, g + 1)
                stt(mg.nmr, mg.mean, -1.0, mg.rstd, ALU.mult, ALU.mult).then_inc(r_nmr, 1)

            def scale(g):
                for tt in range(TPB):
                    dve.wait_ge(rn_ready, 2 * g + tt + 1)
                    rn = RN[:, 2 * (g % 2) + tt, :].rearrange("p (b h) -> p b h", h=D)
                    tt_(rn, rn, WLN[:, 0:1, :].broadcast_to([P, CB, D]), ALU.mult).then_inc(scaled, 1)

            def residual_statistics(g):
                dve.wait_ge(res_ready, 2 * g + 2 if g < NCG - 1 else 2 * g + 1)
                for i in range(TPB * CB * g, TPB * CB * (g + 1)):
                    dve.bn_stats(t.RSTATS[:, i, :], t.RES[:, i, :])

            for g in range(NCG):
                for k in range(2):
                    products(g, k)
                if g == 0:
                    split_low(portions[0][4:])
                    dve.wait_ge(b2_high, 1)
                    stt(t.B2P, t.B2P, t.LOW[0:2, 2:3], t.B2, ALU.mult, ALU.add)
                if g >= 2:
                    scale(g - 2)
                if g >= 1:
                    statistics(g - 1)
                if g >= 1:
                    split_low(portions[g])
                if g >= 3:
                    residual_statistics(g - 3)
            scale(NCG - 2)
            split_low(portions[NCG])
            statistics(NCG - 1)
            residual_statistics(NCG - 3)
            residual_statistics(NCG - 2)
            scale(NCG - 1)
            rn = RN[:, 2 * ((NCG - 1) % 2) + 1, :].rearrange("p (b h) -> p b h", h=D)
            res = t.RES[:, 2 * CB * (NCG - 1) + 1:2 * CB * NCG:2, :]
            dve.wait_ge(scaled, 2 * NCG)
            link(tt_(rn, rn, WLN[:, 1:2, :].broadcast_to([P, CB, D]), ALU.add))
            link(tt_(res, res, rn, ALU.add))
            residual_statistics(NCG - 1)

CHUNK = 2 * GT


def norm_program(nc, t, sem):
    dve_step, var, rstd, nmr = sem("n_dve_step"), sem("n_var"), sem("n_rstd"), sem("n_nmr")
    xn, turned, high, low = [sem("n_xn_act"), sem("n_xn_dve")], sem("n_turned"), sem("n_high"), sem("n_low")
    m = rows_of(t.NRM, 0, NT)
    part = Bag()
    part.low = low

    def tiles(c):
        return slice(CHUNK * c, CHUNK * c + CHUNK)

    def gpsimd(pool):
        pool.wait_ge(var, 1)
        for c in range(NT // CHUNK):
            s = tiles(c)
            nc.gpsimd.tensor_tensor(m.rstd[:, s], m.vareps[:, s], t.MHALF[:, s], ALU.pow).then_inc(rstd, 1)

    def tensor(pe):
        for g in range(NG):
            c = g // 2
            pe.wait_ge(xn[c % 2], 2 * (c // 2) + g % 2 + 1)
            if g >= 4:
                pe.wait_ge(low, g - 3)
            for j in range(GT):
                ins = pe.transpose(t.psum[g % 4][:, P * j:P * j + P], t.XN[:, GT * g + j, :], t.ID)
            ins.then_inc(turned, 1)

    def scalar(act):
        done = 0
        for c in range(0, NT // CHUNK, 2):
            act.wait_ge(nmr, c + 1)
            for i in range(CHUNK * c, CHUNK * c + CHUNK):
                ins = nc.scalar.activation(t.XN[:, i, :], t.RES[:, i, :], ACT.Identity,
                                           bias=m.nmr[:, i:i + 1], scale=m.rstd[:, i:i + 1])
                if i % GT == GT - 1:
                    ins.then_inc(xn[0], 1)
            for g in range(done, 2 if c == 0 else NG):
                act.wait_ge(turned, g + 1)
                nc.scalar.activation(t.XTH[:, BANK * g:BANK * (g + 1)], t.psum[g % 4], ACT.Copy).then_inc(high, 1)
            done = 2

    def vector(dve):
        def link(ins):
            link.n += 1
            ins.then_inc(dve_step, 1)
            dve.wait_ge(dve_step, link.n)
        link.n = 0
        norm_statistics(dve, link, t.RSTATS, m).then_inc(var, 1)
        for c in range(NT // CHUNK):
            s = tiles(c)
            dve.wait_ge(rstd, c + 1)
            dve.scalar_tensor_tensor(m.nmr[:, s], m.mean[:, s], -1.0, m.rstd[:, s], ALU.mult, ALU.mult).then_inc(nmr, 1)
            if c % 2 == 1:
                for i in range(CHUNK * c, CHUNK * c + CHUNK):
                    ins = dve.tensor_scalar(t.XN[:, i, :], t.RES[:, i, :], m.mean[:, i:i + 1], m.rstd[:, i:i + 1],
                                            ALU.subtract, ALU.mult)
                    if i % GT == GT - 1:
                        ins.then_inc(xn[1], 1)
        for g in range(NG):
            dve.wait_ge(high, g + 1)
            s = slice(BANK * g, BANK * (g + 1))
            dve.tensor_tensor(t.XTL[:, s], t.psum[g % 4], t.XTH[:, s], ALU.subtract).then_inc(low, 1)
    part.gpsimd, part.tensor, part.scalar, part.vector = gpsimd, tensor, scalar, vector
    return part


def shared_stage(nc, t, tag):
    with ExitStack() as ctx:
        sem = stage_semaphores(nc, ctx, f"x{tag}_")
        norm = norm_program(nc, t, sem)
        up_mm, hidden, split, down_mm, merged, high, primed = (sem(n) for n in (
            "up_mm", "hidden", "split", "down_mm", "merged", "high", "primed"))
        dve_step, gate_mm, gap, ratio, chosen_set, ranked, row_high, row_low, iotas, placed = (sem(n) for n in (
            "dve_step", "gate_mm", "gap", "ratio", "chosen_set", "ranked", "row_high", "row_low", "iotas", "placed"))
        sent, second = [sem(f"sent{i}") for i in range(2)], sem("second")
        HF = t.arena[:, 0:2 * MT * BANK].rearrange("p (s m n) -> p s m n", m=MT, n=BANK)
        H16 = t.arena[:, 2 * MT * BANK:4 * MT * BANK].bitcast(F16).rearrange("p (s k m n) -> p s k m n", s=2, k=2, m=MT)
        e = NE
        BIAS = t.B1[:, e, :]
        ROWI = t.ROWS.bitcast(I32)
        n = NT * NE
        at = t.arena[:, 4 * MT * BANK:]
        L, EQ, V, O1, O2 = (at[:, i * n:(i + 1) * n].rearrange("p (t e) -> p t e", e=NE) for i in range(5))
        INC, POS, TEMP = (at[:, i * n:(i + 1) * n].rearrange("p (e t) -> p e t", t=NT) for i in range(5, 8))
        ONE = at[:, 8 * n:9 * n]
        CHOSEN = at[:, 9 * n:9 * n + n // 2].bitcast(F16).rearrange("p (e t) -> p e t", t=NT)
        S = at[:, 10 * n:10 * n + 8 * NT].rearrange("p (k t) -> p k t", t=NT)
        M1, M2, MV, GAP, DEN, PK = (S[:, i, :] for i in range(6))
        E8 = at[:, 11 * n:11 * n + 8 * NE].rearrange("p (k e) -> p k e", e=NE)
        LASTS, COUNT, TILES, UPTO, SHIFT = (E8[:, i, :] for i in range(5))
        CMP = at[0:1, 12 * n:12 * n + SLOTS * NE].rearrange("p (s e) -> p s e", e=NE)
        EIDF = at[0:1, 12 * n + SLOTS * NE:12 * n + SLOTS * (NE + 1)]
        block = ctx.enter_context(nc.Block())

        def wide(v):
            return v.rearrange("p (t o) -> p t o", o=1).broadcast_to([P, NT, NE])

        HALVES = [slice(NT // 2 * h, NT // 2 * (h + 1)) for h in range(2)]

        @block.gpsimd
        def _(pool):
            norm.gpsimd(pool)
            nc.gpsimd.iota(ROWI[:, :, ROW // 2 - 1], pattern=[[P, NT]], base=0, channel_multiplier=1).then_inc(iotas, 1)
            for h, s in enumerate(HALVES):
                pool.wait_ge(row_high, h + 1)
                nc.gpsimd.tensor_tensor(t.ROWS[:, s, D:2 * D], t.XN[:, s, :], t.ROWS[:, s, 0:D], ALU.subtract).then_inc(row_low, 1)
            pool.wait_ge(iotas, 1)
            pool.wait_ge(row_low, 2)
            xs = t.dram["slots" + tag]
            for k in range(2):
                pool.wait_ge(placed, k + 1)
                for h, s in enumerate(HALVES):
                    if k == 1:
                        pool.wait_ge(sent[h], 16 * NT // 2)
                        nc.gpsimd.iota(ROWI[:, s, ROW // 2 - 1], pattern=[[P, NT // 2]], base=NT * P + NT // 2 * P * h,
                                       channel_multiplier=1).then_inc(second, 1)
                        pool.wait_ge(second, h + 1)
                    for i in range(NT // 2 * h, NT // 2 * (h + 1)):
                        nc.gpsimd.indirect_dma_start(xs, bass.IndirectOffsetOnAxis(ap=t.PLACE[:, k, i:i + 1], axis=0),
                                                     ROWI[:, i, :], None).then_inc(sent[h], 16)
            for h in range(2):
                pool.wait_ge(sent[h], 16 * NT)

        @block.tensor
        def _(pe):
            norm.tensor(pe)
            for i in range(NT):
                if i % GT == 0:
                    pe.wait_ge(norm.low, i // GT + 1)
                for k, (x, w) in enumerate(((t.XTH, t.GWH), (t.XTL, t.GWH), (t.XTH, t.GWL))):
                    ins = pe.matmul(t.psum[6][:, NE * i:NE * i + NE], x[:, P * i:P * i + P], w, start=(k == 0), stop=(k == 2))
            ins.then_inc(gate_mm, 1)
            pe.wait_ge(chosen_set, 1)
            pe.matmul(t.psum[6][:, 0:n], t.BEFORE, CHOSEN.rearrange("p e t -> p (e t)"), start=True, stop=True)
            pe.matmul(t.psum[7][:, 0:n], t.ONES16, CHOSEN.rearrange("p e t -> p (e t)"), start=True, stop=True).then_inc(ranked, 1)

            def up(g):
                for m in range(MT):
                    pe.wait_ge(hidden, MT * g + m + 1)
                    ms, xs = slice(P * m, P * m + P), slice(BANK * g, BANK * (g + 1))
                    pe.matmul(t.psum[m], t.W1H[:, e, ms], t.XTH[:, xs], start=True, stop=False)
                    pe.matmul(t.psum[m], t.W1H[:, e, ms], t.XTL[:, xs], start=False, stop=False)
                    pe.matmul(t.psum[m], t.W1L[:, e, ms], t.XTH[:, xs], start=False, stop=True).then_inc(up_mm, 1)

            def down(g):
                pe.wait_ge(split, g + 3)
                pe.wait_ge(merged, g + 1)
                for j in range(GT):
                    out = t.psum[4 + g % 2][:, D * j:D * j + D]
                    pe.matmul(out, t.ONES16[0:2, :], t.B2P[0:2, e, :], start=True, stop=False)
                    for m in range(MT):
                        js = slice(P * j, P * j + P)
                        hh, hl = H16[:, g % 2, 0, m, js], H16[:, g % 2, 1, m, js]
                        pe.matmul(out, hh, t.W2H[:, e, m, :], start=False, stop=False)
                        pe.matmul(out, hh, t.W2L[:, e, m, :], start=False, stop=False)
                        ins = pe.matmul(out, hl, t.W2H[:, e, m, :], start=False, stop=(m == MT - 1))
                ins.then_inc(down_mm, 1)

            for g in range(NG):
                up(g)
                if g >= 1:
                    down(g - 1)
            down(NG - 1)

        @block.scalar
        def _(act):
            norm.scalar(act)
            for s in HALVES:
                nc.scalar.activation(t.ROWS[:, s, 0:D], t.XN[:, s, :], ACT.Copy).then_inc(row_high, 1)
            act.wait_ge(gap, 1)
            nc.scalar.activation(GAP, GAP, ACT.Exp).then_inc(ratio, 1)
            nc.scalar.activation(HF[0:1, 0, 0, 0:1], t.MHALF[0:1, 0:1], ACT.Gelu).then_inc(primed, 1)
            act.wait_ge(primed, 1)
            act.sem_inc(hidden, MT)
            for g in range(NG):
                act.wait_ge(split, g + 1)
                for m in range(MT):
                    act.wait_ge(up_mm, MT * g + m + 1)
                    nc.scalar.activation(HF[:, g % 2, m, :], t.psum[m], ACT.Gelu,
                                         bias=BIAS[:, m:m + 1], scale=1.0 / WS).then_inc(hidden, 1)

        @block.vector
        def _(dve):
            norm.vector(dve)

            def link(ins):
                link.n += 1
                ins.then_inc(dve_step, 1)
                dve.wait_ge(dve_step, link.n)
            link.n = 0
            tt, ts, stt = dve.tensor_tensor, dve.tensor_scalar, dve.scalar_tensor_tensor
            rank = t.GB[:, 1:2, :].broadcast_to([P, NT, NE])

            def first_of_largest(out, logits, largest):
                link(dve.tensor_reduce(largest, logits, AX.X, ALU.max))
                link(tt(EQ, logits, wide(largest), ALU.is_equal))
                link(tt(V, EQ, rank, ALU.mult))
                link(dve.tensor_reduce(MV, V, AX.X, ALU.max))
                link(tt(out, V, wide(MV), ALU.is_equal))

            dve.sem_inc(split, 2)
            dve.sem_inc(down_mm, 2)
            dve.sem_inc(merged, 2)
            dve.memset(ONE, 1.0)
            dve.memset(t.EID, 0)
            dve.wait_ge(gate_mm, 1)
            link(stt(L, t.psum[6][:, 0:n].rearrange("p (t e) -> p t e", e=NE), 1.0 / WS,
                     t.GB[:, 0:1, :].broadcast_to([P, NT, NE]), ALU.mult, ALU.add))
            first_of_largest(O1, L, M1)
            link(stt(L, O1, LOWEST, L, ALU.mult, ALU.add))
            first_of_largest(O2, L, M2)
            tt(CHOSEN.rearrange("p e t -> p t e"), O1, O2, ALU.add).then_inc(chosen_set, 1)
            tt(GAP, M2, M1, ALU.subtract).then_inc(gap, 1)
            dve.wait_ge(ranked, 1)
            before, totals = (t.psum[i][:, 0:n] for i in (6, 7))
            inc = INC.rearrange("p e t -> p (e t)")
            link(dve.tensor_tensor_scan(inc, ONE, totals, 0.0, ALU.mult, ALU.add))
            link(tt(TEMP.rearrange("p e t -> p (e t)"), inc, totals, ALU.subtract))
            tt(POS.rearrange("p e t -> p (e t)"), TEMP.rearrange("p e t -> p (e t)"), before, ALU.add)
            link(dve.tensor_copy(LASTS, INC[:, :, NT - 1]))
            dve.tensor_copy(COUNT[:, 0:1], LASTS[:, 0:1])
            link(tt(COUNT[:, 1:NE], LASTS[:, 1:NE], LASTS[:, 0:NE - 1], ALU.subtract))
            link(ts(TILES, COUNT, TS - 1.0, 1.0 / TS, ALU.add, ALU.mult))
            link(ts(TILES, TILES, -(TS - 1.0) / (2 * TS), ROUND, ALU.add, ALU.add))
            link(ts(TILES, TILES, -ROUND, None, ALU.add))
            link(dve.tensor_tensor_scan(UPTO, ONE[:, 0:NE], TILES, 0.0, ALU.mult, ALU.add))
            tt(SHIFT, UPTO, TILES, ALU.subtract)
            link(tt(LASTS, LASTS, COUNT, ALU.subtract))
            link(stt(SHIFT, SHIFT, float(TS), LASTS, ALU.mult, ALU.subtract))
            link(tt(POS, POS, SHIFT.rearrange("p (e o) -> p e o", o=1).broadcast_to([P, NE, NT]), ALU.add))
            for k, chosen in enumerate((O1, O2)):
                link(tt(V, chosen, POS.rearrange("p e t -> p t e"), ALU.mult))
                link(dve.tensor_reduce(PK, V, AX.X, ALU.add))
                dve.tensor_copy(t.PLACE[:, k, :], PK).then_inc(placed, 1)
                dve.wait_ge(placed, k + 1)
            link(tt(CMP, t.SLOTNO.rearrange("p (s o) -> p s o", o=1).broadcast_to([1, SLOTS, NE]),
                    UPTO[0:1].rearrange("p (o e) -> p o e", o=1).broadcast_to([1, SLOTS, NE]), ALU.is_ge))
            link(dve.tensor_reduce(EIDF, CMP, AX.X, ALU.add))
            link(ts(EIDF, EIDF, NE - 1.0, None, ALU.min))
            flat = t.EID.rearrange("p k r u -> p k (r u)")
            dve.tensor_copy(flat[:, 0, 0:SLOTS], EIDF)
            dve.tensor_copy(flat[:, 1, 2:SLOTS], EIDF[:, 0:SLOTS - 2])
            dve.tensor_copy(flat[:, 2, 0:SLOTS - 2], EIDF[:, 2:SLOTS])
            dve.wait_ge(ratio, 1)
            link(ts(DEN, GAP, 1.0, None, ALU.add))
            link(dve.reciprocal(M1, DEN))
            link(tt(M2, GAP, M1, ALU.mult))
            ts(t.WEIGHT[:, 0, :], M1, 1.0 / WS, None, ALU.mult)
            ts(t.WEIGHT[:, 1, :], M2, 1.0 / WS, None, ALU.mult)

            def split_step(g):
                dve.wait_ge(down_mm, g + 1)
                dve.wait_ge(hidden, MT * g + 2 * MT)
                dve.tensor_copy(H16[:, g % 2, 0], HF[:, g % 2]).then_inc(high, 1)
                dve.wait_ge(high, g + 1)
                dve.tensor_tensor(H16[:, g % 2, 1], HF[:, g % 2], H16[:, g % 2, 0], ALU.subtract).then_inc(split, 1)

            def merge_step(g):
                dve.wait_ge(down_mm, g + 3)
                res = t.RES[:, GT * g:GT * g + GT, :]
                stt(res, t.psum[4 + g % 2].rearrange("p (j d) -> p j d", d=D), 1.0 / WS, res, ALU.mult, ALU.add).then_inc(merged, 1)

            for g in range(NG):
                split_step(g)
                if g >= 1:
                    merge_step(g - 1)
            merge_step(NG - 1)


def routed_stage(nc, t, tag, store=None):
    with ExitStack() as ctx:
        sem = stage_semaphores(nc, ctx, f"s{tag}_")
        at = [0]

        def carve(dt, *shape):
            n = int(np.prod(shape))
            words = n if dt == F32 else n // 2
            v = t.arena[:, at[0]:at[0] + words]
            at[0] += words
            v = v if dt == F32 else v.bitcast(dt)
            names = "abcde"[:len(shape)]
            if len(shape) > 1:
                v = v.rearrange(f"p ({' '.join(names)}) -> p {' '.join(names)}", **dict(zip(names, shape)))
            return v

        NHALF = TS // P
        CT = 8
        SLOT = [carve(F16, NHALF, ROW) for _ in range(UN)]
        XST = [carve(F16, 2, TS) for _ in range(2)]
        HF = [carve(F32, MT, TS) for _ in range(2)]
        H16 = [carve(F16, 2, MT, TS) for _ in range(4)]
        Y = [carve(F32, NHALF, D) for _ in range(4)]
        BIAS = [carve(F32, MT) for _ in range(4)]
        BACK = [carve(F32, 2, CT, D) for _ in range(NT // CT)]
        xs, yo = t.dram["slots" + tag], t.dram["expert_out" + tag]
        slot_in, y_out = [sem(f"slot_in{i}") for i in range(UN)], [sem(f"y_out{i}") for i in range(4)]
        turned, xt_set, up_mm, hidden, high, split, down_mm, y_set = (sem(n) for n in (
            "turned", "xt_set", "up_mm", "hidden", "high", "split", "down_mm", "y_set"))
        back_in, back_added, first_added, primed, gated, stored = (
            [sem(f"back_in{i}") for i in range(NT // CT)], sem("back_added"), sem("first_added"), sem("primed"), sem("gated"), sem("stored"))
        ps = t.psum
        UP = [t.psum_all[:, 2 + 2 * i:4 + 2 * i, :].rearrange("p b (m n) -> p (b m) n", n=TS) for i in range(2)]
        bias_set, second_weighted = sem("bias_set"), sem("second_weighted")
        block = ctx.enter_context(nc.Block())

        def after(eng, s, n):
            if not (isinstance(n, int) and n <= 0):
                eng.wait_ge(s, n)

        def rounds(eng, body):
            body(0, True, False)
            with eng.Fori(1, ROUNDS - 1) as k:
                body(k, False, False)
            body(ROUNDS - 1, False, True)

        def tiles_of(last):
            return SLOTS - UN * (ROUNDS - 1) if last else UN

        def written(k, i):
            return k * (16 * NHALF * UN // 4) + 16 * NHALF * (i // 4 + 1)

        names = [0]

        def expert_values(eng, k, table):
            names[0] += 1
            regs = [eng.alloc_register(f"{tag}_experts{names[0]}_{i}") for i in range(UN)]
            eng.load(regs, t.EID[0:1, table, k, :])
            return [eng.snap(r, min_val=0, max_val=NE - 1) for r in regs]

        @block.sync
        def _(sp):
            tiles = xs.rearrange("(s h p) r -> s p h r", p=P, h=NHALF)

            def body(k, first, last):
                for i in range(tiles_of(last)):
                    after(sp, y_out[i % 4], written(k, i) - 16 * NHALF * (UN // 4))
                    sp.dma_start(SLOT[i].bitcast(I32), tiles[k * UN + i]).then_inc(slot_in[i], 16)
            rounds(sp, body)
            for i in range(4):
                sp.wait_ge(y_out[i], 16 * NHALF * -(-(SLOTS - i) // 4))
            rows = yo.rearrange("(k t p) d -> p k t d", k=2, p=P)

            for c in range(NT // CT):
                for k in range(2):
                    sp.dma_start(BACK[c][:, k], rows[:, k, CT * c:CT * c + CT]).then_inc(back_in[c], 16)
            if store is not None:
                for c in range(NT // CT):
                    sp.wait_ge(back_added, c + 1)
                    sp.dma_start(store[:, CT * c:CT * c + CT, :], t.RES[:, CT * c:CT * c + CT, :]).then_inc(stored, 16)
            if store is not None:
                sp.wait_ge(stored, 16 * NT // CT)

        @block.gpsimd
        def _(pool):
            def body(k, first, last):
                for i in range(tiles_of(last)):
                    after(pool, gated, k * UN + i)
                    after(pool, y_set, k * UN + i + 1)
                    nc.gpsimd.tensor_tensor(t.GATE[:, 0:1], t.MHALF[:, 0:1], t.MHALF[:, 0:1], ALU.add).then_inc(gated, 1)
                    for h in range(NHALF):
                        target = SLOT[i].bitcast(I32)[:, h, ROW // 2 - 1:ROW // 2]
                        nc.gpsimd.indirect_dma_start(yo, bass.IndirectOffsetOnAxis(ap=target, axis=0), Y[i % 4][:, h], None,
                                                     bounds_check=2 * NT * P - 1, oob_is_err=False).then_inc(y_out[i % 4], 16)
            rounds(pool, body)
            for c in range(NT // CT) if store is None else ():
                pool.wait_ge(first_added, c + 1)
                pool.wait_ge(second_weighted, c + 1)
                res = t.RES[:, CT * c:CT * c + CT, :]
                nc.gpsimd.tensor_tensor(res, res, BACK[c][:, 1], ALU.add).then_inc(back_added, 1)

        @block.tensor
        def _(pe):
            def turn(k, i):
                n = k * UN + i
                after(pe, slot_in[i], 16 * k + 16)
                after(pe, xt_set, n - 1)
                for part in range(2):
                    for h in range(NHALF):
                        at = TS * part + P * h
                        ins = pe.transpose(ps[i % 2].bitcast(F16)[:, at:at + P],
                                           SLOT[i][:, h, P * part:P * part + P], t.ID16)
                ins.then_inc(turned, 1)

            def up(k, i, e):
                n = k * UN + i
                after(pe, xt_set, n + 1)
                after(pe, hidden, n - 1)
                for m in range(MT):
                    out, ms = UP[i % 2][:, m, :], slice(P * m, P * m + P)
                    pe.matmul(out, t.W1H[:, e, ms], XST[i % 2][:, 0], start=True, stop=False)
                    pe.matmul(out, t.W1H[:, e, ms], XST[i % 2][:, 1], start=False, stop=False)
                    ins = pe.matmul(out, t.W1L[:, e, ms], XST[i % 2][:, 0], start=False, stop=True)
                ins.then_inc(up_mm, 1)

            def down(k, i, e):
                n = k * UN + i
                after(pe, split, n + 1)
                after(pe, y_set, n - 1)
                for h in range(NHALF):
                    out = ps[6 + i % 2][:, D * h:D * h + D]
                    pe.matmul(out, t.ONES16[0:2, :], t.B2P[0:2, e, :], start=True, stop=False)
                    for m in range(MT):
                        hh, hl = (H16[i % 4][:, part, m, P * h:P * h + P] for part in range(2))
                        pe.matmul(out, hh, t.W2L[:, e, m, :], start=False, stop=False)
                        pe.matmul(out, hh, t.W2H[:, e, m, :], start=False, stop=False)
                        ins = pe.matmul(out, hl, t.W2H[:, e, m, :], start=False, stop=(m == MT - 1))
                ins.then_inc(down_mm, 1)

            def body(k, first, last):
                mine = expert_values(pe, k, 0)
                late = expert_values(pe, k, 1)
                if first:
                    turn(0, 0)
                for i in range(tiles_of(last)):
                    if not (last and i == tiles_of(last) - 1):
                        turn(k if i < UN - 1 else k + 1, (i + 1) % UN)
                    up(k, i, mine[i])
                    if not (first and i < 2):
                        down(k, i - 2, late[i])
                if last:
                    for i in range(tiles_of(last) - 2, tiles_of(last)):
                        down(k, i, mine[i])
            rounds(pe, body)

        @block.scalar
        def _(act):
            def take(k, i):
                n = k * UN + i
                after(act, turned, n + 1)
                after(act, up_mm, n - 1)
                nc.scalar.activation(XST[i % 2], ps[i % 2].bitcast(F16)[:, 0:2 * TS].rearrange("p (k n) -> p k n", n=TS),
                                     ACT.Copy).then_inc(xt_set, 1)

            def body(k, first, last):
                if first:
                    take(0, 0)
                for i in range(tiles_of(last)):
                    n = k * UN + i
                    if not (last and i == tiles_of(last) - 1):
                        take(k if i < UN - 1 else k + 1, (i + 1) % UN)
                    after(act, bias_set, n + 1)
                    after(act, split, n - 1)
                    after(act, up_mm, n + 1)
                    for m in range(MT):
                        ins = nc.scalar.activation(HF[i % 2][:, m], UP[i % 2][:, m], ACT.Gelu,
                                                   bias=BIAS[i % 4][:, m:m + 1], scale=1.0 / WS)
                    ins.then_inc(hidden, 1)
            nc.scalar.activation(t.GATE[0:1, 1:2], t.MHALF[0:1, 0:1], ACT.Gelu).then_inc(primed, 1)
            rounds(act, body)
            for c in range(NT // CT):
                act.wait_ge(back_in[c], 32)
                for j in range(CT):
                    i = CT * c + j
                    ins = nc.scalar.activation(BACK[c][:, 1, j], BACK[c][:, 1, j], ACT.Copy, scale=t.WEIGHT[:, 1, i:i + 1])
                ins.then_inc(second_weighted, 1)

        @block.vector
        def _(dve):
            def take_out(k, i):
                n = k * UN + i
                after(dve, down_mm, n + 1)
                after(dve, y_out[i % 4], written(k, i) - 16 * NHALF)
                dve.tensor_copy(Y[i % 4], ps[6 + i % 2][:, 0:NHALF * D].rearrange("p (h d) -> p h d", d=D)).then_inc(y_set, 1)

            def fetch_bias(i, e):
                dve.tensor_copy(BIAS[i % 4], t.B1[:, e, :]).then_inc(bias_set, 1)

            def body(k, first, last):
                ahead = expert_values(dve, k, 2)
                if first:
                    for i, e in enumerate(expert_values(dve, 0, 0)[0:2]):
                        fetch_bias(i, e)
                for i in range(tiles_of(last)):
                    n = k * UN + i
                    after(dve, hidden, n + 1)
                    after(dve, down_mm, n - 3)
                    dve.tensor_copy(H16[i % 4][:, 0], HF[i % 2]).then_inc(high, 1)
                    dve.wait_ge(high, n + 1)
                    dve.tensor_tensor(H16[i % 4][:, 1], HF[i % 2], H16[i % 4][:, 0], ALU.subtract).then_inc(split, 1)
                    if not (last and i >= tiles_of(last) - 2):
                        fetch_bias(i + 2, ahead[i])
                    if not (first and i < 2):
                        take_out(k, i - 2)
                if last:
                    for i in range(tiles_of(last) - 2, tiles_of(last)):
                        take_out(k, i)
            rounds(dve, body)

            def statistics(c):
                dve.wait_ge(back_added, c + 1)
                for i in range(CT * c, CT * c + CT):
                    dve.bn_stats(t.RSTATS[:, i, :], t.RES[:, i, :])
            for c in range(NT // CT):
                dve.wait_ge(back_in[c], 32)
                for j in range(CT):
                    i = CT * c + j
                    res = t.RES[:, i, :]
                    ins = dve.scalar_tensor_tensor(res, BACK[c][:, 0, j], t.WEIGHT[:, 0, i:i + 1], res, ALU.mult, ALU.add)
                ins.then_inc(first_added, 1)
                if store is not None:
                    dve.wait_ge(first_added, c + 1)
                    dve.wait_ge(second_weighted, c + 1)
                    res = t.RES[:, CT * c:CT * c + CT, :]
                    dve.tensor_tensor(res, res, BACK[c][:, 1], ALU.add).then_inc(back_added, 1)
                elif c >= 1:
                    statistics(c - 1)
            if store is None:
                statistics(NT // CT - 1)
def attention_stage(nc, t):
    with ExitStack() as ctx:
        sem = stage_semaphores(nc, ctx, "a_")
        norm = norm_program(nc, t, sem)
        at = [0]

        def carve(dt, *shape):
            n = int(np.prod(shape))
            words = n if dt == F32 else n // 2
            v = t.arena[:, at[0]:at[0] + words]
            at[0] += words
            v = v if dt == F32 else v.bitcast(dt)
            names = "abcde"[:len(shape)]
            if len(shape) > 1:
                v = v.rearrange(f"p ({' '.join(names)}) -> p {' '.join(names)}", **dict(zip(names, shape)))
            return v

        QPAD = [carve(F16, HG, GH, SEQ) for _ in range(2)]
        KST = [carve(F16, HG, SEQ) for _ in range(2)]
        QST = carve(F16, HG, SEQ)
        HI = carve(F16, 2, SEQ)
        V32 = [carve(F32, TPB, NH, 32) for _ in range(2)]
        PR = [carve(F32, 3, BANK) for _ in range(2)]
        OT = [carve(F32, HG, SEQ) for _ in range(2)]
        ATT = carve(F32, TPB, D)
        ATH, ATL = carve(F16, SEQ), carve(F16, SEQ)
        MX = carve(F32, 2, TPB, GH, 2)
        M16 = carve(F16, 2, TPB, GH, 2, 2)
        MROW = [carve(F16, SEQ) for _ in range(2)]
        RC = carve(F32, TPB, NH)
        IDB, MASKB, MASKT = carve(BF16, P), carve(BF16, GH, P), carve(BF16, GH, P)
        ID16 = t.ID16
        CWF, CRF = carve(F32, HG, P), carve(F32, SEQ)
        CW, CR = carve(F16, HG, P), carve(F16, SEQ)
        LOWROW = t.LOW
        XH = t.XTH.rearrange("p (b n) -> p b n", n=SEQ)
        XL = t.XTL.rearrange("p (b n) -> p b n", n=SEQ)
        RESB = t.RES.rearrange("p (b t) d -> p b (t d)", t=TPB)
        ps = t.psum

        (consts_in, cleared, masks, cast, ready, m_high, rc_set) = (sem(n) for n in (
            "consts_in", "cleared", "masks", "cast", "ready", "m_high", "rc_set"))
        (proj, v_mm, hi, parts, vset, m_mm, m_red, m16, mt_mm, mrow_set) = (sem(n) for n in (
            "proj", "v_mm", "hi", "parts", "vset", "m_mm", "m_red", "m16", "mt_mm", "mrow_set"))
        qpad_in, mrow_in = [sem(f"qpad_in{h}") for h in range(2)], [sem(f"mrow_in{h}") for h in range(2)]
        (st_mm, exps, av_mm, ot_set, ft_mm, att, fa_mm, att_hi, att_lo, fo_mm, added) = (sem(n) for n in (
            "st_mm", "exps", "av_mm", "ot_set", "ft_mm", "att", "fa_mm", "att_hi", "att_lo", "fo_mm", "added"))
        block = ctx.enter_context(nc.Block())

        def after(eng, s, n):
            if not (isinstance(n, int) and n <= 0):
                eng.wait_ge(s, n)

        def pipeline(eng, body):
            def peeled(b):
                body(b, b % 2, (0 <= b < NB, -1 <= b < NB - 1, b < NB - 2, 1 <= b, 2 <= b))
            for b in range(-2, 2):
                peeled(b)
            with eng.Fori(0, (NB - 4) // 2) as k:
                for i in range(2):
                    body(2 * k + (2 + i), i, (True,) * 5)
            for b in range(NB - 2, NB + 1):
                peeled(b)

        def projection_bank(b, G):
            return ps[4 + G] if isinstance(b, int) and b == -2 else ps[0]

        @block.sync
        def _(sp):
            sp.dma_start(CWF[0:3], t.dram["cw"]).then_inc(consts_in, 16)
            sp.dma_start(CRF[0:3], t.dram["cr"]).then_inc(consts_in, 16)
            sp.wait_ge(ready, 1)

            def spread_q(c, r, h):
                after(sp, parts, 8 * c + 4 * h + 4)
                for g in range(GH):
                    q = slice(32 * g, 32 * g + 32)
                    sp.dma_start(QPAD[r][q, 2 * h:2 * h + 2, g, :], QST[q, 2 * h:2 * h + 2, :]).then_inc(qpad_in[h], 16)

            def spread_m(c, r, h):
                after(sp, mrow_set, 2 * c + h + 1)
                for g in range(GH):
                    row = 32 * g + 26
                    sp.dma_start(QPAD[r][row:row + 2, 2 * h:2 * h + 2, g, :],
                                 MROW[h][4 * g:4 * g + 4, :]).then_inc(mrow_in[h], 16)

            def body(b, q, stages):
                second, first, projections, output, finished = stages
                if second:
                    spread_m(b, q, 1)
                if projections:
                    spread_q(b + 2, q, 0)
                if first:
                    spread_m(b + 1, 1 - q, 0)
                if projections:
                    spread_q(b + 2, q, 1)
            pipeline(sp, body)

        @block.gpsimd
        def _(pool):
            norm.gpsimd(pool)
            words = [v.rearrange("p G g n -> p (G g n)").bitcast(F32) for v in QPAD]
            for v in (words[0], words[1], V32[0], V32[1], IDB, MASKB, MASKT):
                nc.gpsimd.memset(v, 0.0).then_inc(cleared, 1)
            pool.wait_ge(cleared, 7)
            for v in V32:
                nc.gpsimd.memset(v[:, :, :, 8:9], 1.0).then_inc(masks, 1)
            nc.gpsimd.affine_select(out=IDB, in_=IDB, compare_op=ALU.not_equal, fill=1.0, base=0,
                                    pattern=[[-1, P]], channel_multiplier=1).then_inc(masks, 1)
            nc.gpsimd.affine_select(out=MASKB, in_=MASKB, compare_op=ALU.is_ge, fill=-1.0e30, base=0,
                                    pattern=[[0, GH], [-1, P]], channel_multiplier=1).then_inc(masks, 1)
            nc.gpsimd.affine_select(out=MASKT, in_=MASKT, compare_op=ALU.is_ge, fill=-1.0e30, base=0,
                                    pattern=[[0, GH], [1, P]], channel_multiplier=-1).then_inc(masks, 1)

        @block.tensor
        def _(pe):
            def project(c, G, bank):
                for k in range(2):
                    out = bank[:, SEQ * k:SEQ * k + SEQ]
                    for i, (w, x) in enumerate(((t.QKWH, XH), (t.QKWH, XL), (t.QKWL, XH))):
                        pe.matmul(out, w[:, HG * k + G, :], x[:, c, :], start=(i == 0), stop=(k == 0 and i == 2))
                ins = pe.matmul(out, CW[0:3, G, :], CR[0:3, :], start=False, stop=True)
                ins.then_inc(proj, 1)

            def values(c):
                for tile in range(TPB):
                    js = slice(P * tile, P * tile + P)
                    for i, (x, w) in enumerate(((XH, t.VOWH), (XL, t.VOWH), (XH, t.VOWL))):
                        ins = pe.matmul(ps[1][:, js], x[:, c, js], w[:, 0:D], start=(i == 0), stop=(i == 2))
                ins.then_inc(v_mm, 1)

            def maxima(c, r, G, blocks):
                if G % 2 == 0 and 0 in blocks:
                    after(pe, qpad_in[G // 2], 64 * c + 64)
                for k in blocks:
                    n = 3 * G + k
                    bank = ps[2 + n % 2]
                    after(pe, m_red, 12 * c + n - 1)
                    if k == 0:
                        pe.matmul(bank, IDB, MASKB.rearrange("p g n -> p (g n)"), start=True, stop=False)
                        for g in range(GH):
                            ins = pe.matmul(bank[:, P * g:P * g + P], QPAD[r][:, G, g, 0:P], KST[r][:, G, 0:P],
                                            start=False, stop=(g == GH - 1))
                    else:
                        out = bank.rearrange("p (h t n) -> p h t n", t=TPB, n=P)
                        pe.matmul(out[:, :, 1, :], IDB, MASKB[:, 0:2, :], start=True, stop=False, skip_group_check=True)
                        for h in range(2):
                            g = 2 * (k - 1) + h
                            for tile in range(TPB):
                                ins = pe.matmul(out[:, h, tile, :], QPAD[r][:, G, g, P:2 * P],
                                                KST[r][:, G, P * tile:P * tile + P], start=False,
                                                stop=(h == 1 and tile == 1), skip_group_check=True)
                    ins.then_inc(m_mm, 1)

            def turn_maxima(c, h):
                after(pe, m16, 2 * c + h + 1)
                for tile in range(TPB):
                    ins = pe.transpose(ps[0].bitcast(F16)[0:16, P * tile:P * tile + P],
                                       M16[:, h, tile].rearrange("p g c h -> p (g c h)"), ID16)
                ins.then_inc(mt_mm, 1)

            def scores(b, q, G):
                if G % 2 == 0:
                    after(pe, mrow_in[G // 2], 64 * b + 64)
                after(pe, exps, 4 * b + G)
                for a in range(2):
                    out = ps[5 + a].rearrange("p (h t n) -> p h t n", t=TPB, n=P)
                    pe.matmul(out[:, :, 0, :], IDB, MASKT[:, 0:2, :], start=True, stop=False, skip_group_check=True)
                    pe.matmul(ps[5 + a], KST[q][:, G, 0:P], QPAD[q][:, G, 2 * a:2 * a + 2, :], start=False, stop=True,
                              skip_group_check=True)
                pe.matmul(ps[7], IDB, MASKT.rearrange("p g n -> p (g n)"), start=True, stop=False)
                pe.matmul(ps[7], KST[q][:, G, P:2 * P], QPAD[q][:, G, :, P:2 * P], start=False, stop=True).then_inc(st_mm, 1)

            def weigh(b, q, G):
                after(pe, exps, 4 * b + G + 1)
                if G == 0:
                    after(pe, vset, b + 1)
                if G % 2 == 0:
                    after(pe, ot_set, 2 * b - 1 + G // 2)
                half = ps[4][:, SEQ * (G % 2):SEQ * (G % 2) + SEQ]
                for g in range(GH):
                    out = half[32 * g:32 * g + 32, :]
                    early = PR[G % 2][:, g // 2, SEQ * (g % 2):SEQ * (g % 2) + SEQ]
                    late = PR[G % 2][:, 2, P * g:P * g + P]
                    pe.matmul(out, V32[q][:, 0, 4 * G + g, :], early, start=True, stop=False)
                    ins = pe.matmul(out[:, P:2 * P], V32[q][:, 1, 4 * G + g, :], late, start=False, stop=True)
                ins.then_inc(av_mm, 1)

            def turn_back(b, q, tile):
                if tile == 0:
                    after(pe, ot_set, 2 * b + 2)
                    after(pe, added, b)
                else:
                    after(pe, att, 2 * b + 1)
                for G in range(HG):
                    ins = pe.transpose(ps[1][:, P * G:P * G + P], OT[q][:, G, P * tile:P * tile + P], t.ID)
                ins.then_inc(ft_mm, 1)

            def turn_out(b):
                after(pe, att, 2 * b + 2)
                for tile in range(TPB):
                    ins = pe.transpose(ps[1][:, P * tile:P * tile + P], ATT[:, tile, :], t.ID)
                ins.then_inc(fa_mm, 1)

            def project_out(b):
                after(pe, att_lo, b + 1)
                for tile in range(TPB):
                    js, out = slice(P * tile, P * tile + P), slice(SEQ + P * tile, SEQ + P * tile + P)
                    for i, (x, w) in enumerate(((ATH, t.VOWH), (ATL, t.VOWH), (ATH, t.VOWL))):
                        ins = pe.matmul(ps[1][:, out], x[:, js], w[:, D:2 * D], start=(i == 0), stop=(i == 2))
                ins.then_inc(fo_mm, 1)

            def body(b, q, stages):
                second, first, projections, output, finished = stages
                for G in range(HG):
                    if second:
                        scores(b, q, G)
                    if G == 0 and second:
                        if first:
                            after(pe, parts, 8 * b + 16)
                        after(pe, mrow_set, 2 * b + 1)
                        turn_maxima(b, 1)
                    if G == 2 and first:
                        if projections:
                            after(pe, parts, 8 * b + 20)
                        turn_maxima(b + 1, 0)
                    if isinstance(b, int) and b == -1 and G == 0:
                        pe.wait_ge(masks, 5)
                    if first:
                        maxima(b + 1, 1 - q, G, (0, 1))
                    if projections:
                        if G % 2 == 0:
                            after(pe, mrow_set, 2 * b + 2 + G // 2)
                        if not (isinstance(b, int) and b == -2):
                            after(pe, parts, 8 * b + 16 + 2 * G)
                        project(b + 2, G, projection_bank(b, G))
                    if first:
                        maxima(b + 1, 1 - q, G, (2,))
                    if output:
                        if G == 0 and second:
                            after(pe, vset, b + 1)
                        if G < TPB:
                            turn_back(b - 1, 1 - q, G)
                        elif G == 2:
                            turn_out(b - 1)
                        else:
                            project_out(b - 1)
                    if second:
                        weigh(b, q, G)
                    if first and G == HG - 1:
                        after(pe, added, b)
                        values(b + 1)

            norm.tensor(pe)
            pe.wait_ge(norm.low, NG)
            pe.wait_ge(cast, 2)
            pipeline(pe, body)

        @block.scalar
        def _(act):
            norm.scalar(act)
            act.wait_ge(consts_in, 32)
            nc.scalar.activation(CW[0:3], CWF[0:3], ACT.Copy).then_inc(cast, 1)
            nc.scalar.activation(CR[0:3], CRF[0:3], ACT.Copy).then_inc(cast, 1)
            nc.scalar.activation(RC[0:1, 0, 0:1], t.MHALF[0:1, 0:1], ACT.Exp).then_inc(cast, 1)
            act.wait_ge(cast, 3)
            act.wait_ge(masks, 2)
            act.sem_inc(ready, 1)

            def highs(c, G, bank):
                after(act, proj, 4 * c + G + 1)
                if isinstance(c, int) and c == 0:
                    after(act, parts, 2 * G)
                nc.scalar.activation(HI[:, 0, :], bank[:, 0:SEQ], ACT.Identity, bias=LOWROW[:, 3:4])
                nc.scalar.activation(HI[:, 1, :], bank[:, SEQ:2 * SEQ], ACT.Copy).then_inc(hi, 1)

            def values(c, r):
                after(act, v_mm, c + 1)
                nc.scalar.activation(V32[r][:, :, :, 0:8], ps[1][:, 0:SEQ].rearrange("p (t h d) -> p t h d", t=TPB, d=8),
                                     ACT.Copy).then_inc(vset, 1)

            def maxima_rows(c, h):
                after(act, mt_mm, 2 * c + h + 1)
                after(act, mrow_in[h], 64 * c)
                nc.scalar.activation(MROW[h][0:16, :], ps[0].bitcast(F16)[0:16, 0:SEQ], ACT.Copy).then_inc(mrow_set, 1)

            def expo(b, G):
                after(act, st_mm, 4 * b + G + 1)
                after(act, av_mm, 4 * b + G - 1)
                nc.scalar.activation(PR[G % 2], t.psum_all[:, 5:8, :], ACT.Exp, scale=1.0 / LOGIT).then_inc(exps, 1)

            def take_out(b, q, half):
                after(act, av_mm, 4 * b + 2 * half + 2)
                nc.scalar.activation(OT[q][:, 2 * half:2 * half + 2, :], ps[4].rearrange("p (g n) -> p g n", n=SEQ),
                                     ACT.Copy).then_inc(ot_set, 1)

            def out_high(b):
                after(act, fa_mm, b + 1)
                nc.scalar.activation(ATH, ps[1][:, 0:SEQ], ACT.Copy).then_inc(att_hi, 1)

            def body(b, q, stages):
                second, first, projections, output, finished = stages
                for G in range(HG):
                    if G == 0 and second:
                        maxima_rows(b, 1)
                    if G == 2 and first:
                        maxima_rows(b + 1, 0)
                    if second:
                        expo(b, G)
                    if projections:
                        highs(b + 2, G, projection_bank(b, G))
                    if output and G == 2:
                        out_high(b - 1)
                    if second and G % 2 == 1:
                        take_out(b, q, G // 2)
                if first:
                    values(b + 1, 1 - q)
            pipeline(act, body)

        @block.vector
        def _(dve):
            norm.vector(dve)
            tt, ts, stt = dve.tensor_tensor, dve.tensor_scalar, dve.scalar_tensor_tensor

            def split(c, r, G, bank):
                after(dve, hi, 4 * c + G + 1)
                if G % 2 == 0:
                    after(dve, qpad_in[G // 2], 64 * c)
                after(dve, st_mm, 4 * c + G - 7)
                for k, out in enumerate((QST, KST[r])):
                    stt(out[:, G, :], HI[:, k, :], LOWROW[:, k:k + 1], bank[:, SEQ * k:SEQ * k + SEQ],
                        ALU.mult, ALU.add).then_inc(parts, 1)

            def reduce(c, G):
                for k in range(3):
                    n = 3 * G + k
                    after(dve, m_mm, 12 * c + n + 1)
                    if k == 0:
                        out, src = MX[:, G // 2, 0, :, G % 2], ps[2 + n % 2].rearrange("p (g n) -> p g n", n=P)
                    else:
                        out, src = MX[:, G // 2, 1, 2 * (k - 1):2 * k, G % 2], ps[2 + n % 2].rearrange("p (g n) -> p g n", n=SEQ)
                    dve.tensor_reduce(out, src, AX.X, ALU.max).then_inc(m_red, 1)

            def split_maxima(c, h):
                after(dve, m_red, 12 * c + 6 * h + 6)
                after(dve, mt_mm, 2 * c + h - 1)
                mx = MX[:, h].rearrange("p t g h -> p (t g) h")
                hi_m, lo_m = (M16[:, h, :, :, i, :].rearrange("p t g h -> p (t g) h") for i in range(2))
                ts(hi_m, mx, -1.0 / 1024, None, ALU.mult).then_inc(m_high, 1)
                after(dve, m_high, 2 * c + h + 1)
                stt(lo_m, mx, -1.0 / 1024, hi_m, ALU.mult, ALU.subtract).then_inc(m16, 1)

            def normalise(b, tile):
                after(dve, ft_mm, 2 * b + tile + 1)
                src = ps[1].rearrange("p (h d) -> p h d", d=32)
                dve.reciprocal(RC[:, tile, :], src[:, :, 8]).then_inc(rc_set, 1)
                dve.wait_ge(rc_set, 2 * b + tile + 1)
                tt(ATT[:, tile, :].rearrange("p (h d) -> p h d", d=8), src[:, :, 0:8],
                   RC[:, tile, :].rearrange("p (h o) -> p h o", o=1).broadcast_to([P, NH, 8]), ALU.mult).then_inc(att, 1)

            def statistics(b):
                for tile in range(TPB):
                    dve.bn_stats(t.RSTATS[:, TPB * b + tile, :], t.RES[:, TPB * b + tile, :])

            def out_low(b):
                after(dve, att_hi, b + 1)
                tt(ATL, ps[1][:, 0:SEQ], ATH, ALU.subtract).then_inc(att_lo, 1)

            def add(b):
                after(dve, fo_mm, b + 1)
                stt(RESB[:, b, :], ps[1][:, SEQ:2 * SEQ], 1.0 / (WQ * WQ), RESB[:, b, :], ALU.mult, ALU.add).then_inc(added, 1)

            def body(b, q, stages):
                second, first, projections, output, finished = stages
                for G in range(HG):
                    if first:
                        reduce(b + 1, G)
                    if finished and G == 2:
                        after(dve, added, b - 1)
                    if output and G == HG - 1:
                        add(b - 1)
                    if projections:
                        split(b + 2, q, G, projection_bank(b, G))
                    if finished and G == 2:
                        statistics(b - 2)
                    if first and G % 2 == 1:
                        split_maxima(b + 1, G // 2)
                    if output:
                        if G < TPB:
                            normalise(b - 1, G)
                        elif G == 2:
                            out_low(b - 1)
            pipeline(dve, body)
            dve.wait_ge(added, NB)
            statistics(NB - 1)
def host_tables():
    c = {}
    s = np.arange(SEQ)
    f = np.arange(SEQ)
    ang = 2 * np.pi * np.outer(s, f) / NFFT
    fwd = np.concatenate([np.cos(ang), -np.sin(ang)], 1)
    fwd[:, SEQ] = (-1.0) ** s
    inv = np.concatenate([2 * np.cos(ang.T), -2 * np.sin(ang.T)], 0) / NFFT
    inv[0] = 1.0 / NFFT
    inv[SEQ] = (-1.0) ** s / NFFT
    c["fwd"] = fwd.reshape(TPB, P, NFFT)
    c["inv"] = inv.reshape(NFT, P, SEQ)
    off = np.zeros((P, 4))
    off[:NM] = [0.25, 0.25, 0.5, 0]
    off[NM:] = [0.5, 0, 0.25, 0]
    c["offsets"] = off
    keep = np.zeros((P, 2))
    keep[:, 0] = 1
    keep[0] = [0, 1]
    c["keep"] = keep
    c["rank"] = np.tile(np.arange(NE, 0, -1.0), (P, 1))
    slopes = 2.0 ** (-8.0 / NH * np.arange(1, NH + 1)) * LOGIT / WQ
    cw = np.zeros((3, HG, GH, 32))
    high = slopes.astype(np.float16).astype(np.float64)
    cw[0, :, :, 24:26] = high.reshape(HG, GH, 1)
    cw[1, :, :, 24:26] = (slopes - high).astype(np.float16).astype(np.float64).reshape(HG, GH, 1)
    cw[2, :, :, 26:28] = 1024
    c["cw"] = cw.reshape(3, HG, P)
    c["cr"] = np.stack([np.arange(SEQ), np.arange(SEQ), np.ones(SEQ)])
    c["slotno"] = np.arange(SLOTS).reshape(1, SLOTS)
    low = np.zeros((GH, 32, 4))
    low[0, 1, 2] = -1
    low[:, 24:26, 0] = 1
    low[:, 24:26, 3] = WQ
    low[:, 16:24, 0] = -1
    low[:, 8:16, 1] = -1
    low[:, 25, 1] = -1
    c["lowrow"] = low.reshape(P, 4)
    c["ident"] = np.eye(P)
    return {k: np.ascontiguousarray(v, dtype=np.float32) for k, v in c.items()}


def build(nc, dram):
    with ExitStack() as ctx:
        t = Bag()
        t.dram = dram

        def sb(name, shape, dt=F32):
            return ctx.enter_context(nc.sbuf_tensor(name, shape, dt))
        t.RES = sb("RES", [P, NT, D])[:]
        t.XN = sb("XN", [P, NT, D])[:]
        t.ID = sb("ID", [P, P])[:]
        t.STATS = sb("STATS", [P, NT, 6])[:]
        t.RSTATS = sb("RSTATS", [P, NT, 6])[:]
        t.NRM = sb("NRM", [P, 8, 2 * NT])[:]
        t.MHALF = sb("MHALF", [P, NT])[:]
        t.psum_all = ctx.enter_context(nc.psum_tensor("banks", [P, 8, BANK], F32))[:]
        t.psum = [t.psum_all[:, i, :] for i in range(8)]
        t.W1H, t.W1L = sb("W1H", [P, NX, HID], F16)[:], sb("W1L", [P, NX, HID], F16)[:]
        t.W2H, t.W2L = sb("W2H", [P, NX, MT, D], F16)[:], sb("W2L", [P, NX, MT, D], F16)[:]
        t.GWH, t.GWL = sb("GWH", [P, NE], F16)[:], sb("GWL", [P, NE], F16)[:]
        t.QKWH, t.QKWL = sb("QKWH", [P, 2 * HG, P], F16)[:], sb("QKWL", [P, 2 * HG, P], F16)[:]
        t.VOWH, t.VOWL = sb("VOWH", [P, 2 * D], F16)[:], sb("VOWL", [P, 2 * D], F16)[:]
        t.XTH, t.XTL = sb("XTH", [P, NT * P], F16)[:], sb("XTL", [P, NT * P], F16)[:]
        t.B1 = sb("B1", [P, NX, MT])[:]
        t.ID16, t.ONES16, t.BEFORE = sb("ID16", [P, P], F16)[:], sb("ONES16", [P, P], F16)[:], sb("BEFORE", [P, P], F16)[:]
        t.LOW, t.GATE = sb("LOW", [P, 4])[:], sb("GATE", [P, 2])[:]
        t.EID = sb("EID", [1, 3, ROUNDS, UN], I32)[:]
        t.SLOTNO = sb("SLOTNO", [1, SLOTS])[:]
        t.PLACE, t.WEIGHT = sb("PLACE", [P, 2, NT], I32)[:], sb("WEIGHT", [P, 2, NT])[:]
        t.EMPTY = sb("EMPTY", [P, ROW], F16)[:]
        t.GB = sb("GB", [P, 2, NE])[:]
        t.B2, t.B2P = sb("B2", [2, NX, D])[:], sb("B2P", [2, NX, D], F16)[:]
        t.STG = [half.bitcast(F32)[:, HID * i:HID * i + HID] for half in (t.XTH, t.XTL) for i in range(NT * P // (2 * HID))]
        t.arena = sb("ARENA", [P, ARENA])[:]
        t.ROWS = t.arena[:, ARENA - NT * ROW // 2:ARENA].bitcast(F16).rearrange("p (t r) -> p t r", r=ROW)
        conv_stage(nc, t)
        shared_stage(nc, t, "f")
        routed_stage(nc, t, "f")
        attention_stage(nc, t)
        shared_stage(nc, t, "g")
        routed_stage(nc, t, "g", store=dram["out"].rearrange("b (t p) d -> p (b t) d", p=P))


def kernel(**inputs):
    import concourse.bacc as bacc
    from concourse.bass_utils import run_bass_kernel_spmd

    def of(name):
        return np.asarray(inputs["L0_" + name])

    def both(a):
        return np.concatenate([a.T, a.T], 0)

    arrays = host_tables()
    arrays["x"] = of("attn_a_x")
    arrays["params"] = np.stack([both(of("attn_a_log_A_real")), both(of("attn_a_A_imag")), both(of("attn_a_C_re")),
                                 both(of("attn_a_C_im")), np.broadcast_to(of("attn_a_log_dt"), (P, D))])
    arrays["ln"] = np.stack([np.broadcast_to(of("attn_a_ln_w"), (P, D)), np.broadcast_to(of("attn_a_ln_b"), (P, D))])
    arrays["dcol"] = of("attn_a_D").reshape(D, 1)
    arrays["w1"] = np.concatenate([of("ffn_w1"), of("ffn_ws1")[None]])
    arrays["w2"] = np.concatenate([of("ffn_w2"), of("ffn_ws2")[None]])
    arrays["b1"] = np.concatenate([of("ffn_b1"), of("ffn_bs1")[None]]).reshape(NX, MT, P).transpose(2, 0, 1)
    arrays["b2_rows"] = np.broadcast_to(np.concatenate([of("ffn_b2"), of("ffn_bs2")[None]]), (2, NX, D))
    qkv = of("attn_b_Wqkv").reshape(D, 3, HG, GH, 1, HD)
    w_qk = np.zeros((D, 2, HG, GH, 4, HD), np.float32)
    w_qk[:, :, :, :, 0:3] = qkv[:, 0:2]
    arrays["w_qk"] = w_qk.reshape(D, 2 * HG, P)
    arrays["w_vo"] = np.concatenate([of("attn_b_Wqkv")[:, 2 * D:], of("attn_b_Wout")], 1)
    arrays["gate_w"] = of("ffn_gate_w")
    arrays["gate_b"] = np.broadcast_to(of("ffn_gate_b"), (P, NE))
    arrays = {k: np.ascontiguousarray(v) for k, v in arrays.items()}
    nc = bacc.Bacc("TRN2", target_bir_lowering=False, num_devices=1)
    dram = {k: nc.dram_tensor("in_" + k, v.shape, F32, kind="ExternalInput").ap() for k, v in arrays.items()}
    for tag in "fg":
        dram["slots" + tag] = nc.dram_tensor("slots_" + tag, (SLOTS * TS, ROW // 2), I32).ap()
        dram["expert_out" + tag] = nc.dram_tensor("expert_out_" + tag, (2 * NT * P, D), F32).ap()
    dram["out"] = nc.dram_tensor("out_x", (NB, SEQ, D), F32, kind="ExternalOutput").ap()
    build(nc, dram)
    result = run_bass_kernel_spmd(nc, [{"in_" + k: v for k, v in arrays.items()}], core_ids=[0])
    return result.results[0]["out_x"]
```
